# Optimizing a Trainium2 kernel written in Bass

```python
import numpy as np
import jax
import jax.numpy as jnp

def _softmax(x, axis=-1):
    return jax.nn.softmax(x, axis=axis)

def _gelu(x):
    return jax.nn.gelu(x, approximate=True)

def _silu(x):
    return jax.nn.silu(x)

def _sigmoid(x):
    return jax.nn.sigmoid(x)

def _layernorm(x, axis=-1, eps=1e-05):
    m = jnp.mean(x, axis=axis, keepdims=True)
    v = jnp.var(x, axis=axis, keepdims=True)
    return (x - m) / jnp.sqrt(v + eps)

def _scatter_add(tgt, idx, src, axis=0):
    return tgt.at[idx].add(src)

def _segment_sum(src, seg, n):
    return jax.ops.segment_sum(src, seg, n)
kernel_name = 'mk_hybrid_d1_jaxref_r8_442325'

def setup_inputs(seed: int=0):
    np.random.seed(seed)
    _w = jnp.asarray

    def _L0_attn_a_setup():
        import jax, jax.numpy as jnp
        import numpy as np
        B, N, D = (4, 512, 128)
        H, F = (16, 128)
        HD = D // H
        key = jax.random.key(seed)
        k1, k2, k3, k4, k5 = jax.random.split(key, 5)
        x = jax.random.normal(k1, (B, N, D), dtype=jnp.float32)
        W_qkv = jax.random.normal(k2, (3 * D, D), dtype=jnp.float32) * np.sqrt(2.0 / D)
        proj = jax.random.normal(k3, (H, HD, F), dtype=jnp.float32) / np.sqrt(HD)
        W_out = jax.random.normal(k4, (D, D), dtype=jnp.float32) * np.sqrt(2.0 / D)
        b_out = jnp.zeros((D,), dtype=jnp.float32)
        return {'x': x, 'W_qkv': W_qkv, 'proj': proj, 'W_out': W_out, 'b_out': b_out}
    _L0_attn_a_in = _L0_attn_a_setup()

    def _L0_attn_b_setup():
        import jax, jax.numpy as jnp
        import numpy as np
        EMBED_DIM = 128
        VALUE_DIM = 256
        NUM_HEADS = 8
        KEY_DIM = EMBED_DIM // NUM_HEADS
        HEAD_DIM = VALUE_DIM // NUM_HEADS
        EPS = 1e-05
        B, S = (2, 256)

        def _xavier(k, shape, gain):
            a = gain * np.sqrt(6.0 / (shape[0] + shape[1]))
            return jax.random.uniform(k, shape, jnp.float32, -a, a)

        def _rel_pos(slen):
            lin = jnp.linspace(0.0, 1.0, KEY_DIM // 2)
            angle = jnp.repeat(1.0 / 10000.0 ** lin, 2)
            decay = jnp.log1p(-2.0 ** (-5.0 - jnp.arange(NUM_HEADS, dtype=jnp.float32)))
            idx = jnp.arange(slen, dtype=jnp.float32)
            sin = jnp.sin(idx[:, None] * angle[None, :])
            cos = jnp.cos(idx[:, None] * angle[None, :])
            diff = idx[:, None] - idx[None, :]
            m = jnp.where(diff[None] >= 0, jnp.exp(diff[None] * decay[:, None, None]), 0.0)
            m = m / jnp.sqrt(m.sum(-1, keepdims=True))
            return (sin, cos, m)

        def _rotate_every_two(x):
            x1 = x[..., ::2]
            x2 = x[..., 1::2]
            return jnp.stack((-x2, x1), axis=-1).reshape(x.shape)
        key = jax.random.key(seed)
        ks = jax.random.split(key, 6)
        g = 2.0 ** (-2.5)
        return {'x': jax.random.normal(ks[0], (B, S, EMBED_DIM), jnp.float32), 'wq': _xavier(ks[1], (EMBED_DIM, EMBED_DIM), g), 'wk': _xavier(ks[2], (EMBED_DIM, EMBED_DIM), g), 'wv': _xavier(ks[3], (EMBED_DIM, VALUE_DIM), g), 'wg': _xavier(ks[4], (EMBED_DIM, VALUE_DIM), g), 'wo': _xavier(ks[5], (VALUE_DIM, EMBED_DIM), 1.0)}
    _L0_attn_b_in = _L0_attn_b_setup()

    def _L0_ffn_setup():
        import jax, jax.numpy as jnp
        import numpy as np
        NUM_EXPERTS = 8
        IN_FEATURES = 128
        HIDDEN_FEATURES = 512
        GATE_DIM = 16
        EPS = 0.0001
        key = jax.random.key(seed)
        ks = jax.random.split(key, 7)
        hidden_states = jax.random.normal(ks[0], (1, 256, IN_FEATURES), dtype=jnp.float32)
        wg_red = jax.random.normal(ks[1], (GATE_DIM, IN_FEATURES), dtype=jnp.float32) * 0.02
        wg = jax.random.normal(ks[2], (NUM_EXPERTS, GATE_DIM), dtype=jnp.float32)
        w1 = jax.random.uniform(ks[3], (NUM_EXPERTS, IN_FEATURES, HIDDEN_FEATURES), dtype=jnp.float32)
        b1 = jax.random.uniform(ks[4], (NUM_EXPERTS, HIDDEN_FEATURES), dtype=jnp.float32)
        w2 = jax.random.uniform(ks[5], (NUM_EXPERTS, HIDDEN_FEATURES, IN_FEATURES), dtype=jnp.float32)
        b2 = jax.random.uniform(ks[6], (NUM_EXPERTS, IN_FEATURES), dtype=jnp.float32)
        return {'hidden_states': hidden_states, 'wg_red': wg_red, 'wg': wg, 'w1': w1, 'b1': b1, 'w2': w2, 'b2': b2}
    _L0_ffn_in = _L0_ffn_setup()
    _d = {'L0_attn_a_x': _L0_attn_a_in['x'], 'L0_attn_a_W_qkv': _L0_attn_a_in['W_qkv'], 'L0_attn_a_proj': _L0_attn_a_in['proj'], 'L0_attn_a_W_out': _L0_attn_a_in['W_out'], 'L0_attn_a_b_out': _L0_attn_a_in['b_out'], 'L0_attn_b_wq': _L0_attn_b_in['wq'], 'L0_attn_b_wk': _L0_attn_b_in['wk'], 'L0_attn_b_wv': _L0_attn_b_in['wv'], 'L0_attn_b_wg': _L0_attn_b_in['wg'], 'L0_attn_b_wo': _L0_attn_b_in['wo'], 'L0_ffn_wg_red': _L0_ffn_in['wg_red'], 'L0_ffn_wg': _L0_ffn_in['wg'], 'L0_ffn_w1': _L0_ffn_in['w1'], 'L0_ffn_b1': _L0_ffn_in['b1'], 'L0_ffn_w2': _L0_ffn_in['w2'], 'L0_ffn_b2': _L0_ffn_in['b2']}
    _x0 = _d['L0_attn_a_x']
    _d['L0_attn_a_x'] = jax.random.normal(jax.random.fold_in(jax.random.key(seed), 1), (32, 256, 128), dtype=_x0.dtype)
    del _x0
    return _d

def reference(L0_attn_a_x, L0_attn_a_W_qkv, L0_attn_a_proj, L0_attn_a_W_out, L0_attn_a_b_out, L0_attn_b_wq, L0_attn_b_wk, L0_attn_b_wv, L0_attn_b_wg, L0_attn_b_wo, L0_ffn_wg_red, L0_ffn_wg, L0_ffn_w1, L0_ffn_b1, L0_ffn_w2, L0_ffn_b2):

    def _L0_attn_a_ref(x, W_qkv, proj, W_out, b_out):
        import jax, jax.numpy as jnp
        import numpy as np
        B, N, D = (4, 512, 128)
        H, F = (16, 128)
        HD = D // H
        b, n, d = x.shape
        qkv = x @ W_qkv.T
        q, k, v = jnp.split(qkv, 3, axis=-1)
        reshp = lambda t: t.reshape(b, n, H, HD).transpose(0, 2, 1, 3)
        q, k, v = (reshp(q), reshp(k), reshp(v))
        q_p = jax.nn.elu(jnp.einsum('bhnd,hdf->bhnf', q, proj)) + 1.0
        k_p = jax.nn.elu(jnp.einsum('bhnd,hdf->bhnf', k, proj)) + 1.0
        kv = jnp.einsum('bhnf,bhnd->bhfd', k_p, v)
        attn = jnp.einsum('bhnf,bhfd->bhnd', q_p, kv)
        k_sum = k_p.sum(axis=2)
        z = 1.0 / (jnp.einsum('bhnf,bhf->bhn', q_p, k_sum) + 1e-08)
        attn = attn * z[..., None]
        attn = attn.transpose(0, 2, 1, 3).reshape(b, n, d)
        return attn @ W_out.T + b_out

    def _L0_attn_b_ref(x, wq, wk, wv, wg, wo):
        import jax, jax.numpy as jnp
        import numpy as np
        EMBED_DIM = 128
        VALUE_DIM = 256
        NUM_HEADS = 8
        KEY_DIM = EMBED_DIM // NUM_HEADS
        HEAD_DIM = VALUE_DIM // NUM_HEADS
        EPS = 1e-05
        B, S = (2, 256)

        def _xavier(k, shape, gain):
            a = gain * np.sqrt(6.0 / (shape[0] + shape[1]))
            return jax.random.uniform(k, shape, jnp.float32, -a, a)

        def _rel_pos(slen):
            lin = jnp.linspace(0.0, 1.0, KEY_DIM // 2)
            angle = jnp.repeat(1.0 / 10000.0 ** lin, 2)
            decay = jnp.log1p(-2.0 ** (-5.0 - jnp.arange(NUM_HEADS, dtype=jnp.float32)))
            idx = jnp.arange(slen, dtype=jnp.float32)
            sin = jnp.sin(idx[:, None] * angle[None, :])
            cos = jnp.cos(idx[:, None] * angle[None, :])
            diff = idx[:, None] - idx[None, :]
            m = jnp.where(diff[None] >= 0, jnp.exp(diff[None] * decay[:, None, None]), 0.0)
            m = m / jnp.sqrt(m.sum(-1, keepdims=True))
            return (sin, cos, m)

        def _rotate_every_two(x):
            x1 = x[..., ::2]
            x2 = x[..., 1::2]
            return jnp.stack((-x2, x1), axis=-1).reshape(x.shape)
        b, s, _ = x.shape
        sin, cos, mask = _rel_pos(s)
        q = x @ wq
        k = x @ wk * KEY_DIM ** (-0.5)
        v = x @ wv
        g = x @ wg
        q = q.reshape(b, s, NUM_HEADS, KEY_DIM).transpose(0, 2, 1, 3)
        k = k.reshape(b, s, NUM_HEADS, KEY_DIM).transpose(0, 2, 1, 3)
        qr = q * cos + _rotate_every_two(q) * sin
        kr = k * cos + _rotate_every_two(k) * sin
        vr = v.reshape(b, s, NUM_HEADS, HEAD_DIM).transpose(0, 2, 1, 3)
        qk = jnp.einsum('bhik,bhjk->bhij', qr, kr) * mask[None]
        denom = jnp.clip(jnp.abs(jax.lax.stop_gradient(qk).sum(-1, keepdims=True)), 1.0, None)
        qk = qk / denom
        out = jnp.einsum('bhij,bhjd->bihd', qk, vr)
        out = out * jax.lax.rsqrt(jnp.mean(out * out, axis=-1, keepdims=True) + EPS)
        out = out.reshape(b, s, VALUE_DIM)
        out = jax.nn.silu(g) * out
        return out @ wo

    def _L0_ffn_ref(hidden_states, wg_red, wg, w1, b1, w2, b2):
        import jax, jax.numpy as jnp
        import numpy as np
        NUM_EXPERTS = 8
        IN_FEATURES = 128
        HIDDEN_FEATURES = 512
        GATE_DIM = 16
        EPS = 0.0001
        b, t, c = hidden_states.shape
        x = hidden_states.reshape(-1, c)
        xr = x @ wg_red.T
        wg_unit = wg / jnp.maximum(jnp.linalg.norm(wg, axis=1, keepdims=True), EPS)
        logits = xr @ wg_unit.T
        gates = jax.nn.softmax(logits, axis=1)
        indices_s = jnp.argmax(gates, axis=1)
        scores = jnp.max(gates, axis=1)
        E = wg.shape[0]
        out = jnp.zeros_like(x)
        for e in range(E):
            mask = (indices_s == e).astype(x.dtype)[:, None]
            h = jax.nn.gelu(x @ w1[e] + b1[e], approximate=False)
            out = out + mask * (h @ w2[e] + b2[e])
        out = out * scores[:, None]
        return out.reshape(b, t, c)
    x = L0_attn_a_x
    x = x + _L0_attn_a_ref(_layernorm(x, axis=-1), L0_attn_a_W_qkv, L0_attn_a_proj, L0_attn_a_W_out, L0_attn_a_b_out)
    x = x + _L0_ffn_ref(_layernorm(x, axis=-1), L0_ffn_wg_red, L0_ffn_wg, L0_ffn_w1, L0_ffn_b1, L0_ffn_w2, L0_ffn_b2)
    x = x + _L0_attn_b_ref(_layernorm(x, axis=-1), L0_attn_b_wq, L0_attn_b_wk, L0_attn_b_wv, L0_attn_b_wg, L0_attn_b_wo)
    x = x + _L0_ffn_ref(_layernorm(x, axis=-1), L0_ffn_wg_red, L0_ffn_wg, L0_ffn_w1, L0_ffn_b1, L0_ffn_w2, L0_ffn_b2)
    return x

_drawn_inputs = setup_inputs


def setup_inputs(seed=0):
    import zlib

    import numpy as np

    out = dict(_drawn_inputs(seed))
    spreads = {'L0_attn_a_b_out': (0.0, 0.1)}
    factors = {'L0_attn_a_proj': 12.011,
     'L0_attn_b_wq': 8.0,
     'L0_attn_b_wk': 8.0,
     'L0_attn_b_wv': 8.0,
     'L0_attn_b_wg': 8.0,
     'L0_attn_b_wo': 8.0,
     'L0_ffn_b1': 3.881,
     'L0_ffn_b2': 8.0}
    for name, (base, spread) in spreads.items():
        noise = np.random.default_rng([zlib.crc32(name.encode()), seed]).standard_normal(out[name].shape)
        drawn = base * np.exp(spread * noise) if base else spread * noise
        out[name] = jnp.asarray(drawn.astype(out[name].dtype))
    for name, factor in factors.items():
        out[name] = (out[name] * factor).astype(out[name].dtype)
    return out
```

```python
from contextlib import ExitStack

import numpy as np

import concourse.bass as bass
from concourse import mybir

F32 = mybir.dt.float32
BF16 = mybir.dt.bfloat16
I32 = mybir.dt.int32
ALU = mybir.AluOpType
ACT = mybir.ActivationFunctionType
AX = mybir.AxisListType.X
ds = bass.ds

P = 128
NB = 32
TPB = 2
NT = NB * TPB
D = 128
EPS = 1e-5
H, HD, F = 16, 8, 128
KVW = HD + 1
U = 16
E, HID, GD = 8, 512, 16
HC = HID // P
NBLK = NT + E
W1W = HID + HC
RH, KD, VD = 8, 16, 256
RHD = VD // RH
RW = RHD + 1
SC = 3 * P


def build(nc, ap, out):
    ctx = ExitStack()

    def sb(name, shape, dt=F32):
        return ctx.enter_context(nc.sbuf_tensor(name, shape, dt))

    def sem(name):
        return ctx.enter_context(nc.semaphore(name))

    with ctx:
        bank = [ctx.enter_context(nc.psum_tensor(f"bank{i}", [P, 512], F32)) for i in range(8)]
        xs = sb("xs", [P, NT, D])
        xn_all = sb("xn_all", [P, NT, D])
        ident = sb("ident", [P, P])
        buf = dict(
            bank=bank, xs=xs, xn_all=xn_all, ident=ident,
            xn=sb("xn", [P, TPB, D]), xnT=sb("xnT", [P, TPB * P]),
            stats=sb("stats", [P, TPB, 6]), both=sb("both", [P, TPB, 2]),
            diff=sb("diff", [P, TPB]), sq=sb("sq", [P, TPB]), mean=sb("mean", [P, TPB]), quarter=sb("quarter", [P, TPB]),
            var=sb("var", [P, TPB]), rstd=sb("rstd", [P, TPB]), mhalf=sb("mhalf", [P, 16]),
        )
        xdisp = nc.dram_tensor("xdisp", (NBLK * P, D), F32).ap()
        ydisp = nc.dram_tensor("ydisp", (NBLK * P, D), F32).ap()
        ldx = [sem(f"ld_x{i}") for i in range(8)]

        moe = dict(
            w1b=sb("w1b", [P, E, W1W]), w2s=sb("w2s", [P, E * HC, D]), b2bc=sb("b2bc", [P, E * D]),
            G=sb("G", [P, E]), U128=sb("U128", [P, P]), ones=sb("ones", [P, P]), xdisp=xdisp, ydisp=ydisp,
        )
        setup(nc, ap, buf, moe, ldx, sem, sb)
        linear_attention(nc, ap, buf, ldx, sem)
        expert_layer(nc, ap, buf, moe, sem, "f0")
        retention(nc, ap, buf, sem)
        expert_layer(nc, ap, buf, moe, sem, "f1")

        st = sem("store_x")
        block = ctx.enter_context(nc.Block())

        @block.sync
        def _(sp):
            sp.dma_start(out, xs[:, :, :]).then_inc(st, 16)
            sp.wait_ge(st, 16)


def setup(nc, ap, buf, moe, ldx, sem, sb):
    ld_c, ld_w, gate_step, zero_step = sem("ld_const"), sem("ld_moe"), sem("gate_step"), sem("zero_step")
    ld_z = sem("ld_zero")
    pe_g, dve_g = sem("gate_pe"), sem("gate_dve")
    bank = buf["bank"]
    with (
        nc.sbuf_tensor("wgr", [GD, D], F32) as wgr,
        nc.sbuf_tensor("wge", [E, GD], F32) as wge,
        nc.sbuf_tensor("wsq", [E, GD], F32) as wsq,
        nc.sbuf_tensor("wn", [E, 4], F32) as wn,
        nc.sbuf_tensor("wgT", [GD, E], F32) as wgT,
        nc.sbuf_tensor("zrow", [P, 8 * D], F32) as zrow,
        nc.Block() as block,
    ):
        @block.sync
        def _(sp):
            for i in range(8):
                sp.dma_start(buf["xs"][:, 8 * i:8 * i + 8, :], ap["x"][:, 8 * i:8 * i + 8, :]).then_inc(ldx[i], 16)

        @block.scalar
        def _(act):
            act.dma_start(buf["ident"][:], ap["ident"]).then_inc(ld_c, 16)
            act.dma_start(wgr[:], ap["wg_red"]).then_inc(ld_c, 16)
            act.dma_start(wge[:], ap["wg"]).then_inc(ld_c, 16)
            act.dma_start(moe["U128"][:], ap["before"]).then_inc(ld_c, 16)
            act.dma_start(moe["w1b"][:, :, 0:HID], ap["w1"]).then_inc(ld_w, 16)
            act.dma_start(moe["w1b"][:, :, HID:W1W], ap["b1"]).then_inc(ld_w, 16)
            act.dma_start(moe["w2s"][:], ap["w2"]).then_inc(ld_w, 16)
            act.dma_start(moe["b2bc"][:], ap["b2"].to_broadcast([P, E * D])).then_inc(ld_w, 16)
            act.wait_ge(zero_step, 1)
            for i in range(NBLK // 8):
                act.dma_start(moe["xdisp"][i * 1024:(i + 1) * 1024, :].rearrange("(p r) d -> p (r d)", p=P),
                              zrow[:]).then_inc(ld_z, 16)
            act.wait_ge(ld_z, 16 * (NBLK // 8))
            act.wait_ge(ld_w, 64)

        @block.gpsimd
        def _(pool):
            nc.gpsimd.memset(zrow[:], 0.0).then_inc(zero_step, 1)
            nc.gpsimd.memset(buf["mhalf"][:], -0.5)
            nc.gpsimd.memset(buf["quarter"][:], 0.25)

        @block.vector
        def _(dve):
            nc.vector.memset(moe["ones"][:], 1.0)
            dve.wait_ge(ld_c, 64)
            nc.vector.tensor_tensor(wsq[:], wge[:], wge[:], ALU.mult).then_inc(dve_g, 1)
            dve.wait_ge(dve_g, 1)
            nc.vector.reduce_sum(wn[:, 0:1], wsq[:], AX).then_inc(dve_g, 1)
            dve.wait_ge(gate_step, 1)
            nc.vector.tensor_scalar_max(wn[:, 2:3], wn[:, 1:2], 1e-4).then_inc(dve_g, 1)
            dve.wait_ge(dve_g, 3)
            nc.vector.reciprocal(wn[:, 3:4], wn[:, 2:3]).then_inc(dve_g, 1)
            dve.wait_ge(dve_g, 4)
            nc.vector.tensor_scalar(wsq[:], wge[:], wn[:, 3:4], None, ALU.mult).then_inc(dve_g, 1)
            dve.wait_ge(pe_g, 1)
            nc.vector.tensor_copy(wgT[:], bank[0][0:GD, 0:E]).then_inc(dve_g, 1)
            dve.wait_ge(pe_g, 2)
            nc.vector.tensor_copy(moe["G"][:], bank[1][:, 0:E])

        @block.scalar
        def _(act):
            act.wait_ge(dve_g, 2)
            nc.scalar.activation(wn[:, 1:2], wn[:, 0:1], ACT.Sqrt).then_inc(gate_step, 1)

        @block.tensor
        def _(pe):
            pe.wait_ge(dve_g, 5)
            nc.tensor.transpose(bank[0][0:GD, 0:E], wsq[:], buf["ident"][0:E, 0:E]).then_inc(pe_g, 1)
            pe.wait_ge(dve_g, 6)
            nc.tensor.matmul(bank[1][:, 0:E], wgr[:], wgT[:], start=True, stop=True).then_inc(pe_g, 1)


class Norm:

    def __init__(self, nc, buf, sem, tag):
        self.nc, self.buf = nc, buf
        self.stat, self.power, self.done = sem(f"{tag}_ln_stat"), sem(f"{tag}_ln_power"), sem(f"{tag}_ln_done")

    def stats(self, dve, b):
        nc, buf = self.nc, self.buf
        for t in range(TPB):
            nc.vector.bn_stats(buf["stats"][:, t, :], buf["xs"][:, 2 * b + t, :]).then_inc(self.stat, 1)
        st = buf["stats"][:].rearrange("p t (o c) -> p t o c", o=2)
        dve.wait_ge(self.stat, 4 * b + 2)
        nc.vector.tensor_tensor(buf["both"][:], st[:, :, 0, 1:3], st[:, :, 1, 1:3], ALU.add).then_inc(self.stat, 1)
        nc.vector.tensor_tensor(buf["diff"][:], st[:, :, 0, 1], st[:, :, 1, 1], ALU.subtract).then_inc(self.stat, 1)

    def root(self, pool, b):
        nc, buf = self.nc, self.buf
        pool.wait_ge(self.stat, 4 * b + 4)
        nc.gpsimd.tensor_tensor(buf["sq"][:], buf["diff"][:], buf["diff"][:], ALU.mult).then_inc(self.power, 1)
        nc.gpsimd.tensor_scalar(buf["mean"][:], buf["both"][:, :, 0], 0.5, 0.0, ALU.mult, ALU.add).then_inc(self.power, 1)
        nc.gpsimd.tensor_scalar(buf["var"][:], buf["both"][:, :, 1], 1.0 / D, EPS, ALU.mult, ALU.add).then_inc(self.power, 1)
        pool.wait_ge(self.power, 6 * b + 1)
        nc.gpsimd.tensor_tensor(buf["sq"][:], buf["sq"][:], buf["quarter"][:], ALU.mult).then_inc(self.power, 1)
        pool.wait_ge(self.power, 6 * b + 4)
        nc.gpsimd.tensor_tensor(buf["var"][:], buf["var"][:], buf["sq"][:], ALU.add).then_inc(self.power, 1)
        pool.wait_ge(self.power, 6 * b + 5)
        nc.gpsimd.tensor_tensor(buf["rstd"][:], buf["var"][:], buf["mhalf"][:, 0:TPB], ALU.pow).then_inc(self.power, 1)

    def scale(self, dve, b, dst):
        nc, buf = self.nc, self.buf
        dve.wait_ge(self.power, 6 * b + 6)
        for t in range(TPB):
            last = nc.vector.tensor_scalar(dst(t), buf["xs"][:, 2 * b + t, :], buf["mean"][:, t:t + 1],
                                           buf["rstd"][:, t:t + 1], ALU.subtract, ALU.mult)
        last.then_inc(self.done, 1)


def linear_attention(nc, ap, buf, ldx, sem):
    bank, ident = buf["bank"], buf["ident"]
    biased, neg_act, neg_dve = sem("a_biased"), sem("a_neg_act"), sem("a_neg_dve")
    T_BANK, QK_BANK, VY_BANK, KV_BANK = bank[4], bank[5], bank[6], bank[7]
    kv_ps = KV_BANK[:, 0:H * KVW]
    at_ps = KV_BANK[:, H * KVW:3 * H * KVW].rearrange("p (t h c) -> p t h c", t=TPB, h=H)
    v_ps = VY_BANK[:, 0:TPB * D].rearrange("p (t h c) -> p t h c", t=TPB, h=H)
    y_ps = VY_BANK[:, 256:512].rearrange("p (t c) -> p t c", t=TPB)
    ld, setup_done, ld_p = sem("a_ld"), sem("a_setup"), sem("a_ld_proj")
    proj_zero = sem("a_proj_zero")
    ln = Norm(nc, buf, sem, "a")
    xnT_ps, xnT_sb, qkv_ps, kT_sb, qT_sb, v_sb = (sem("a_" + n) for n in
                                                  ("xnT_ps", "xnT_sb", "qkv_ps", "kT_sb", "qT_sb", "v_sb"))
    feat, expd, phi = sem("a_feature"), sem("a_exp"), sem("a_phi")
    kv_done, kv_sb_done, at_done, an_step, an_done = (sem("a_" + n) for n in
                                                      ("kv_done", "kv_sb", "at_done", "an_step", "an_done"))
    anT_ps, anT_sb_done, y_done, x_added = (sem("a_" + n) for n in ("anT_ps", "anT_sb", "y_ps", "x_added"))
    with ExitStack() as c:
        def sb(name, shape, dt=F32):
            return c.enter_context(nc.sbuf_tensor(name, shape, dt))
        wqkv, wout, bout = sb("wqkv", [P, 3 * D]), sb("wout", [P, D]), sb("bout", [P, D])
        proj = sb("proj", [P, H * F])
        kT, qT = sb("kT", [P, 256]), sb("qT", [P, 256])
        v9 = sb("v9", [P, TPB, H, KVW])
        neg, ex = sb("neg", [P, 4, 512]), sb("ex", [P, 4, 512])
        kphi, qphi = sb("kphi", [P, 8, 512]), sb("qphi", [P, 4, 512])
        kv = sb("kv", [P, H * KVW])
        den, rec = sb("den", [P, TPB, H]), sb("rec", [P, TPB, H])
        an, anT = sb("an", [P, TPB, D]), sb("anT", [P, TPB * P])
        block = c.enter_context(nc.Block())

        @block.sync
        def _(sp):
            sp.dma_start(wqkv[:], ap["wqkvT"]).then_inc(ld, 16)
            sp.dma_start(wout[:], ap["woutT"]).then_inc(ld, 16)
            sp.dma_start(bout[:], ap["b_out"].to_broadcast([P, D])).then_inc(ld, 16)
            sp.wait_ge(proj_zero, 1)
            for h in range(H):
                sp.dma_start(proj[HD * h:HD * h + HD, h * F:(h + 1) * F], ap["proj"][h]).then_inc(ld_p, 16)

        @block.gpsimd
        def _(pool):
            nc.gpsimd.memset(proj[:], 0.0).then_inc(proj_zero, 1)
            nc.gpsimd.memset(v9[:], 1.0).then_inc(setup_done, 1)
            with pool.Fori(0, NB) as b:
                ln.root(pool, b)

        def xn_transposes(pe, b):
            pe.wait_ge(ln.done, b + 1)
            for t in range(TPB):
                last = nc.tensor.transpose(T_BANK[:, t * P:(t + 1) * P], buf["xn"][:, t, :], ident[:])
            last.then_inc(xnT_ps, 1)

        def qkv(pe, b):
            pe.wait_ge(xnT_sb, b + 1)
            for j in range(2):
                nc.tensor.matmul(QK_BANK[:, j * 256:(j + 1) * 256], wqkv[:, j * D:(j + 1) * D], buf["xnT"][:],
                                 start=True, stop=True)
            for t in range(TPB):
                last = nc.tensor.matmul(VY_BANK[:, t * D:(t + 1) * D], buf["xnT"][:, t * P:(t + 1) * P],
                                        wqkv[:, 2 * D:3 * D], start=True, stop=True)
            last.then_inc(qkv_ps, 1)

        @block.tensor
        def _(pe):
            def feature(b, s, first):
                if s == 0:
                    pe.wait_ge(kT_sb, b + 1)
                if s == 8:
                    pe.wait_ge(qT_sb, b + 1)
                if not (first and s < 4):
                    pe.wait_ge(phi, U * b + s - 3)
                dst = bank[s % 4]
                if s < 8:
                    g, t = s // 2, s % 2
                    nc.tensor.matmul(dst[:], kT[:, t * P:(t + 1) * P], proj[:, g * 512:(g + 1) * 512],
                                     start=True, stop=True).then_inc(feat, 1)
                else:
                    for j in range(2):
                        h = 2 * (s - 8) + j
                        last = nc.tensor.matmul(dst[:, j * 256:(j + 1) * 256], proj[:, h * F:(h + 1) * F], qT[:],
                                                start=True, stop=True)
                    last.then_inc(feat, 1)

            def key_value(b, g, first):
                pe.wait_ge(phi, U * b + 2 * g + 2)
                if g == 0:
                    pe.wait_ge(v_sb, b + 1)
                    if not first:
                        pe.wait_ge(an_done, b)
                for j in range(4):
                    h = 4 * g + j
                    for t in range(TPB):
                        last = nc.tensor.matmul(kv_ps[:, h * KVW:(h + 1) * KVW],
                                                kphi[:, 2 * g + t, j * F:(j + 1) * F], v9[:, t, h, :],
                                                start=(t == 0), stop=(t == 1))
                last.then_inc(kv_done, 1)

            def attend(b, w):
                pe.wait_ge(phi, U * b + 8 + w + 1)
                if w == 0:
                    pe.wait_ge(kv_sb_done, b + 1)
                for j in range(2):
                    h = 2 * w + j
                    for t in range(TPB):
                        last = nc.tensor.matmul(at_ps[:, t, h, :], qphi[:, w % 4, j * 256 + t * P:j * 256 + (t + 1) * P],
                                                kv[:, h * KVW:(h + 1) * KVW], start=True, stop=True)
                last.then_inc(at_done, 1)

            def an_transposes(b, last_batch):
                pe.wait_ge(an_done, b + 1)
                pe.wait_ge(qT_sb, b + (1 if last_batch else 2))
                for t in range(TPB):
                    last = nc.tensor.transpose(QK_BANK[:, t * P:(t + 1) * P], an[:, t, :], ident[:])
                last.then_inc(anT_ps, 1)

            def project(b, last_batch):
                pe.wait_ge(anT_sb_done, b + 1)
                pe.wait_ge(v_sb, b + (1 if last_batch else 2))
                for t in range(TPB):
                    last = nc.tensor.matmul(y_ps[:, t, :], anT[:, t * P:(t + 1) * P], wout[:], start=True, stop=True)
                last.then_inc(y_done, 1)

            def body(b, first=False, last=False):
                for s in range(U):
                    feature(b, s, first)
                    if s < 4 and not first:
                        attend(b - 1, 4 + s)
                    if s in (5, 7, 9, 11):
                        key_value(b, (s - 5) // 2, first)
                    if s == 6 and not first:
                        an_transposes(b - 1, False)
                    if s == 6 and not last:
                        xn_transposes(pe, b + 1)
                    if s == 8 and not first:
                        project(b - 1, False)
                    if s == 10 and not last:
                        if not first:
                            pe.wait_ge(x_added, b)
                            pe.wait_ge(anT_sb_done, b)
                        qkv(pe, b + 1)
                    if s >= 12:
                        attend(b, s - 12)

            pe.wait_ge(ld, 48)
            pe.wait_ge(ld_p, 16 * H)
            pe.wait_ge(setup_done, 1)
            xn_transposes(pe, 0)
            qkv(pe, 0)
            body(0, first=True)
            with pe.Fori(1, NB - 1) as b:
                body(b)
            body(NB - 1, last=True)
            for w in (4, 5, 6, 7):
                attend(NB - 1, w)
            an_transposes(NB - 1, True)
            project(NB - 1, True)

        @block.scalar
        def _(act):
            def copy_xnT(b):
                act.wait_ge(xnT_ps, b + 1)
                nc.scalar.copy(buf["xnT"][:], T_BANK[:, 0:256]).then_inc(xnT_sb, 1)

            def copy_k(b):
                act.wait_ge(qkv_ps, b + 1)
                nc.scalar.copy(kT[:], QK_BANK[:, 256:512]).then_inc(kT_sb, 1)

            def copy_q(b):
                nc.scalar.copy(qT[:], QK_BANK[:, 0:256]).then_inc(qT_sb, 1)

            def copy_v(b, first):
                if not first:
                    act.wait_ge(kv_done, 4 * b)
                nc.scalar.copy(v9[:, :, :, 0:HD], v_ps).then_inc(v_sb, 1)

            def copy_anT(b):
                act.wait_ge(anT_ps, b + 1)
                nc.scalar.copy(anT[:], QK_BANK[:, 0:256]).then_inc(anT_sb_done, 1)

            def negative(b, s):
                act.wait_ge(feat, U * b + s + 1)
                nc.scalar.activation(neg[:, s % 4, :], bank[s % 4][:], ACT.Relu, scale=-1.0).then_inc(neg_act, 1)

            def exponential(b, s):
                if s % 2 == 0:
                    act.wait_ge(neg_act, U // 2 * b + s // 2 + 1)
                else:
                    act.wait_ge(neg_dve, U // 2 * b + s // 2 + 1)
                nc.scalar.activation(ex[:, s % 4, :], neg[:, s % 4, :], ACT.Exp,
                                     scale=-1.0 if s % 2 == 0 else 1.0).then_inc(expd, 1)

            def body(b, first=False, last=False):
                for s in range(U):
                    if s % 2 == 0:
                        negative(b, s)
                    if s > 0:
                        exponential(b, s - 1)
                    elif not first:
                        exponential(b - 1, U - 1)
                    if s == 2:
                        copy_q(b)
                    if s == 7 and not first:
                        copy_anT(b - 1)
                    if s == 7 and not last:
                        copy_xnT(b + 1)
                    if s == 11 and not last:
                        copy_k(b + 1)
                    if s == 12 and not last:
                        copy_v(b + 1, False)

            act.wait_ge(setup_done, 1)
            copy_xnT(0)
            copy_k(0)
            copy_v(0, True)
            body(0, first=True)
            with act.Fori(1, NB - 1) as b:
                body(b)
            body(NB - 1, last=True)
            exponential(NB - 1, U - 1)
            copy_anT(NB - 1)

        @block.vector
        def _(dve):
            def xn(t):
                return buf["xn"][:, t, :]

            def normalise(b):
                dve.wait_ge(at_done, 8 * (b + 1))
                nc.vector.tensor_scalar(den[:], at_ps[:, :, :, HD], 1e-8, None, ALU.add).then_inc(an_step, 1)
                dve.wait_ge(an_step, 2 * b + 1)
                nc.vector.reciprocal(rec[:], den[:]).then_inc(an_step, 1)
                dve.wait_ge(an_step, 2 * b + 2)
                for t in range(TPB):
                    last = nc.vector.tensor_tensor(an[:, t, :].rearrange("p (h c) -> p h c", h=H), at_ps[:, t, :, 0:HD],
                                                   rec[:, t, :, None].to_broadcast([P, H, HD]), ALU.mult)
                last.then_inc(an_done, 1)

            def add_bias(b):
                nc.vector.tensor_tensor(buf["xs"][:, ds(2 * b, 2), :], buf["xs"][:, ds(2 * b, 2), :],
                                        bout[:, None, :].to_broadcast([P, TPB, D]), ALU.add).then_inc(biased, 1)

            def add_y(b):
                dve.wait_ge(y_done, b + 1)
                dve.wait_ge(biased, b + 1)
                nc.vector.tensor_tensor(buf["xs"][:, ds(2 * b, 2), :], y_ps, buf["xs"][:, ds(2 * b, 2), :],
                                        ALU.add).then_inc(x_added, 1)

            def negative(b, s):
                dve.wait_ge(feat, U * b + s + 1)
                nc.vector.tensor_scalar_min(neg[:, s % 4, :], bank[s % 4][:], 0.0).then_inc(neg_dve, 1)

            def features(b, s, first):
                dve.wait_ge(expd, U * b + s + 1)
                if s < 8:
                    if not first:
                        dve.wait_ge(kv_done, 4 * b - 4 + s // 2 + 1)
                    dst = kphi[:, s, :]
                else:
                    w = s - 8
                    if w >= 4:
                        dve.wait_ge(at_done, 8 * b + w - 3)
                    elif not first:
                        dve.wait_ge(at_done, 8 * b - 8 + w + 5)
                    dst = qphi[:, w % 4, :]
                nc.vector.scalar_tensor_tensor(dst, bank[s % 4][:], 0.0, ex[:, s % 4, :], ALU.max,
                                               ALU.add).then_inc(phi, 1)

            def body(b, first=False, last=False):
                for s in range(U):
                    if s % 2:
                        negative(b, s)
                    if s >= 2:
                        features(b, s - 2, first)
                    elif not first:
                        features(b - 1, U - 2 + s, False)
                    if s == 2 and not last:
                        ln.stats(dve, b + 1)
                    if s == 4 and not first:
                        normalise(b - 1)
                    if s == 4 and not last:
                        dve.wait_ge(xnT_ps, b + 1)
                        ln.scale(dve, b + 1, xn)
                    if s == 5:
                        add_bias(b)
                    if s == 9 and not first:
                        add_y(b - 1)
                    if s == 12:
                        dve.wait_ge(kv_done, 4 * b + 4)
                        nc.vector.tensor_copy(kv[:], kv_ps).then_inc(kv_sb_done, 1)

            dve.wait_ge(setup_done, 1)
            dve.wait_ge(ld, 48)
            for i in range(8):
                dve.wait_ge(ldx[i], 16)
            ln.stats(dve, 0)
            ln.scale(dve, 0, xn)
            body(0, first=True)
            with dve.Fori(1, NB - 1) as b:
                body(b)
            body(NB - 1, last=True)
            features(NB - 1, U - 2, False)
            features(NB - 1, U - 1, False)
            normalise(NB - 1)
            add_y(NB - 1)


def expert_layer(nc, ap, buf, moe, sem, tag):
    bank, ident, xs, xn_all = buf["bank"], buf["ident"], buf["xs"], buf["xn_all"]
    S = lambda n: sem(f"{tag}_{n}")
    ln = Norm(nc, buf, sem, tag)
    xnT_ps, xnT_sb, lg_ps, lg_sb = S("xnT_ps"), S("xnT_sb"), S("logit_ps"), S("logit_sb")
    step, expd, rank_ps, routed = S("step"), S("exp"), S("rank_ps"), S("routed")
    scat, wl, xl, st, gat = S("scatter"), [S("ld_w0"), S("ld_w1")], [S("ld_x0"), S("ld_x1")], [S("st_y0"), S("st_y1")], [S(f"gather{i}") for i in range(8)]
    xT_ps, xT_sb, h_ps, h_sb, w_used, y_ps_done, y_sb = (S(n) for n in
                                                         ("xT_ps", "xT_sb", "h_ps", "h_sb", "w_used", "y_ps", "y_sb"))
    pld, onehot, shifted = S("ld_pos"), S("onehot"), S("shifted")
    with ExitStack() as c:
        def sb(name, shape, dt=F32):
            return c.enter_context(nc.sbuf_tensor(f"{tag}_{name}", shape, dt))
        lg, oh, t1, t2, t3 = (sb(n, [P, NT, E]) for n in ("lg", "oh", "t1", "t2", "t3"))
        m, sc = sb("m", [P, NT]), sb("sc", [P, NT])
        pos, posi = sb("pos", [P, NT]), sb("posi", [P, NT], I32)
        tot, off, nbi = sb("tot", [P, E]), sb("off", [P, E + 1]), sb("nbi", [P, E], I32)
        cnt, eb, cmp8 = sb("cnt", [P, NBLK]), sb("eb", [P, NBLK], I32), sb("cmp8", [P, NBLK, E])
        prio, start = sb("prio", [P, E]), sb("start", [P, NBLK])
        wc = sb("wc", [P, 2, W1W])
        xb, xT, hT, yb = sb("xb", [P, 2, D]), sb("xT", [P, 2, P]), sb("hT", [P, 2, HC * P]), sb("yb", [P, 2, D])

        with nc.Block() as block:
            @block.sync
            def _(sp):
                sp.dma_start(prio[:], ap["prio"].to_broadcast([P, E])).then_inc(pld, 16)
                sp.dma_start(start[:], ap["start"].to_broadcast([P, NBLK])).then_inc(pld, 16)

            @block.gpsimd
            def _(pool):
                with pool.Fori(0, NB) as b:
                    ln.root(pool, b)
                pool.wait_ge(routed, 1)
                for i in range(NT):
                    pool.indirect_dma_start(moe["xdisp"], bass.IndirectOffsetOnAxis(ap=posi[:, i:i + 1], axis=0),
                                            xn_all[:, i, :], None).then_inc(scat, 16)
                pool.wait_ge(scat, 16 * NT)

            @block.tensor
            def _(pe):
                def body(b, first):
                    pe.wait_ge(ln.done, b + 1)
                    if not first:
                        pe.wait_ge(xnT_sb, b)
                    for t in range(TPB):
                        last = nc.tensor.transpose(bank[0][:, t * P:(t + 1) * P], buf["xn"][:, t, :], ident[:])
                    last.then_inc(xnT_ps, 1)
                    pe.wait_ge(xnT_sb, b + 1)
                    if not first:
                        pe.wait_ge(lg_sb, b)
                    for t in range(TPB):
                        last = nc.tensor.matmul(bank[1][:, t * E:(t + 1) * E], buf["xnT"][:, t * P:(t + 1) * P],
                                                moe["G"][:], start=True, stop=True)
                    last.then_inc(lg_ps, 1)
                body(0, True)
                with pe.Fori(1, NB) as b:
                    body(b, False)
                pe.wait_ge(onehot, 1)
                ohf = oh[:].rearrange("p t e -> p (t e)")
                nc.tensor.matmul(bank[2][:], moe["U128"][:], ohf, start=True, stop=True)
                nc.tensor.matmul(bank[3][:], moe["ones"][:], ohf, start=True, stop=True).then_inc(rank_ps, 1)

            @block.scalar
            def _(act):
                def body(b, first):
                    if not first:
                        act.wait_ge(lg_ps, b)
                    act.wait_ge(xnT_ps, b + 1)
                    nc.scalar.copy(buf["xnT"][:], bank[0][:, 0:256]).then_inc(xnT_sb, 1)
                body(0, True)
                with act.Fori(1, NB) as b:
                    body(b, False)
                act.wait_ge(shifted, 2)
                nc.scalar.activation(t1[:], t1[:], ACT.Exp).then_inc(expd, 1)

            @block.vector
            def _(dve):
                def xn(t):
                    return buf["xn"][:, t, :]

                def body(b, first):
                    ln.stats(dve, b)
                    if not first:
                        dve.wait_ge(xnT_ps, b)
                    ln.scale(dve, b, xn)
                    dve.wait_ge(ln.done, b + 1)
                    nc.vector.tensor_copy(xn_all[:, ds(2 * b, 2), :], buf["xn"][:])
                    dve.wait_ge(lg_ps, b + 1)
                    nc.vector.tensor_copy(lg[:, ds(2 * b, 2), :], bank[1][:, 0:TPB * E].rearrange(
                        "p (t e) -> p t e", t=TPB)).then_inc(lg_sb, 1)
                body(0, True)
                with dve.Fori(1, NB) as b:
                    body(b, False)

                n = [0]

                def then(ins):
                    n[0] += 1
                    ins.then_inc(step, 1)
                    dve.wait_ge(step, n[0])

                def over_e(a):
                    return a[:, :, None].to_broadcast([P, NT, E])

                dve.wait_ge(lg_sb, NB)
                dve.wait_ge(pld, 32)
                then(nc.vector.reduce_max(m[:], lg[:], AX))
                nc.vector.tensor_tensor(t1[:], lg[:], over_e(m), ALU.subtract).then_inc(shifted, 1)
                dve.wait_ge(shifted, 1)
                nc.vector.tensor_scalar(t2[:], t1[:], 0.0, None, ALU.is_equal).then_inc(shifted, 1)
                dve.wait_ge(shifted, 2)
                then(nc.vector.tensor_tensor(t2[:], t2[:], prio[:, None, :].to_broadcast([P, NT, E]), ALU.mult))
                then(nc.vector.reduce_max(m[:], t2[:], AX))
                nc.vector.tensor_tensor(oh[:], t2[:], over_e(m), ALU.is_equal).then_inc(onehot, 1)
                dve.wait_ge(expd, 1)
                then(nc.vector.reduce_sum(sc[:], t1[:], AX))
                then(nc.vector.reciprocal(sc[:], sc[:]))
                dve.wait_ge(rank_ps, 1)
                then(nc.vector.tensor_copy(t1[:], bank[3][:].rearrange("p (t e) -> p t e", e=E)))
                then(nc.vector.tensor_copy(t3[:], t1[:]))
                a, z = t1, t2
                k = 1
                while k < NT:
                    nc.vector.tensor_copy(z[:, 0:k, :], a[:, 0:k, :])
                    then(nc.vector.tensor_tensor(z[:, k:NT, :], a[:, k:NT, :], a[:, 0:NT - k, :], ALU.add))
                    a, z = z, a
                    k *= 2
                then(nc.vector.tensor_scalar(nbi[:], a[:, NT - 1, :], float(P - 1), None, ALU.add))
                then(nc.vector.tensor_single_scalar(nbi[:], nbi[:], -P, ALU.bitwise_and))
                then(nc.vector.tensor_copy(tot[:], nbi[:]))
                then(nc.vector.memset(off[:, 0:1], 0.0))
                for e in range(E):
                    then(nc.vector.tensor_tensor(off[:, e + 1:e + 2], off[:, e:e + 1], tot[:, e:e + 1], ALU.add))
                then(nc.vector.tensor_tensor(a[:], a[:], t3[:], ALU.subtract))
                then(nc.vector.tensor_tensor(a[:], a[:], bank[2][:].rearrange("p (t e) -> p t e", e=E), ALU.add))
                then(nc.vector.tensor_tensor(a[:], a[:], off[:, None, 0:E].to_broadcast([P, NT, E]), ALU.add))
                then(nc.vector.tensor_tensor(a[:], a[:], oh[:], ALU.mult))
                then(nc.vector.reduce_sum(pos[:], a[:], AX))
                nc.vector.tensor_copy(posi[:], pos[:]).then_inc(routed, 1)
                then(nc.vector.tensor_tensor(cmp8[:], off[:, None, 1:E + 1].to_broadcast([P, NBLK, E]),
                                             start[:, :, None].to_broadcast([P, NBLK, E]), ALU.is_le))
                then(nc.vector.reduce_sum(cnt[:], cmp8[:], AX))
                then(nc.vector.tensor_scalar(eb[:], cnt[:], float(E - 1), None, ALU.min))

        with nc.Block() as block:
            NI = NBLK // 2

            @block.sync
            def _(sp):
                def body(i, first):
                    for p in range(2):
                        j = 2 * i + p
                        if not first:
                            sp.wait_ge(w_used, j - 1)
                            sp.wait_ge(xT_ps, j - 1)
                        e = sp.value_load(eb[0:1, ds(j, 1)], min_val=0, max_val=E - 1)
                        sp.dma_start(wc[:, p, None, :], moe["w1b"][:, ds(e, 1), :]).then_inc(wl[p], 16)
                        sp.dma_start(xb[:, p, :], moe["xdisp"][ds(j * P, P), :]).then_inc(xl[p], 16)
                body(0, True)
                with sp.Fori(1, NI) as i:
                    body(i, False)

            @block.tensor
            def _(pe):
                def tr(i, p, j, first):
                    pe.wait_ge(xl[p], 16 * i + 16)
                    if not first:
                        pe.wait_ge(xT_sb, j - 1)
                    nc.tensor.transpose(bank[p][:, 0:P], xb[:, p, :], ident[:]).then_inc(xT_ps, 1)

                def hidden(i, p, j, first):
                    pe.wait_ge(xT_sb, j + 1)
                    pe.wait_ge(wl[p], 16 * i + 16)
                    if not first:
                        pe.wait_ge(h_sb, HC * (j - 1))
                    for k in range(HC):
                        last = nc.tensor.matmul(bank[2 + p][:, k * P:(k + 1) * P], wc[:, p, k * P:(k + 1) * P],
                                                xT[:, p, :], start=True, stop=True)
                    last.then_inc(h_ps, 1)

                def result(i, p, j, first):
                    pe.wait_ge(h_sb, HC * (j + 1))
                    if not first:
                        pe.wait_ge(y_sb, j - 1)
                    e = pe.value_load(eb[0:1, ds(j, 1)], min_val=0, max_val=E - 1)
                    for k in range(HC):
                        last = nc.tensor.matmul(bank[4 + p][:, None, 0:D], hT[:, p, k * P:(k + 1) * P],
                                                moe["w2s"][:, ds(e * HC + k, 1), :], start=(k == 0), stop=(k == HC - 1))
                    last.then_inc(w_used, 1)

                def body(i, first):
                    for p in range(2):
                        j = 2 * i + p
                        tr(i, p, j, first)
                        hidden(i, p, j, first)
                        if p == 1:
                            result(i, 0, j - 1, first)
                        elif not first:
                            result(i - 1, 1, j - 1, i == 1 if isinstance(i, int) else False)
                body(0, True)
                body_i = 1
                for p in range(2):
                    j = 2 + p
                    tr(body_i, p, j, False)
                    hidden(body_i, p, j, False)
                    result(body_i - 1 + p, 1 - p, j - 1, p == 0)
                with pe.Fori(2, NI) as i:
                    body(i, False)
                result(NI - 1, 1, NBLK - 1, False)

            @block.scalar
            def _(act):
                def body(i, first):
                    for p in range(2):
                        j = 2 * i + p
                        act.wait_ge(h_ps, j + 1)
                        if not first:
                            act.wait_ge(w_used, j - 1)
                        for k in range(HC):
                            nc.scalar.activation(hT[:, p, k * P:(k + 1) * P], bank[2 + p][:, k * P:(k + 1) * P],
                                                 ACT.Gelu, bias=wc[:, p, HID + k:HID + k + 1]).then_inc(h_sb, 1)
                body(0, True)
                with act.Fori(1, NI) as i:
                    body(i, False)

            @block.vector
            def _(dve):
                def xT_copy(i, p, j, first):
                    dve.wait_ge(xT_ps, j + 1)
                    if not first:
                        dve.wait_ge(h_ps, j - 1)
                    nc.vector.tensor_copy(xT[:, p, :], bank[p][:, 0:P]).then_inc(xT_sb, 1)

                def y_copy(i, p, j, first):
                    dve.wait_ge(w_used, j + 1)
                    if not first:
                        dve.wait_ge(st[p], 16 * i)
                    e = dve.value_load(eb[0:1, ds(j, 1)], min_val=0, max_val=E - 1)
                    nc.vector.tensor_tensor(yb[:, p, :], bank[4 + p][:, 0:D], moe["b2bc"][:, ds(e * D, D)],
                                            ALU.add).then_inc(y_sb, 1)
                xT_copy(0, 0, 0, True)
                xT_copy(0, 1, 1, True)
                y_copy(0, 0, 0, True)
                xT_copy(1, 0, 2, False)
                y_copy(0, 1, 1, True)
                xT_copy(1, 1, 3, False)
                y_copy(1, 0, 2, False)
                with dve.Fori(2, NI) as i:
                    xT_copy(i, 0, 2 * i, False)
                    y_copy(i - 1, 1, 2 * i - 1, False)
                    xT_copy(i, 1, 2 * i + 1, False)
                    y_copy(i, 0, 2 * i, False)
                y_copy(NI - 1, 1, NBLK - 1, False)

            @block.gpsimd
            def _(pool):
                with pool.Fori(0, NI) as i:
                    for p in range(2):
                        pool.wait_ge(y_sb, 2 * i + p + 1)
                        pool.dma_start(moe["ydisp"][ds((2 * i + p) * P, P), :], yb[:, p, :]).then_inc(st[p], 16)
                for p in range(2):
                    pool.wait_ge(st[p], 16 * NI)
                for i in range(NT):
                    pool.indirect_dma_start(xn_all[:, i, :], None, moe["ydisp"],
                                            bass.IndirectOffsetOnAxis(ap=posi[:, i:i + 1], axis=0)).then_inc(gat[i // 8], 16)

            @block.vector
            def _(dve):
                for i in range(NT):
                    if i % 8 == 0:
                        dve.wait_ge(gat[i // 8], 128)
                    nc.vector.scalar_tensor_tensor(xs[:, i, :], xn_all[:, i, :], sc[:, i:i + 1], xs[:, i, :],
                                                   ALU.mult, ALU.add)


def retention(nc, ap, buf, sem):
    bank, ident = buf["bank"], buf["ident"]
    T_BANK, QK_BANK = bank[0], bank[1:3]
    VG_BANK = bank[3]
    S_BANK = bank[4:6]
    O_BANK = bank[6:8]
    S = lambda n: sem(f"r_{n}")
    ln = Norm(nc, buf, sem, "r")
    ld, init = S("ld"), S("init")
    xnT_ps, xnT_sb, qk_ps, v_ps, g_ps, v_sb, g_sb, rot, rot_step = (S(n) for n in (
        "xnT_ps", "xnT_sb", "qk_ps", "v_ps", "g_ps", "v_sb", "g_sb", "rot", "rot_step"))
    k_split, s_ps, s_sb, o_ps, sq, o_step, root, gated = (S(n) for n in (
        "k_split", "s_ps", "s_sb", "o_ps", "sq", "o_step", "root", "gated"))
    gT_ps, gT_sb, y_ps, x_added, o_scaled = (S(n) for n in ("gT_ps", "gT_sb", "y_ps", "x_added", "o_scaled"))
    with ExitStack() as c:
        def sb(name, shape, dt=F32):
            return c.enter_context(nc.sbuf_tensor("r_" + name, shape, dt))
        w4, wv, wg, wo = sb("w4", [P, 4, D]), sb("wv", [P, VD]), sb("wg", [P, VD]), sb("wo", [P, 2, D])
        tab = sb("tab", [P, 4, 256])
        mask = sb("mask", [P, RH, SC])
        par = sb("par", [P, 2])
        r1, r2 = sb("r1", [P, 2, 256]), sb("r2", [P, 2, 256])
        qr, kr, kz = sb("qr", [P, 256]), sb("kr", [P, 256]), sb("kz", [P, 2, 256])
        v33, gate = sb("v33", [P, TPB, RH, RW]), sb("gate", [P, TPB, VD])
        sT = sb("sT", [P, 4, SC])
        osq, dn, ms, fac = sb("osq", [P, TPB, RH, RHD]), sb("dn", [P, 16]), sb("ms", [P, 16]), sb("fac", [P, TPB, RH])
        on, onT = sb("on", [P, TPB, VD]), sb("onT", [P, 4 * P])
        block = c.enter_context(nc.Block())

        @block.sync
        def _(sp):
            for dst, name in ((w4, "w4"), (wv, "wv"), (wg, "wgate"), (wo, "wo"), (tab, "tab"), (mask, "mask"), (par, "par")):
                sp.dma_start(dst[:], ap[name]).then_inc(ld, 16)

        @block.gpsimd
        def _(pool):
            nc.gpsimd.memset(v33[:], 1.0).then_inc(init, 1)

            def body(b):
                ln.root(pool, b)
                pool.wait_ge(o_step, 7 * b + 7)
                nc.gpsimd.tensor_tensor(fac[:].rearrange("p t h -> p (t h)"), ms[:], buf["mhalf"][:], ALU.pow).then_inc(root, 1)
            with pool.Fori(0, NB) as b:
                body(b)

        @block.tensor
        def _(pe):
            def scores(b, h, first):
                if not (first and h < 2):
                    pe.wait_ge(s_sb, RH * b + h - 1)
                g = 32 * (h // 2)
                dst = S_BANK[h % 2]
                nc.tensor.matmul(dst[:, 0:256], kz[g:g + 32, h % 2, 0:P], qr[g:g + 32, :], start=True, stop=True)
                nc.tensor.matmul(dst[:, 256:SC], kz[g:g + 32, h % 2, P:256], qr[g:g + 32, P:256],
                                 start=True, stop=True).then_inc(s_ps, 1)

            def outputs(b, h):
                pe.wait_ge(s_sb, RH * b + h + 1)
                s = sT[:, h % 4, :]
                col = slice(h * RW, (h + 1) * RW)
                nc.tensor.matmul(O_BANK[0][:, col], s[:, 0:P], v33[:, 0, h, :], start=True, stop=True)
                nc.tensor.matmul(O_BANK[1][:, col], s[:, P:256], v33[:, 0, h, :], start=True, stop=False)
                nc.tensor.matmul(O_BANK[1][:, col], s[:, 256:SC], v33[:, 1, h, :], start=False,
                                 stop=True).then_inc(o_ps, 1)

            def body(b, first):
                pe.wait_ge(ln.done, b + 1)
                if not first:
                    pe.wait_ge(gT_sb, b)
                for t in range(TPB):
                    last = nc.tensor.transpose(T_BANK[:, t * P:(t + 1) * P], buf["xn"][:, t, :], ident[:])
                last.then_inc(xnT_ps, 1)
                pe.wait_ge(xnT_sb, b + 1)
                if not first:
                    pe.wait_ge(x_added, b)
                for j in range(4):
                    last = nc.tensor.matmul(QK_BANK[j // 2][:, (j % 2) * 256:(j % 2) * 256 + 256], w4[:, j, :],
                                            buf["xnT"][:], start=True, stop=True)
                last.then_inc(qk_ps, 1)
                for t in range(TPB):
                    last = nc.tensor.matmul(VG_BANK[:, t * VD:(t + 1) * VD], buf["xnT"][:, t * P:(t + 1) * P], wv[:],
                                            start=True, stop=True)
                last.then_inc(v_ps, 1)
                pe.wait_ge(v_sb, b + 1)
                for t in range(TPB):
                    last = nc.tensor.matmul(VG_BANK[:, t * VD:(t + 1) * VD], buf["xnT"][:, t * P:(t + 1) * P], wg[:],
                                            start=True, stop=True)
                last.then_inc(g_ps, 1)
                pe.wait_ge(k_split, 2 * b + 2)
                for h in range(RH):
                    scores(b, h, first)
                    if h >= 1:
                        outputs(b, h - 1)
                outputs(b, RH - 1)
                pe.wait_ge(gated, b + 1)
                for t in range(TPB):
                    for k in range(2):
                        last = nc.tensor.transpose(T_BANK[:, (2 * t + k) * P:(2 * t + k + 1) * P],
                                                   on[:, t, k * P:(k + 1) * P], ident[:])
                last.then_inc(gT_ps, 1)
                pe.wait_ge(gT_sb, b + 1)
                for t in range(TPB):
                    for k in range(2):
                        last = nc.tensor.matmul(VG_BANK[:, t * D:(t + 1) * D], onT[:, (2 * t + k) * P:(2 * t + k + 1) * P],
                                                wo[:, k, :], start=(k == 0), stop=(k == 1))
                last.then_inc(y_ps, 1)

            pe.wait_ge(ld, 112)
            body(0, True)
            with pe.Fori(1, NB) as b:
                body(b, False)

        @block.scalar
        def _(act):
            act.wait_ge(init, 1)
            act.wait_ge(ld, 112)
            with act.Fori(0, NB) as b:
                act.wait_ge(xnT_ps, b + 1)
                nc.scalar.copy(buf["xnT"][:], T_BANK[:, 0:256]).then_inc(xnT_sb, 1)
                act.wait_ge(v_ps, b + 1)
                nc.scalar.copy(v33[:, :, :, 0:RHD], VG_BANK[:].rearrange("p (t h c) -> p t h c", t=TPB, h=RH)).then_inc(v_sb, 1)
                act.wait_ge(g_ps, b + 1)
                nc.scalar.activation(gate[:], VG_BANK[:].rearrange("p (t c) -> p t c", t=TPB), ACT.Silu).then_inc(g_sb, 1)
                act.wait_ge(rot, 2 * b + 2)
                for q in range(2):
                    nc.scalar.activation(kz[:, q, :], kr[:], ACT.Copy, scale=par[:, q:q + 1]).then_inc(k_split, 1)
                act.wait_ge(o_ps, RH * b + RH)
                for t in range(TPB):
                    o4 = O_BANK[t][:, 0:RH * RW].rearrange("p (h c) -> p h c", c=RW)
                    nc.scalar.activation(osq[:, t], o4[:, :, 0:RHD], ACT.Square).then_inc(sq, 1)
                act.wait_ge(gT_ps, b + 1)
                nc.scalar.copy(onT[:], T_BANK[:]).then_inc(gT_sb, 1)

        @block.vector
        def _(dve):
            def xn(t):
                return buf["xn"][:, t, :]

            def rotate(b):
                dve.wait_ge(qk_ps, b + 1)
                for i in range(2):
                    nc.vector.tensor_tensor(r1[:, i, :], QK_BANK[i][:, 0:256], tab[:, 2 * i, :], ALU.mult)
                    nc.vector.tensor_tensor(r2[:, i, :], QK_BANK[i][:, 256:512], tab[:, 2 * i + 1, :], ALU.mult).then_inc(rot_step, 1)
                dve.wait_ge(rot_step, 2 * b + 2)
                nc.vector.tensor_tensor(qr[:], r1[:, 0, :], r2[:, 0, :], ALU.add).then_inc(rot, 1)
                nc.vector.tensor_tensor(kr[:], r1[:, 1, :], r2[:, 1, :], ALU.add).then_inc(rot, 1)

            dve.wait_ge(ld, 112)
            with dve.Fori(0, NB) as b:
                ln.stats(dve, b)
                ln.scale(dve, b, xn)
                rotate(b)
                for h in range(RH):
                    dve.wait_ge(s_ps, RH * b + h + 1)
                    nc.vector.tensor_tensor(sT[:, h % 4, :], S_BANK[h % 2][:, 0:SC], mask[:, h, :], ALU.mult).then_inc(s_sb, 1)
                dve.wait_ge(sq, 2 * b + 2)
                for t in range(TPB):
                    o4 = O_BANK[t][:, 0:RH * RW].rearrange("p (h c) -> p h c", c=RW)
                    nc.vector.tensor_scalar(dn[:, t * RH:(t + 1) * RH], o4[:, :, RHD], 1.0, None, ALU.max).then_inc(o_step, 1)
                dve.wait_ge(o_step, 7 * b + 2)
                for t in range(TPB):
                    o4 = O_BANK[t][:, 0:RH * RW].rearrange("p (h c) -> p h c", c=RW)
                    last = nc.vector.scalar_tensor_tensor(dn[:, t * RH:(t + 1) * RH], o4[:, :, RHD], -1.0,
                                                          dn[:, t * RH:(t + 1) * RH], ALU.mult, ALU.max)
                last.then_inc(o_step, 1)
                nc.vector.reduce_sum(ms[:], osq[:].rearrange("p t h c -> p (t h) c"), AX).then_inc(o_step, 1)
                dve.wait_ge(o_step, 7 * b + 4)
                nc.vector.scalar_tensor_tensor(dn[:], dn[:], EPS, dn[:], ALU.mult, ALU.mult).then_inc(o_step, 1)
                nc.vector.tensor_scalar(ms[:], ms[:], 1.0 / RHD, None, ALU.mult).then_inc(o_step, 1)
                dve.wait_ge(o_step, 7 * b + 6)
                nc.vector.tensor_tensor(ms[:], ms[:], dn[:], ALU.add).then_inc(o_step, 1)
                dve.wait_ge(root, b + 1)
                dve.wait_ge(g_sb, b + 1)
                for t in range(TPB):
                    o4 = O_BANK[t][:, 0:RH * RW].rearrange("p (h c) -> p h c", c=RW)
                    nc.vector.tensor_tensor(osq[:, t], o4[:, :, 0:RHD], fac[:, t, :, None].to_broadcast([P, RH, RHD]),
                                            ALU.mult).then_inc(o_scaled, 1)
                dve.wait_ge(o_scaled, 2 * b + 2)
                nc.vector.tensor_tensor(on[:], osq[:].rearrange("p t h c -> p t (h c)"), gate[:], ALU.mult).then_inc(gated, 1)
                dve.wait_ge(y_ps, b + 1)
                nc.vector.tensor_tensor(buf["xs"][:, ds(2 * b, 2), :], VG_BANK[:, 0:256].rearrange("p (t c) -> p t c", t=TPB),
                                        buf["xs"][:, ds(2 * b, 2), :], ALU.add).then_inc(x_added, 1)


def tables():
    f = np.float32
    S = TPB * P
    angle = np.repeat(f(1.0) / f(10000.0) ** np.linspace(0.0, 1.0, KD // 2, dtype=f), 2).astype(f)
    idx = np.arange(S, dtype=f)
    arg = (idx[None, :] * angle[:, None]).astype(f)
    cos, sin = np.cos(arg).astype(f), np.sin(arg).astype(f)
    sign = np.where(np.arange(KD) % 2 == 0, -1.0, 1.0).astype(f)[:, None]
    c, s = np.tile(cos, (RH, 1)), np.tile(sin * sign, (RH, 1))
    scale = f(KD ** -0.5)
    tab = np.stack([c, s, c * scale, s * scale], 1).astype(f)
    decay = np.log1p(-2.0 ** (-5.0 - np.arange(RH))).astype(f)
    diff = idx[:, None] - idx[None, :]
    m = np.where(diff[None] >= 0, np.exp(diff[None] * decay[:, None, None]), 0.0).astype(f)
    m = (m / np.sqrt(m.sum(-1, keepdims=True, dtype=f))).astype(f)
    mt = m.transpose(2, 0, 1)
    mask = np.concatenate([mt[0:P], mt[P:S, :, P:S]], 2)
    par = np.zeros((P, 2), f)
    for h in range(RH):
        par[h * KD:(h + 1) * KD, h % 2] = 1
    return dict(
        tab=tab, mask=mask, par=par, ident=np.eye(P, dtype=f), before=np.triu(np.ones((P, P), f), 1),
        prio=(E - np.arange(E, dtype=f))[None], start=(P * np.arange(NBLK, dtype=f))[None],
    )


def kernel(L0_attn_a_x, L0_attn_a_W_qkv, L0_attn_a_proj, L0_attn_a_W_out, L0_attn_a_b_out, L0_attn_b_wq, L0_attn_b_wk,
           L0_attn_b_wv, L0_attn_b_wg, L0_attn_b_wo, L0_ffn_wg_red, L0_ffn_wg, L0_ffn_w1, L0_ffn_b1, L0_ffn_w2, L0_ffn_b2):
    import concourse.bacc as bacc
    from concourse.bass_utils import run_bass_kernel_spmd

    A = lambda a: np.asarray(a)
    swap = np.arange(D) ^ 1
    wq, wk = A(L0_attn_b_wq), A(L0_attn_b_wk)
    arrays = dict(
        x=A(L0_attn_a_x).reshape(NT, P, D).transpose(1, 0, 2),
        wqkvT=A(L0_attn_a_W_qkv).T, proj=A(L0_attn_a_proj), woutT=A(L0_attn_a_W_out).T, b_out=A(L0_attn_a_b_out)[None],
        w4=np.stack([wq, wq[:, swap], wk, wk[:, swap]], 1), wv=A(L0_attn_b_wv), wgate=A(L0_attn_b_wg),
        wo=A(L0_attn_b_wo).reshape(2, P, D).transpose(1, 0, 2),
        wg_red=A(L0_ffn_wg_red), wg=A(L0_ffn_wg), w1=A(L0_ffn_w1).transpose(1, 0, 2),
        b1=A(L0_ffn_b1).reshape(E, HC, P).transpose(2, 0, 1),
        w2=A(L0_ffn_w2).reshape(E * HC, P, D).transpose(1, 0, 2), b2=A(L0_ffn_b2).reshape(1, E * D),
        **tables(),
    )
    arrays = {k: np.ascontiguousarray(v) for k, v in arrays.items()}
    nc = bacc.Bacc("TRN2", target_bir_lowering=False, num_devices=1)
    ap = {k: nc.dram_tensor("in_" + k, v.shape, F32, kind="ExternalInput").ap() for k, v in arrays.items()}
    out = nc.dram_tensor("out", (P, NT, D), F32, kind="ExternalOutput").ap()
    build(nc, ap, out)
    r = run_bass_kernel_spmd(nc, [{"in_" + k: v for k, v in arrays.items()}], core_ids=[0])
    return r.results[0]["out"].transpose(1, 0, 2).reshape(NB, TPB * P, D)
```

```python
from contextlib import ExitStack, contextmanager

import numpy as np

import concourse.bass as bass
from concourse import mybir

F32 = mybir.dt.float32
BF16 = mybir.dt.bfloat16
I32 = mybir.dt.int32
ALU = mybir.AluOpType
ACT = mybir.ActivationFunctionType
AX = mybir.AxisListType.X
ds = bass.ds

P = 128
NB = 32
TPB = 2
NT = NB * TPB
D = 128
EPS = 1e-5
H, HD, F = 16, 8, 128
KVW = HD + 1
U = 16
E, HID, GD = 8, 512, 16
HC = HID // P
NBLK = NT + E
W1W = HID + HC
RH, KD, VD = 8, 16, 256
RHD = VD // RH
RW = RHD + 1
PART_A, PART_B = (0, 0, 1, 1, 0, 2), (0, 1, 0, 1, 2, 0)
NTERM = len(PART_A)
SC = 3 * P


@contextmanager
def phase(nc, name):
    with ExitStack() as c:
        taken = []

        def sem(n):
            taken.append(c.enter_context(nc.semaphore(n)))
            return taken[-1]

        yield sem
        with nc.Block(f"{name}_clear") as block:
            @block.vector
            def _(dve):
                for one in taken:
                    dve.sem_clear(one)


def build(nc, ap, out):
    ctx = ExitStack()

    def sb(name, shape, dt=F32):
        return ctx.enter_context(nc.sbuf_tensor(name, shape, dt))

    def sem(name):
        return ctx.enter_context(nc.semaphore(name))

    with ctx:
        bank = [ctx.enter_context(nc.psum_tensor(f"bank{i}", [P, 512], F32)) for i in range(8)]
        xs = sb("xs", [P, NT, D])
        xn_all = sb("xn_all", [P, NT, D])
        ident = sb("ident", [P, P])
        buf = dict(
            bank=bank, xs=xs, xn_all=xn_all, ident=ident,
            xn=sb("xn", [P, TPB, D]), xnT=sb("xnT", [P, TPB * P]),
            stats=sb("stats", [P, TPB, 6]), both=sb("both", [P, TPB, 2]),
            diff=sb("diff", [P, TPB]), sq=sb("sq", [P, TPB]), mean=sb("mean", [P, TPB]), quarter=sb("quarter", [P, TPB]),
            var=sb("var", [P, TPB]), rstd=sb("rstd", [P, TPB]), mhalf=sb("mhalf", [P, 16]),
        )
        xdisp = nc.dram_tensor("xdisp", (NBLK * P, D), F32).ap()
        ydisp = nc.dram_tensor("ydisp", (NBLK * P, D), F32).ap()
        ldx = [sem(f"ld_x{i}") for i in range(8)]

        moe = dict(
            w1b=sb("w1b", [P, E, W1W]), w2s=sb("w2s", [P, E * HC, D]), b2bc=sb("b2bc", [P, E * D]),
            G=sb("G", [P, E]), U128=sb("U128", [P, P]), ones=sb("ones", [P, P]), xdisp=xdisp, ydisp=ydisp,
        )
        setup(nc, ap, buf, moe, ldx, sem, sb)
        with phase(nc, "attention") as psem:
            linear_attention(nc, ap, buf, ldx, psem)
        with phase(nc, "experts_0") as psem:
            expert_layer(nc, ap, buf, moe, psem, "f0")
        with phase(nc, "retention") as psem:
            retention(nc, ap, buf, psem)
        with phase(nc, "experts_1") as psem:
            expert_layer(nc, ap, buf, moe, psem, "f1")

        st = sem("store_x")
        block = ctx.enter_context(nc.Block())

        @block.sync
        def _(sp):
            sp.dma_start(out, xs[:, :, :]).then_inc(st, 16)
            sp.wait_ge(st, 16)


def setup(nc, ap, buf, moe, ldx, sem, sb):
    ld_c, ld_w, gate_step, zero_step = sem("ld_const"), sem("ld_moe"), sem("gate_step"), sem("zero_step")
    ld_z = sem("ld_zero")
    pe_g, dve_g = sem("gate_pe"), sem("gate_dve")
    bank = buf["bank"]
    with (
        nc.sbuf_tensor("wgr", [GD, D], F32) as wgr,
        nc.sbuf_tensor("wge", [E, GD], F32) as wge,
        nc.sbuf_tensor("wsq", [E, GD], F32) as wsq,
        nc.sbuf_tensor("wn", [E, 4], F32) as wn,
        nc.sbuf_tensor("wgT", [GD, E], F32) as wgT,
        nc.sbuf_tensor("zrow", [P, 8 * D], F32) as zrow,
        nc.Block() as block,
    ):
        @block.sync
        def _(sp):
            for i in range(8):
                sp.dma_start(buf["xs"][:, 8 * i:8 * i + 8, :], ap["x"][:, 8 * i:8 * i + 8, :]).then_inc(ldx[i], 16)

        @block.scalar
        def _(act):
            act.dma_start(buf["ident"][:], ap["ident"]).then_inc(ld_c, 16)
            act.dma_start(wgr[:], ap["wg_red"]).then_inc(ld_c, 16)
            act.dma_start(wge[:], ap["wg"]).then_inc(ld_c, 16)
            act.dma_start(moe["U128"][:], ap["before"]).then_inc(ld_c, 16)
            act.dma_start(moe["w1b"][:, :, 0:HID], ap["w1"]).then_inc(ld_w, 16)
            act.dma_start(moe["w1b"][:, :, HID:W1W], ap["b1"]).then_inc(ld_w, 16)
            act.dma_start(moe["w2s"][:], ap["w2"]).then_inc(ld_w, 16)
            act.dma_start(moe["b2bc"][:], ap["b2"].to_broadcast([P, E * D])).then_inc(ld_w, 16)
            act.wait_ge(zero_step, 1)
            for i in range(NBLK // 8):
                act.dma_start(moe["xdisp"][i * 1024:(i + 1) * 1024, :].rearrange("(p r) d -> p (r d)", p=P),
                              zrow[:]).then_inc(ld_z, 16)
            act.wait_ge(ld_z, 16 * (NBLK // 8))
            act.wait_ge(ld_w, 64)

        @block.gpsimd
        def _(pool):
            nc.gpsimd.memset(zrow[:], 0.0).then_inc(zero_step, 1)
            nc.gpsimd.memset(buf["mhalf"][:], -0.5)
            nc.gpsimd.memset(buf["quarter"][:], 0.25)

        @block.vector
        def _(dve):
            nc.vector.memset(moe["ones"][:], 1.0)
            dve.wait_ge(ld_c, 64)
            nc.vector.tensor_tensor(wsq[:], wge[:], wge[:], ALU.mult).then_inc(dve_g, 1)
            dve.wait_ge(dve_g, 1)
            nc.vector.reduce_sum(wn[:, 0:1], wsq[:], AX).then_inc(dve_g, 1)
            dve.wait_ge(gate_step, 1)
            nc.vector.tensor_scalar_max(wn[:, 2:3], wn[:, 1:2], 1e-4).then_inc(dve_g, 1)
            dve.wait_ge(dve_g, 3)
            nc.vector.reciprocal(wn[:, 3:4], wn[:, 2:3]).then_inc(dve_g, 1)
            dve.wait_ge(dve_g, 4)
            nc.vector.tensor_scalar(wsq[:], wge[:], wn[:, 3:4], None, ALU.mult).then_inc(dve_g, 1)
            dve.wait_ge(pe_g, 1)
            nc.vector.tensor_copy(wgT[:], bank[0][0:GD, 0:E]).then_inc(dve_g, 1)
            dve.wait_ge(pe_g, 2)
            nc.vector.tensor_copy(moe["G"][:], bank[1][:, 0:E])

        @block.scalar
        def _(act):
            act.wait_ge(dve_g, 2)
            nc.scalar.activation(wn[:, 1:2], wn[:, 0:1], ACT.Sqrt).then_inc(gate_step, 1)

        @block.tensor
        def _(pe):
            pe.wait_ge(dve_g, 5)
            nc.tensor.transpose(bank[0][0:GD, 0:E], wsq[:], buf["ident"][0:E, 0:E]).then_inc(pe_g, 1)
            pe.wait_ge(dve_g, 6)
            nc.tensor.matmul(bank[1][:, 0:E], wgr[:], wgT[:], start=True, stop=True).then_inc(pe_g, 1)


class Norm:

    def __init__(self, nc, buf, sem, tag):
        self.nc, self.buf = nc, buf
        self.stat, self.power, self.done = sem(f"{tag}_ln_stat"), sem(f"{tag}_ln_power"), sem(f"{tag}_ln_done")

    def stats(self, dve, b):
        nc, buf = self.nc, self.buf
        for t in range(TPB):
            nc.vector.bn_stats(buf["stats"][:, t, :], buf["xs"][:, 2 * b + t, :]).then_inc(self.stat, 1)
        st = buf["stats"][:].rearrange("p t (o c) -> p t o c", o=2)
        dve.wait_ge(self.stat, 4 * b + 2)
        nc.vector.tensor_tensor(buf["both"][:], st[:, :, 0, 1:3], st[:, :, 1, 1:3], ALU.add).then_inc(self.stat, 1)
        nc.vector.tensor_tensor(buf["diff"][:], st[:, :, 0, 1], st[:, :, 1, 1], ALU.subtract).then_inc(self.stat, 1)

    def root(self, pool, b):
        nc, buf = self.nc, self.buf
        pool.wait_ge(self.stat, 4 * b + 4)
        nc.gpsimd.tensor_tensor(buf["sq"][:], buf["diff"][:], buf["diff"][:], ALU.mult).then_inc(self.power, 1)
        nc.gpsimd.tensor_scalar(buf["mean"][:], buf["both"][:, :, 0], 0.5, 0.0, ALU.mult, ALU.add).then_inc(self.power, 1)
        nc.gpsimd.tensor_scalar(buf["var"][:], buf["both"][:, :, 1], 1.0 / D, EPS, ALU.mult, ALU.add).then_inc(self.power, 1)
        pool.wait_ge(self.power, 6 * b + 1)
        nc.gpsimd.tensor_tensor(buf["sq"][:], buf["sq"][:], buf["quarter"][:], ALU.mult).then_inc(self.power, 1)
        pool.wait_ge(self.power, 6 * b + 4)
        nc.gpsimd.tensor_tensor(buf["var"][:], buf["var"][:], buf["sq"][:], ALU.add).then_inc(self.power, 1)
        pool.wait_ge(self.power, 6 * b + 5)
        nc.gpsimd.tensor_tensor(buf["rstd"][:], buf["var"][:], buf["mhalf"][:, 0:TPB], ALU.pow).then_inc(self.power, 1)

    def scale(self, dve, b, dst):
        nc, buf = self.nc, self.buf
        dve.wait_ge(self.power, 6 * b + 6)
        for t in range(TPB):
            last = nc.vector.tensor_scalar(dst(t), buf["xs"][:, 2 * b + t, :], buf["mean"][:, t:t + 1],
                                           buf["rstd"][:, t:t + 1], ALU.subtract, ALU.mult)
        last.then_inc(self.done, 1)


def linear_attention(nc, ap, buf, ldx, sem):
    bank, ident = buf["bank"], buf["ident"]
    biased, neg_act, neg_dve = sem("a_biased"), sem("a_neg_act"), sem("a_neg_dve")
    T_BANK, QK_BANK, VY_BANK, KV_BANK = bank[4], bank[5], bank[6], bank[7]
    kv_ps = KV_BANK[:, 0:H * KVW]
    at_ps = KV_BANK[:, H * KVW:3 * H * KVW].rearrange("p (t h c) -> p t h c", t=TPB, h=H)
    v_ps = VY_BANK[:, 0:TPB * D].rearrange("p (t h c) -> p t h c", t=TPB, h=H)
    y_ps = VY_BANK[:, 256:512].rearrange("p (t c) -> p t c", t=TPB)
    ld, setup_done, ld_p = sem("a_ld"), sem("a_setup"), sem("a_ld_proj")
    proj_zero = sem("a_proj_zero")
    ln = Norm(nc, buf, sem, "a")
    xnT_ps, xnT_sb, qkv_ps, kT_sb, qT_sb, v_sb = (sem("a_" + n) for n in
                                                  ("xnT_ps", "xnT_sb", "qkv_ps", "kT_sb", "qT_sb", "v_sb"))
    feat, expd, phi = sem("a_feature"), sem("a_exp"), sem("a_phi")
    kv_done, kv_sb_done, at_done, an_step, an_done = (sem("a_" + n) for n in
                                                      ("kv_done", "kv_sb", "at_done", "an_step", "an_done"))
    anT_ps, anT_sb_done, y_done, x_added = (sem("a_" + n) for n in ("anT_ps", "anT_sb", "y_ps", "x_added"))
    with ExitStack() as c:
        def sb(name, shape, dt=F32):
            return c.enter_context(nc.sbuf_tensor(name, shape, dt))
        wqkv, wout, bout = sb("wqkv", [P, 3 * D]), sb("wout", [P, D]), sb("bout", [P, D])
        proj = sb("proj", [P, H * F])
        kT, qT = sb("kT", [P, 256]), sb("qT", [P, 256])
        v9 = sb("v9", [P, TPB, H, KVW])
        neg, ex = sb("neg", [P, 4, 512]), sb("ex", [P, 4, 512])
        kphi, qphi = sb("kphi", [P, 8, 512]), sb("qphi", [P, 4, 512])
        kv = sb("kv", [P, H * KVW])
        den, rec = sb("den", [P, TPB, H]), sb("rec", [P, TPB, H])
        an, anT = sb("an", [P, TPB, D]), sb("anT", [P, TPB * P])
        block = c.enter_context(nc.Block())

        @block.sync
        def _(sp):
            sp.dma_start(wqkv[:], ap["wqkvT"]).then_inc(ld, 16)
            sp.dma_start(wout[:], ap["woutT"]).then_inc(ld, 16)
            sp.dma_start(bout[:], ap["b_out"].to_broadcast([P, D])).then_inc(ld, 16)
            sp.wait_ge(proj_zero, 1)
            for h in range(H):
                sp.dma_start(proj[HD * h:HD * h + HD, h * F:(h + 1) * F], ap["proj"][h]).then_inc(ld_p, 16)

        @block.gpsimd
        def _(pool):
            nc.gpsimd.memset(proj[:], 0.0).then_inc(proj_zero, 1)
            nc.gpsimd.memset(v9[:], 1.0).then_inc(setup_done, 1)
            with pool.Fori(0, NB) as b:
                ln.root(pool, b)

        def xn_transposes(pe, b):
            pe.wait_ge(ln.done, b + 1)
            for t in range(TPB):
                last = nc.tensor.transpose(T_BANK[:, t * P:(t + 1) * P], buf["xn"][:, t, :], ident[:])
            last.then_inc(xnT_ps, 1)

        def qkv(pe, b):
            pe.wait_ge(xnT_sb, b + 1)
            for j in range(2):
                nc.tensor.matmul(QK_BANK[:, j * 256:(j + 1) * 256], wqkv[:, j * D:(j + 1) * D], buf["xnT"][:],
                                 start=True, stop=True)
            for t in range(TPB):
                last = nc.tensor.matmul(VY_BANK[:, t * D:(t + 1) * D], buf["xnT"][:, t * P:(t + 1) * P],
                                        wqkv[:, 2 * D:3 * D], start=True, stop=True)
            last.then_inc(qkv_ps, 1)

        @block.tensor
        def _(pe):
            def feature(b, s, first):
                if s == 0:
                    pe.wait_ge(kT_sb, b + 1)
                if s == 8:
                    pe.wait_ge(qT_sb, b + 1)
                if not (first and s < 4):
                    pe.wait_ge(phi, U * b + s - 3)
                dst = bank[s % 4]
                if s < 8:
                    g, t = s // 2, s % 2
                    nc.tensor.matmul(dst[:], kT[:, t * P:(t + 1) * P], proj[:, g * 512:(g + 1) * 512],
                                     start=True, stop=True).then_inc(feat, 1)
                else:
                    for j in range(2):
                        h = 2 * (s - 8) + j
                        last = nc.tensor.matmul(dst[:, j * 256:(j + 1) * 256], proj[:, h * F:(h + 1) * F], qT[:],
                                                start=True, stop=True)
                    last.then_inc(feat, 1)

            def key_value(b, g, first):
                pe.wait_ge(phi, U * b + 2 * g + 2)
                if g == 0:
                    pe.wait_ge(v_sb, b + 1)
                    if not first:
                        pe.wait_ge(an_done, b)
                for j in range(4):
                    h = 4 * g + j
                    for t in range(TPB):
                        last = nc.tensor.matmul(kv_ps[:, h * KVW:(h + 1) * KVW],
                                                kphi[:, 2 * g + t, j * F:(j + 1) * F], v9[:, t, h, :],
                                                start=(t == 0), stop=(t == 1))
                last.then_inc(kv_done, 1)

            def attend(b, w):
                pe.wait_ge(phi, U * b + 8 + w + 1)
                if w == 0:
                    pe.wait_ge(kv_sb_done, b + 1)
                for j in range(2):
                    h = 2 * w + j
                    for t in range(TPB):
                        last = nc.tensor.matmul(at_ps[:, t, h, :], qphi[:, w % 4, j * 256 + t * P:j * 256 + (t + 1) * P],
                                                kv[:, h * KVW:(h + 1) * KVW], start=True, stop=True)
                last.then_inc(at_done, 1)

            def an_transposes(b, last_batch):
                pe.wait_ge(an_done, b + 1)
                pe.wait_ge(qT_sb, b + (1 if last_batch else 2))
                for t in range(TPB):
                    last = nc.tensor.transpose(QK_BANK[:, t * P:(t + 1) * P], an[:, t, :], ident[:])
                last.then_inc(anT_ps, 1)

            def project(b, last_batch):
                pe.wait_ge(anT_sb_done, b + 1)
                pe.wait_ge(v_sb, b + (1 if last_batch else 2))
                for t in range(TPB):
                    last = nc.tensor.matmul(y_ps[:, t, :], anT[:, t * P:(t + 1) * P], wout[:], start=True, stop=True)
                last.then_inc(y_done, 1)

            def body(b, first=False, last=False):
                for s in range(U):
                    feature(b, s, first)
                    if s < 4 and not first:
                        attend(b - 1, 4 + s)
                    if s in (5, 7, 9, 11):
                        key_value(b, (s - 5) // 2, first)
                    if s == 6 and not first:
                        an_transposes(b - 1, False)
                    if s == 6 and not last:
                        xn_transposes(pe, b + 1)
                    if s == 8 and not first:
                        project(b - 1, False)
                    if s == 10 and not last:
                        if not first:
                            pe.wait_ge(x_added, b)
                            pe.wait_ge(anT_sb_done, b)
                        qkv(pe, b + 1)
                    if s >= 12:
                        attend(b, s - 12)

            pe.wait_ge(ld, 48)
            pe.wait_ge(ld_p, 16 * H)
            pe.wait_ge(setup_done, 1)
            xn_transposes(pe, 0)
            qkv(pe, 0)
            body(0, first=True)
            with pe.Fori(1, NB - 1) as b:
                body(b)
            body(NB - 1, last=True)
            for w in (4, 5, 6, 7):
                attend(NB - 1, w)
            an_transposes(NB - 1, True)
            project(NB - 1, True)

        @block.scalar
        def _(act):
            def copy_xnT(b):
                act.wait_ge(xnT_ps, b + 1)
                nc.scalar.copy(buf["xnT"][:], T_BANK[:, 0:256]).then_inc(xnT_sb, 1)

            def copy_k(b):
                act.wait_ge(qkv_ps, b + 1)
                nc.scalar.copy(kT[:], QK_BANK[:, 256:512]).then_inc(kT_sb, 1)

            def copy_q(b):
                nc.scalar.copy(qT[:], QK_BANK[:, 0:256]).then_inc(qT_sb, 1)

            def copy_v(b, first):
                if not first:
                    act.wait_ge(kv_done, 4 * b)
                nc.scalar.copy(v9[:, :, :, 0:HD], v_ps).then_inc(v_sb, 1)

            def copy_anT(b):
                act.wait_ge(anT_ps, b + 1)
                nc.scalar.copy(anT[:], QK_BANK[:, 0:256]).then_inc(anT_sb_done, 1)

            def negative(b, s):
                act.wait_ge(feat, U * b + s + 1)
                nc.scalar.activation(neg[:, s % 4, :], bank[s % 4][:], ACT.Relu, scale=-1.0).then_inc(neg_act, 1)

            def exponential(b, s):
                if s % 2 == 0:
                    act.wait_ge(neg_act, U // 2 * b + s // 2 + 1)
                else:
                    act.wait_ge(neg_dve, U // 2 * b + s // 2 + 1)
                nc.scalar.activation(ex[:, s % 4, :], neg[:, s % 4, :], ACT.Exp,
                                     scale=-1.0 if s % 2 == 0 else 1.0).then_inc(expd, 1)

            def body(b, first=False, last=False):
                for s in range(U):
                    if s % 2 == 0:
                        negative(b, s)
                    if s > 0:
                        exponential(b, s - 1)
                    elif not first:
                        exponential(b - 1, U - 1)
                    if s == 2:
                        copy_q(b)
                    if s == 7 and not first:
                        copy_anT(b - 1)
                    if s == 7 and not last:
                        copy_xnT(b + 1)
                    if s == 11 and not last:
                        copy_k(b + 1)
                    if s == 12 and not last:
                        copy_v(b + 1, False)

            act.wait_ge(setup_done, 1)
            copy_xnT(0)
            copy_k(0)
            copy_v(0, True)
            body(0, first=True)
            with act.Fori(1, NB - 1) as b:
                body(b)
            body(NB - 1, last=True)
            exponential(NB - 1, U - 1)
            copy_anT(NB - 1)

        @block.vector
        def _(dve):
            def xn(t):
                return buf["xn"][:, t, :]

            def normalise(b):
                dve.wait_ge(at_done, 8 * (b + 1))
                nc.vector.tensor_scalar(den[:], at_ps[:, :, :, HD], 1e-8, None, ALU.add).then_inc(an_step, 1)
                dve.wait_ge(an_step, 2 * b + 1)
                nc.vector.reciprocal(rec[:], den[:]).then_inc(an_step, 1)
                dve.wait_ge(an_step, 2 * b + 2)
                for t in range(TPB):
                    last = nc.vector.tensor_tensor(an[:, t, :].rearrange("p (h c) -> p h c", h=H), at_ps[:, t, :, 0:HD],
                                                   rec[:, t, :, None].to_broadcast([P, H, HD]), ALU.mult)
                last.then_inc(an_done, 1)

            def add_bias(b):
                nc.vector.tensor_tensor(buf["xs"][:, ds(2 * b, 2), :], buf["xs"][:, ds(2 * b, 2), :],
                                        bout[:, None, :].to_broadcast([P, TPB, D]), ALU.add).then_inc(biased, 1)

            def add_y(b):
                dve.wait_ge(y_done, b + 1)
                dve.wait_ge(biased, b + 1)
                nc.vector.tensor_tensor(buf["xs"][:, ds(2 * b, 2), :], y_ps, buf["xs"][:, ds(2 * b, 2), :],
                                        ALU.add).then_inc(x_added, 1)

            def negative(b, s):
                dve.wait_ge(feat, U * b + s + 1)
                nc.vector.tensor_scalar_min(neg[:, s % 4, :], bank[s % 4][:], 0.0).then_inc(neg_dve, 1)

            def features(b, s, first):
                dve.wait_ge(expd, U * b + s + 1)
                if s < 8:
                    if not first:
                        dve.wait_ge(kv_done, 4 * b - 4 + s // 2 + 1)
                    dst = kphi[:, s, :]
                else:
                    w = s - 8
                    if w >= 4:
                        dve.wait_ge(at_done, 8 * b + w - 3)
                    elif not first:
                        dve.wait_ge(at_done, 8 * b - 8 + w + 5)
                    dst = qphi[:, w % 4, :]
                nc.vector.scalar_tensor_tensor(dst, bank[s % 4][:], 0.0, ex[:, s % 4, :], ALU.max,
                                               ALU.add).then_inc(phi, 1)

            def body(b, first=False, last=False):
                for s in range(U):
                    if s % 2:
                        negative(b, s)
                    if s >= 2:
                        features(b, s - 2, first)
                    elif not first:
                        features(b - 1, U - 2 + s, False)
                    if s == 2 and not last:
                        ln.stats(dve, b + 1)
                    if s == 4 and not first:
                        normalise(b - 1)
                    if s == 4 and not last:
                        dve.wait_ge(xnT_ps, b + 1)
                        ln.scale(dve, b + 1, xn)
                    if s == 5:
                        add_bias(b)
                    if s == 9 and not first:
                        add_y(b - 1)
                    if s == 12:
                        dve.wait_ge(kv_done, 4 * b + 4)
                        nc.vector.tensor_copy(kv[:], kv_ps).then_inc(kv_sb_done, 1)

            dve.wait_ge(setup_done, 1)
            dve.wait_ge(ld, 48)
            for i in range(8):
                dve.wait_ge(ldx[i], 16)
            ln.stats(dve, 0)
            ln.scale(dve, 0, xn)
            body(0, first=True)
            with dve.Fori(1, NB - 1) as b:
                body(b)
            body(NB - 1, last=True)
            features(NB - 1, U - 2, False)
            features(NB - 1, U - 1, False)
            normalise(NB - 1)
            add_y(NB - 1)


def expert_layer(nc, ap, buf, moe, sem, tag):
    bank, ident, xs, xn_all = buf["bank"], buf["ident"], buf["xs"], buf["xn_all"]
    S = lambda n: sem(f"{tag}_{n}")
    ln = Norm(nc, buf, sem, tag)
    xnT_ps, xnT_sb, lg_ps, lg_sb = S("xnT_ps"), S("xnT_sb"), S("logit_ps"), S("logit_sb")
    step, expd, rank_ps, routed = S("step"), S("exp"), S("rank_ps"), S("routed")
    scat, wl, xl, st, gat = S("scatter"), [S(f"ld_w{p}") for p in range(4)], [S(f"ld_x{p}") for p in range(4)], [S(f"st_y{p}") for p in range(4)], [S(f"gather{i}") for i in range(8)]
    xT_ps, xT_sb, h_ps, h_sb, y_ps_done, y_sb = (S(n) for n in ("xT_ps", "xT_sb", "h_ps", "h_sb", "y_ps", "y_sb"))
    pld, onehot, shifted = S("ld_pos"), S("onehot"), S("shifted")
    with ExitStack() as c:
        def sb(name, shape, dt=F32):
            return c.enter_context(nc.sbuf_tensor(f"{tag}_{name}", shape, dt))
        lg, oh, t1, t2, t3 = (sb(n, [P, NT, E]) for n in ("lg", "oh", "t1", "t2", "t3"))
        m, sc = sb("m", [P, NT]), sb("sc", [P, NT])
        pos, posi = sb("pos", [P, NT]), sb("posi", [P, NT], I32)
        tot, off, nbi = sb("tot", [P, E]), sb("off", [P, E + 1]), sb("nbi", [P, E], I32)
        cnt, eb, cmp8 = sb("cnt", [P, NBLK]), sb("eb", [P, NBLK], I32), sb("cmp8", [P, NBLK, E])
        prio, start = sb("prio", [P, E]), sb("start", [P, NBLK])
        wc = sb("wc", [P, 4, W1W])
        xb, xT, hT, yb = sb("xb", [P, 4, D]), sb("xT", [P, 4, P]), sb("hT", [P, 4, HC * P]), sb("yb", [P, 4, D])

        with nc.Block() as block:
            @block.sync
            def _(sp):
                sp.dma_start(prio[:], ap["prio"].to_broadcast([P, E])).then_inc(pld, 16)
                sp.dma_start(start[:], ap["start"].to_broadcast([P, NBLK])).then_inc(pld, 16)

            @block.gpsimd
            def _(pool):
                with pool.Fori(0, NB) as b:
                    ln.root(pool, b)
                pool.wait_ge(routed, 1)
                for i in range(NT):
                    pool.indirect_dma_start(moe["xdisp"], bass.IndirectOffsetOnAxis(ap=posi[:, i:i + 1], axis=0),
                                            xn_all[:, i, :], None).then_inc(scat, 16)
                pool.wait_ge(scat, 16 * NT)

            @block.tensor
            def _(pe):
                def body(b, first):
                    pe.wait_ge(ln.done, b + 1)
                    if not first:
                        pe.wait_ge(xnT_sb, b)
                    for t in range(TPB):
                        last = nc.tensor.transpose(bank[0][:, t * P:(t + 1) * P], buf["xn"][:, t, :], ident[:])
                    last.then_inc(xnT_ps, 1)
                    pe.wait_ge(xnT_sb, b + 1)
                    if not first:
                        pe.wait_ge(lg_sb, b)
                    for t in range(TPB):
                        last = nc.tensor.matmul(bank[1][:, t * E:(t + 1) * E], buf["xnT"][:, t * P:(t + 1) * P],
                                                moe["G"][:], start=True, stop=True)
                    last.then_inc(lg_ps, 1)
                body(0, True)
                with pe.Fori(1, NB) as b:
                    body(b, False)
                pe.wait_ge(onehot, 1)
                ohf = oh[:].rearrange("p t e -> p (t e)")
                nc.tensor.matmul(bank[2][:], moe["U128"][:], ohf, start=True, stop=True)
                nc.tensor.matmul(bank[3][:], moe["ones"][:], ohf, start=True, stop=True).then_inc(rank_ps, 1)

            @block.scalar
            def _(act):
                def body(b, first):
                    if not first:
                        act.wait_ge(lg_ps, b)
                    act.wait_ge(xnT_ps, b + 1)
                    nc.scalar.copy(buf["xnT"][:], bank[0][:, 0:256]).then_inc(xnT_sb, 1)
                body(0, True)
                with act.Fori(1, NB) as b:
                    body(b, False)
                act.wait_ge(shifted, 2)
                nc.scalar.activation(t1[:], t1[:], ACT.Exp).then_inc(expd, 1)

            @block.vector
            def _(dve):
                def xn(t):
                    return buf["xn"][:, t, :]

                def body(b, first):
                    ln.stats(dve, b)
                    if not first:
                        dve.wait_ge(xnT_ps, b)
                    ln.scale(dve, b, xn)
                    dve.wait_ge(ln.done, b + 1)
                    nc.vector.tensor_copy(xn_all[:, ds(2 * b, 2), :], buf["xn"][:])
                    dve.wait_ge(lg_ps, b + 1)
                    nc.vector.tensor_copy(lg[:, ds(2 * b, 2), :], bank[1][:, 0:TPB * E].rearrange(
                        "p (t e) -> p t e", t=TPB)).then_inc(lg_sb, 1)
                body(0, True)
                with dve.Fori(1, NB) as b:
                    body(b, False)

                n = [0]

                def then(ins):
                    n[0] += 1
                    ins.then_inc(step, 1)
                    dve.wait_ge(step, n[0])

                def over_e(a):
                    return a[:, :, None].to_broadcast([P, NT, E])

                dve.wait_ge(lg_sb, NB)
                dve.wait_ge(pld, 32)
                then(nc.vector.reduce_max(m[:], lg[:], AX))
                nc.vector.tensor_tensor(t1[:], lg[:], over_e(m), ALU.subtract).then_inc(shifted, 1)
                dve.wait_ge(shifted, 1)
                nc.vector.tensor_scalar(t2[:], t1[:], 0.0, None, ALU.is_equal).then_inc(shifted, 1)
                dve.wait_ge(shifted, 2)
                then(nc.vector.tensor_tensor(t2[:], t2[:], prio[:, None, :].to_broadcast([P, NT, E]), ALU.mult))
                then(nc.vector.reduce_max(m[:], t2[:], AX))
                nc.vector.tensor_tensor(oh[:], t2[:], over_e(m), ALU.is_equal).then_inc(onehot, 1)
                dve.wait_ge(expd, 1)
                then(nc.vector.reduce_sum(sc[:], t1[:], AX))
                then(nc.vector.reciprocal(sc[:], sc[:]))
                dve.wait_ge(rank_ps, 1)
                then(nc.vector.tensor_copy(t1[:], bank[3][:].rearrange("p (t e) -> p t e", e=E)))
                then(nc.vector.tensor_copy(t3[:], t1[:]))
                a, z = t1, t2
                k = 1
                while k < NT:
                    nc.vector.tensor_copy(z[:, 0:k, :], a[:, 0:k, :])
                    then(nc.vector.tensor_tensor(z[:, k:NT, :], a[:, k:NT, :], a[:, 0:NT - k, :], ALU.add))
                    a, z = z, a
                    k *= 2
                then(nc.vector.tensor_scalar(nbi[:], a[:, NT - 1, :], float(P - 1), None, ALU.add))
                then(nc.vector.tensor_single_scalar(nbi[:], nbi[:], -P, ALU.bitwise_and))
                then(nc.vector.tensor_copy(tot[:], nbi[:]))
                then(nc.vector.memset(off[:, 0:1], 0.0))
                for e in range(E):
                    then(nc.vector.tensor_tensor(off[:, e + 1:e + 2], off[:, e:e + 1], tot[:, e:e + 1], ALU.add))
                then(nc.vector.tensor_tensor(a[:], a[:], t3[:], ALU.subtract))
                then(nc.vector.tensor_tensor(a[:], a[:], bank[2][:].rearrange("p (t e) -> p t e", e=E), ALU.add))
                then(nc.vector.tensor_tensor(a[:], a[:], off[:, None, 0:E].to_broadcast([P, NT, E]), ALU.add))
                then(nc.vector.tensor_tensor(a[:], a[:], oh[:], ALU.mult))
                then(nc.vector.reduce_sum(pos[:], a[:], AX))
                nc.vector.tensor_copy(posi[:], pos[:]).then_inc(routed, 1)
                then(nc.vector.tensor_tensor(cmp8[:], off[:, None, 1:E + 1].to_broadcast([P, NBLK, E]),
                                             start[:, :, None].to_broadcast([P, NBLK, E]), ALU.is_le))
                then(nc.vector.reduce_sum(cnt[:], cmp8[:], AX))
                then(nc.vector.tensor_scalar(eb[:], cnt[:], float(E - 1), None, ALU.min))

        NS = 4
        with nc.Block() as block:

            def quads(eng, body):
                for j in range(NS):
                    body(j, j)
                with eng.Fori(0, NBLK // NS - 2) as i:
                    for p in range(NS):
                        body(NS * i + NS + p, p)
                for j in range(NBLK - NS, NBLK):
                    body(j, j % NS)

            def early(j, n):
                return isinstance(j, int) and j < n

            def slot_count(j, p):
                return 16 * (j // NS + 1) if isinstance(j, int) else (j - p + NS) * (16 // NS)

            @block.sync
            def _(sp):
                def load(j, p):
                    if not early(j, NS):
                        sp.wait_ge(xT_ps, j - NS + 1)
                    sp.dma_start(xb[:, p, :], moe["xdisp"][ds(j * P, P), :]).then_inc(xl[p], 16)
                quads(sp, load)

            @block.tensor
            def _(pe):
                def rows_transpose(j, p):
                    pe.wait_ge(xl[p], slot_count(j, p))
                    if not early(j, 2):
                        pe.wait_ge(xT_sb, j - 1)
                    nc.tensor.transpose(bank[p % 2][:, 0:P], xb[:, p, :], ident[:]).then_inc(xT_ps, 1)

                def hidden(j, p):
                    pe.wait_ge(xT_sb, j + 1)
                    pe.wait_ge(wl[p], slot_count(j, p))
                    if not early(j, 2):
                        pe.wait_ge(h_sb, HC * (j - 1))
                    for k in range(HC):
                        last = nc.tensor.matmul(bank[2 + p % 2][:, k * P:(k + 1) * P], wc[:, p, k * P:(k + 1) * P],
                                                xT[:, p, :], start=True, stop=True)
                    last.then_inc(h_ps, 1)

                def result(j, p):
                    e = pe.value_load(eb[0:1, ds(j, 1)], min_val=0, max_val=E - 1)
                    pe.wait_ge(h_sb, HC * (j + 1))
                    if not early(j, 2):
                        pe.wait_ge(y_sb, j - 1)
                    for k in range(HC):
                        last = nc.tensor.matmul(bank[4 + p % 2][:, None, 0:D], hT[:, p, k * P:(k + 1) * P],
                                                moe["w2s"][:, ds(e * HC + k, 1), :], start=(k == 0), stop=(k == HC - 1))
                    last.then_inc(y_ps_done, 1)

                def body(j, p):
                    if not isinstance(j, int) or j + 1 < NBLK:
                        rows_transpose(j + 1, (p + 1) % NS)
                    hidden(j, p)
                    if not early(j, 2):
                        result(j - 2, (p - 2) % NS)

                rows_transpose(0, 0)
                quads(pe, body)
                for j in (NBLK - 2, NBLK - 1):
                    result(j, j % NS)

            @block.scalar
            def _(act):
                def gelu(j, p):
                    act.wait_ge(h_ps, j + 1)
                    if not early(j, NS):
                        act.wait_ge(y_ps_done, j - NS + 1)
                    for k in range(HC):
                        nc.scalar.activation(hT[:, p, k * P:(k + 1) * P], bank[2 + p % 2][:, k * P:(k + 1) * P],
                                             ACT.Gelu, bias=wc[:, p, HID + k:HID + k + 1]).then_inc(h_sb, 1)

                def load_weights(j, p):
                    e = act.value_load(eb[0:1, ds(j, 1)], min_val=0, max_val=E - 1)
                    if not early(j, NS):
                        act.wait_ge(h_sb, HC * (j - NS + 1))
                    act.dma_start(wc[:, p, None, :], moe["w1b"][:, ds(e, 1), :]).then_inc(wl[p], 16)

                def body(j, p):
                    gelu(j, p)
                    if not isinstance(j, int) or j + NS - 1 < NBLK:
                        load_weights(j + NS - 1, (p + NS - 1) % NS)

                for j in range(NS - 1):
                    load_weights(j, j)
                quads(act, body)

            @block.vector
            def _(dve):
                def copy_xT(j, p):
                    dve.wait_ge(xT_ps, j + 1)
                    if not early(j, NS):
                        dve.wait_ge(h_ps, j - NS + 1)
                    nc.vector.tensor_copy(xT[:, p, :], bank[p % 2][:, 0:P]).then_inc(xT_sb, 1)

                def copy_y(j, p):
                    e = dve.value_load(eb[0:1, ds(j, 1)], min_val=0, max_val=E - 1)
                    dve.wait_ge(y_ps_done, j + 1)
                    if not early(j, NS):
                        dve.wait_ge(st[p], slot_count(j, p) - 16)
                    nc.vector.tensor_tensor(yb[:, p, :], bank[4 + p % 2][:, 0:D], moe["b2bc"][:, ds(e * D, D)],
                                            ALU.add).then_inc(y_sb, 1)

                def body(j, p):
                    if not isinstance(j, int) or j + 1 < NBLK:
                        copy_xT(j + 1, (p + 1) % NS)
                    if not early(j, 2):
                        copy_y(j - 2, (p - 2) % NS)

                copy_xT(0, 0)
                quads(dve, body)
                for j in (NBLK - 2, NBLK - 1):
                    copy_y(j, j % NS)

            @block.gpsimd
            def _(pool):
                def store(j, p):
                    pool.wait_ge(y_sb, j + 1)
                    pool.dma_start(moe["ydisp"][ds(j * P, P), :], yb[:, p, :]).then_inc(st[p], 16)
                quads(pool, store)
                for p in range(NS):
                    pool.wait_ge(st[p], 16 * NBLK // NS)
                for i in range(NT):
                    pool.indirect_dma_start(xn_all[:, i, :], None, moe["ydisp"],
                                            bass.IndirectOffsetOnAxis(ap=posi[:, i:i + 1], axis=0)).then_inc(gat[i // 8], 16)

            @block.vector
            def _(dve):
                for i in range(NT):
                    if i % 8 == 0:
                        dve.wait_ge(gat[i // 8], 128)
                    nc.vector.scalar_tensor_tensor(xs[:, i, :], xn_all[:, i, :], sc[:, i:i + 1], xs[:, i, :],
                                                   ALU.mult, ALU.add)


def retention(nc, ap, buf, sem):
    bank, ident, xs = buf["bank"], buf["ident"], buf["xs"]
    T_BANK, Q_BANK, K_BANK, VG_BANK = bank[0], bank[1], bank[2], bank[3]
    S_BANK, O_BANK = bank[4:6], bank[6:8]
    S = lambda n: sem(f"r_{n}")
    ln = Norm(nc, buf, sem, "r")
    ld, init = S("ld"), S("init")
    xnT_ps, xnT_sb, q_ps, k_ps, v_ps, g_ps, v_sb, g_sb = (S(n) for n in (
        "xnT_ps", "xnT_sb", "q_ps", "k_ps", "v_ps", "g_ps", "v_sb", "g_sb"))
    turned, rotated, hi_done, rest_done, mid_done, lo_done = (S(n) for n in (
        "turned", "rotated", "hi", "rest", "mid", "lo"))
    stored, stacked = [S("stored0"), S("stored1")], [S("stacked0"), S("stacked1")]
    s_ps, s_sb, o_ps, squared, o_step, root, scaled, gated = (S(n) for n in (
        "s_ps", "s_sb", "o_ps", "squared", "o_step", "root", "scaled", "gated"))
    gT_ps, gT_sb, y_ps, x_added = (S(n) for n in ("gT_ps", "gT_sb", "y_ps", "x_added"))
    bounce = nc.dram_tensor("r_bounce", (2, P, 3, 2, 256), BF16).ap()
    with ExitStack() as c:
        def sb(name, shape, dt=F32):
            return c.enter_context(nc.sbuf_tensor("r_" + name, shape, dt))
        w4, wv, wg, wo = sb("w4", [P, 4, D]), sb("wv", [P, VD]), sb("wg", [P, VD]), sb("wo", [P, 2, D])
        tab, mask = sb("tab", [P, 4, 256]), sb("mask", [P, RH, SC])
        xnT = sb("xnT", [P, 2, 256])
        r1, r2 = sb("r1", [P, 2, 256]), sb("r2", [P, 2, 256])
        qk, rest = sb("qk", [P, 2, 256]), sb("rest", [P, 2, 256])
        parts = sb("parts", [P, 3, 2, 256], BF16)
        stk = sb("stk", [NTERM * KD, 2, 2, RH, 256], BF16)
        v33, gate = sb("v33", [P, 2, TPB, RH, RW]), sb("gate", [P, 2, TPB, VD])
        sT = sb("sT", [P, RH, SC])
        osq, dn, ms, fac = sb("osq", [P, TPB, RH, RHD]), sb("dn", [P, 16]), sb("ms", [P, 16]), sb("fac", [P, TPB, RH])
        oh, on, onT = sb("oh", [P, TPB, RH, RHD]), sb("on", [P, TPB, VD]), sb("onT", [P, 4 * P])
        block = c.enter_context(nc.Block())

        def rounds(eng, body):
            for b in (0, 1):
                body(b, b)
            with eng.Fori(0, (NB - 6) // 2) as i:
                body(2 * i + 2, 0)
                body(2 * i + 3, 1)
            for b in range(NB - 4, NB):
                body(b, b % 2)

        def known(b):
            return isinstance(b, int)

        @block.sync
        def _(sp):
            for dst, name in ((w4, "w4"), (wv, "wv"), (wg, "wgate"), (wo, "wo"), (tab, "tab"), (mask, "mask")):
                sp.dma_start(dst[:], ap[name]).then_inc(ld, 16)

            def stack(b, p, turn):
                sp.wait_ge(lo_done, b + 1)
                sp.dma_start(bounce[p], parts[:]).then_inc(stored[p], 16)
                if not known(b) or b >= 2:
                    sp.wait_ge(s_ps, RH * (b - 1))
                sp.wait_ge(stored[p], 16 * turn)
                for t in range(NTERM):
                    for side, part in ((0, PART_A[t]), (1, PART_B[t])):
                        sp.dma_start(stk[KD * t:KD * (t + 1), p, side, :, :],
                                     bounce[p, :, part, side, :].rearrange("(h d) n -> d h n", d=KD)).then_inc(stacked[p], 16)
            stack(0, 0, 1)
            stack(1, 1, 1)
            with sp.Fori(0, NB // 2 - 1) as i:
                stack(2 * i + 2, 0, i + 2)
                stack(2 * i + 3, 1, i + 2)

        @block.gpsimd
        def _(pool):
            nc.gpsimd.memset(v33[:], 1.0).then_inc(init, 1)

            def split(b):
                pool.wait_ge(hi_done, b + 1)
                nc.gpsimd.tensor_tensor(rest[:], qk[:], parts[:, 0], ALU.subtract).then_inc(rest_done, 1)
                pool.wait_ge(mid_done, b + 1)
                nc.gpsimd.tensor_tensor(parts[:, 2], rest[:], parts[:, 1], ALU.subtract).then_inc(lo_done, 1)

            def head_root(b):
                pool.wait_ge(o_step, 6 * b + 6)
                nc.gpsimd.tensor_tensor(fac[:].rearrange("p t h -> p (t h)"), ms[:], buf["mhalf"][:],
                                        ALU.pow).then_inc(root, 1)

            def body(b, p):
                if not known(b) or b > 0:
                    head_root(b - 1)
                if not known(b) or b + 2 < NB:
                    split(b + 2)
                if not known(b) or b + 3 < NB:
                    ln.root(pool, b + 3)
            for b in range(2):
                ln.root(pool, b)
                split(b)
            ln.root(pool, 2)
            rounds(pool, body)
            head_root(NB - 1)

        @block.tensor
        def _(pe):
            def norm_transposes(b, p):
                pe.wait_ge(ln.done, b + 1)
                if not known(b) or b >= 4:
                    pe.wait_ge(gT_sb, b - 3)
                if not known(b) or b >= 1:
                    pe.wait_ge(xnT_sb, b)
                for t in range(TPB):
                    last = nc.tensor.transpose(T_BANK[:, t * P:(t + 1) * P], buf["xn"][:, t, :], ident[:])
                last.then_inc(xnT_ps, 1)

            def project(b, p, side):
                if side == 0:
                    pe.wait_ge(xnT_sb, b + 1)
                if not known(b) or b >= 1:
                    pe.wait_ge(turned, 2 * b - (1 - side))
                for j in range(2):
                    last = nc.tensor.matmul((Q_BANK, K_BANK)[side][:, j * 256:j * 256 + 256], w4[:, 2 * side + j, :],
                                            xnT[:, p, :], start=True, stop=True)
                last.then_inc((q_ps, k_ps)[side], 1)

            def values(b, p):
                if not known(b) or b >= 3:
                    pe.wait_ge(x_added, b - 2)
                if not known(b) or b >= 1:
                    pe.wait_ge(g_sb, b)
                for t in range(TPB):
                    last = nc.tensor.matmul(VG_BANK[:, t * VD:(t + 1) * VD], xnT[:, p, t * P:(t + 1) * P], wv[:],
                                            start=True, stop=True)
                last.then_inc(v_ps, 1)

            def gates(b, p):
                pe.wait_ge(v_sb, b + 1)
                for t in range(TPB):
                    last = nc.tensor.matmul(VG_BANK[:, t * VD:(t + 1) * VD], xnT[:, p, t * P:(t + 1) * P], wg[:],
                                            start=True, stop=True)
                last.then_inc(g_ps, 1)

            def scores(b, p, h):
                if h == 0:
                    pe.wait_ge(stacked[p], 16 * 2 * NTERM * ((b - p) // 2 + 1) if known(b) else 16 * NTERM * (b - p + 2))
                if not known(b) or b > 0 or h >= 2:
                    pe.wait_ge(s_sb, RH * b + h - 1)
                dst = S_BANK[h % 2]
                nc.tensor.matmul(dst[:, 0:256], stk[:, p, 1, h, 0:P], stk[:, p, 0, h, :], start=True, stop=True)
                nc.tensor.matmul(dst[:, 256:SC], stk[:, p, 1, h, P:256], stk[:, p, 0, h, P:256],
                                 start=True, stop=True).then_inc(s_ps, 1)

            def outputs(b, p, h):
                pe.wait_ge(s_sb, RH * b + h + 1)
                if h == 0:
                    pe.wait_ge(v_sb, b + 1)
                    if not known(b) or b > 0:
                        pe.wait_ge(scaled, 2 * b)
                col = slice(h * RW, (h + 1) * RW)
                nc.tensor.matmul(O_BANK[0][:, col], sT[:, h, 0:P], v33[:, p, 0, h, :], start=True, stop=True)
                nc.tensor.matmul(O_BANK[1][:, col], sT[:, h, P:256], v33[:, p, 0, h, :], start=True, stop=False)
                nc.tensor.matmul(O_BANK[1][:, col], sT[:, h, 256:SC], v33[:, p, 1, h, :], start=False,
                                 stop=True).then_inc(o_ps, 1)

            def gated_transposes(b):
                pe.wait_ge(gated, b + 1)
                pe.wait_ge(xnT_sb, b + 4 if not known(b) or b + 4 <= NB else NB)
                for t in range(TPB):
                    for k in range(2):
                        last = nc.tensor.transpose(T_BANK[:, (2 * t + k) * P:(2 * t + k + 1) * P],
                                                   on[:, t, k * P:(k + 1) * P], ident[:])
                last.then_inc(gT_ps, 1)

            def output_product(b):
                pe.wait_ge(gT_sb, b + 1)
                pe.wait_ge(g_sb, b + 3 if not known(b) or b + 3 <= NB else NB)
                for t in range(TPB):
                    for k in range(2):
                        last = nc.tensor.matmul(VG_BANK[:, t * D:(t + 1) * D], onT[:, (2 * t + k) * P:(2 * t + k + 1) * P],
                                                wo[:, k, :], start=(k == 0), stop=(k == 1))
                last.then_inc(y_ps, 1)

            def body(b, p):
                first, two_more, one_more = known(b) and b == 0, not known(b) or b + 2 < NB, not known(b) or b + 1 < NB
                scores(b, p, 0)
                scores(b, p, 1)
                if two_more:
                    norm_transposes(b + 2, p)
                if one_more:
                    values(b + 1, 1 - p)
                scores(b, p, 2)
                if two_more:
                    project(b + 2, p, 0)
                scores(b, p, 3)
                if two_more:
                    project(b + 2, p, 1)
                scores(b, p, 4)
                outputs(b, p, 0)
                scores(b, p, 5)
                outputs(b, p, 1)
                if one_more:
                    gates(b + 1, 1 - p)
                scores(b, p, 6)
                outputs(b, p, 2)
                scores(b, p, 7)
                outputs(b, p, 3)
                outputs(b, p, 4)
                if not first:
                    gated_transposes(b - 1)
                outputs(b, p, 5)
                outputs(b, p, 6)
                if not first:
                    output_product(b - 1)
                outputs(b, p, 7)

            pe.wait_ge(ld, 96)
            for b in range(2):
                norm_transposes(b, b)
                project(b, b, 0)
                project(b, b, 1)
            values(0, 0)
            gates(0, 0)
            rounds(pe, body)
            gated_transposes(NB - 1)
            output_product(NB - 1)

        @block.scalar
        def _(act):
            def copy_xnT(b, p):
                act.wait_ge(xnT_ps, b + 1)
                if not known(b) or b >= 2:
                    act.wait_ge(g_ps, b - 1)
                nc.scalar.copy(xnT[:, p, :], T_BANK[:, 0:256]).then_inc(xnT_sb, 1)

            def copy_v(b, p):
                act.wait_ge(v_ps, b + 1)
                if not known(b) or b >= 2:
                    act.wait_ge(o_ps, RH * (b - 1))
                nc.scalar.copy(v33[:, p, :, :, 0:RHD], VG_BANK[:].rearrange("p (t h c) -> p t h c", t=TPB, h=RH)).then_inc(v_sb, 1)

            def silu_g(b, p):
                act.wait_ge(g_ps, b + 1)
                if not known(b) or b >= 2:
                    act.wait_ge(gated, b - 1)
                nc.scalar.activation(gate[:, p], VG_BANK[:].rearrange("p (t c) -> p t c", t=TPB), ACT.Silu).then_inc(g_sb, 1)

            def high(b, p):
                act.wait_ge(rotated, b + 1)
                if not known(b) or b > 0:
                    act.wait_ge(stored[1 - p], 8 * (b + p))
                nc.scalar.copy(parts[:, 0], qk[:]).then_inc(hi_done, 1)

            def middle(b):
                act.wait_ge(rest_done, b + 1)
                nc.scalar.copy(parts[:, 1], rest[:]).then_inc(mid_done, 1)

            def squares(b):
                act.wait_ge(o_ps, RH * (b + 1))
                for t in range(TPB):
                    o4 = O_BANK[t][:, 0:RH * RW].rearrange("p (h c) -> p h c", c=RW)
                    nc.scalar.activation(osq[:, t], o4[:, :, 0:RHD], ACT.Square).then_inc(squared, 1)

            def copy_onT(b):
                act.wait_ge(gT_ps, b + 1)
                nc.scalar.copy(onT[:], T_BANK[:]).then_inc(gT_sb, 1)

            def body(b, p):
                first, two_more, one_more = known(b) and b == 0, not known(b) or b + 2 < NB, not known(b) or b + 1 < NB
                if not first:
                    squares(b - 1)
                if two_more:
                    copy_xnT(b + 2, p)
                if one_more:
                    copy_v(b + 1, 1 - p)
                if two_more:
                    high(b + 2, p)
                if one_more:
                    silu_g(b + 1, 1 - p)
                if two_more:
                    middle(b + 2)
                if not first:
                    copy_onT(b - 1)

            act.wait_ge(init, 1)
            act.wait_ge(ld, 96)
            for b in range(2):
                copy_xnT(b, b)
                high(b, b)
                middle(b)
            copy_v(0, 0)
            silu_g(0, 0)
            rounds(act, body)
            squares(NB - 1)
            copy_onT(NB - 1)

        @block.vector
        def _(dve):
            def xn(t):
                return buf["xn"][:, t, :]

            def normalised(b):
                if not known(b) or b > 0:
                    dve.wait_ge(xnT_ps, b)
                ln.scale(dve, b, xn)

            def rotate(b):
                for i in range(2):
                    dve.wait_ge((q_ps, k_ps)[i], b + 1)
                    nc.vector.tensor_tensor(r1[:, i, :], (Q_BANK, K_BANK)[i][:, 0:256], tab[:, 2 * i, :], ALU.mult)
                    nc.vector.tensor_tensor(r2[:, i, :], (Q_BANK, K_BANK)[i][:, 256:512], tab[:, 2 * i + 1, :],
                                            ALU.mult).then_inc(turned, 1)
                dve.wait_ge(turned, 2 * b + 2)
                if not known(b) or b > 0:
                    dve.wait_ge(lo_done, b)
                nc.vector.tensor_tensor(qk[:], r1[:], r2[:], ALU.add).then_inc(rotated, 1)

            def masked(b, h):
                dve.wait_ge(s_ps, RH * b + h + 1)
                if not known(b) or b > 0:
                    dve.wait_ge(o_ps, RH * b - RH + h + 1)
                nc.vector.tensor_tensor(sT[:, h, :], S_BANK[h % 2][:, 0:SC], mask[:, h, :], ALU.mult).then_inc(s_sb, 1)

            def head_stats(b):
                dve.wait_ge(squared, 2 * b + 2)
                sums = [O_BANK[t][:, 0:RH * RW].rearrange("p (h c) -> p h c", c=RW)[:, :, RHD] for t in range(TPB)]
                for t in range(TPB):
                    nc.vector.tensor_scalar(dn[:, t * RH:(t + 1) * RH], sums[t], 1.0, None, ALU.max).then_inc(o_step, 1)
                nc.vector.reduce_sum(ms[:], osq[:].rearrange("p t h c -> p (t h) c"), AX).then_inc(o_step, 1)
                dve.wait_ge(o_step, 6 * b + 2)
                for t in range(TPB):
                    last = nc.vector.scalar_tensor_tensor(dn[:, t * RH:(t + 1) * RH], sums[t], -1.0,
                                                          dn[:, t * RH:(t + 1) * RH], ALU.mult, ALU.max)
                last.then_inc(o_step, 1)
                dve.wait_ge(o_step, 6 * b + 4)
                nc.vector.scalar_tensor_tensor(dn[:], dn[:], EPS, dn[:], ALU.mult, ALU.mult).then_inc(o_step, 1)
                dve.wait_ge(o_step, 6 * b + 5)
                nc.vector.scalar_tensor_tensor(ms[:], ms[:], 1.0 / RHD, dn[:], ALU.mult, ALU.add).then_inc(o_step, 1)

            def scale_heads(b, p):
                dve.wait_ge(root, b + 1)
                for t in range(TPB):
                    o4 = O_BANK[t][:, 0:RH * RW].rearrange("p (h c) -> p h c", c=RW)
                    nc.vector.tensor_tensor(oh[:, t], o4[:, :, 0:RHD], fac[:, t, :, None].to_broadcast([P, RH, RHD]),
                                            ALU.mult).then_inc(scaled, 1)
                dve.wait_ge(scaled, 2 * b + 2)
                dve.wait_ge(g_sb, b + 1)
                if not known(b) or b > 0:
                    dve.wait_ge(gT_ps, b)
                nc.vector.tensor_tensor(on[:], oh[:].rearrange("p t h c -> p t (h c)"), gate[:, p],
                                        ALU.mult).then_inc(gated, 1)

            def add(b):
                dve.wait_ge(y_ps, b + 1)
                nc.vector.tensor_tensor(xs[:, ds(2 * b, 2), :], VG_BANK[:, 0:256].rearrange("p (t c) -> p t c", t=TPB),
                                        xs[:, ds(2 * b, 2), :], ALU.add).then_inc(x_added, 1)

            def body(b, p):
                first, two_more = known(b) and b == 0, not known(b) or b + 2 < NB
                masked(b, 0)
                if not first:
                    head_stats(b - 1)
                masked(b, 1)
                masked(b, 2)
                if not first:
                    scale_heads(b - 1, 1 - p)
                masked(b, 3)
                masked(b, 4)
                if two_more:
                    rotate(b + 2)
                masked(b, 5)
                masked(b, 6)
                if not known(b) or b + 3 < NB:
                    ln.stats(dve, b + 3)
                masked(b, 7)
                if not first:
                    add(b - 1)
                if not known(b) or b + 3 < NB:
                    normalised(b + 3)

            dve.wait_ge(ld, 96)
            for b in range(2):
                ln.stats(dve, b)
                normalised(b)
                rotate(b)
            ln.stats(dve, 2)
            normalised(2)
            rounds(dve, body)
            head_stats(NB - 1)
            scale_heads(NB - 1, 1)
            add(NB - 1)


def tables():
    f = np.float32
    S = TPB * P
    angle = np.repeat(f(1.0) / f(10000.0) ** np.linspace(0.0, 1.0, KD // 2, dtype=f), 2).astype(f)
    idx = np.arange(S, dtype=f)
    arg = (idx[None, :] * angle[:, None]).astype(f)
    cos, sin = np.cos(arg).astype(f), np.sin(arg).astype(f)
    sign = np.where(np.arange(KD) % 2 == 0, -1.0, 1.0).astype(f)[:, None]
    c, s = np.tile(cos, (RH, 1)), np.tile(sin * sign, (RH, 1))
    scale = f(KD ** -0.5)
    tab = np.stack([c, s, c * scale, s * scale], 1).astype(f)
    decay = np.log1p(-2.0 ** (-5.0 - np.arange(RH))).astype(f)
    diff = idx[:, None] - idx[None, :]
    m = np.where(diff[None] >= 0, np.exp(diff[None] * decay[:, None, None]), 0.0).astype(f)
    m = (m / np.sqrt(m.sum(-1, keepdims=True, dtype=f))).astype(f)
    mt = m.transpose(2, 0, 1)
    mask = np.concatenate([mt[0:P], mt[P:S, :, P:S]], 2)
    par = np.zeros((P, 2), f)
    for h in range(RH):
        par[h * KD:(h + 1) * KD, h % 2] = 1
    return dict(
        tab=tab, mask=mask, par=par, ident=np.eye(P, dtype=f), before=np.triu(np.ones((P, P), f), 1),
        prio=(E - np.arange(E, dtype=f))[None], start=(P * np.arange(NBLK, dtype=f))[None],
    )


def kernel(L0_attn_a_x, L0_attn_a_W_qkv, L0_attn_a_proj, L0_attn_a_W_out, L0_attn_a_b_out, L0_attn_b_wq, L0_attn_b_wk,
           L0_attn_b_wv, L0_attn_b_wg, L0_attn_b_wo, L0_ffn_wg_red, L0_ffn_wg, L0_ffn_w1, L0_ffn_b1, L0_ffn_w2, L0_ffn_b2):
    import concourse.bacc as bacc
    from concourse.bass_utils import run_bass_kernel_spmd

    A = lambda a: np.asarray(a)
    swap = np.arange(D) ^ 1
    wq, wk = A(L0_attn_b_wq), A(L0_attn_b_wk)
    arrays = dict(
        x=A(L0_attn_a_x).reshape(NT, P, D).transpose(1, 0, 2),
        wqkvT=A(L0_attn_a_W_qkv).T, proj=A(L0_attn_a_proj), woutT=A(L0_attn_a_W_out).T, b_out=A(L0_attn_a_b_out)[None],
        w4=np.stack([wq, wq[:, swap], wk, wk[:, swap]], 1), wv=A(L0_attn_b_wv), wgate=A(L0_attn_b_wg),
        wo=A(L0_attn_b_wo).reshape(2, P, D).transpose(1, 0, 2),
        wg_red=A(L0_ffn_wg_red), wg=A(L0_ffn_wg), w1=A(L0_ffn_w1).transpose(1, 0, 2),
        b1=A(L0_ffn_b1).reshape(E, HC, P).transpose(2, 0, 1),
        w2=A(L0_ffn_w2).reshape(E * HC, P, D).transpose(1, 0, 2), b2=A(L0_ffn_b2).reshape(1, E * D),
        **tables(),
    )
    arrays = {k: np.ascontiguousarray(v) for k, v in arrays.items()}
    nc = bacc.Bacc("TRN2", target_bir_lowering=False, num_devices=1)
    ap = {k: nc.dram_tensor("in_" + k, v.shape, F32, kind="ExternalInput").ap() for k, v in arrays.items()}
    out = nc.dram_tensor("out", (P, NT, D), F32, kind="ExternalOutput").ap()
    build(nc, ap, out)
    r = run_bass_kernel_spmd(nc, [{"in_" + k: v for k, v in arrays.items()}], core_ids=[0])
    return r.results[0]["out"].transpose(1, 0, 2).reshape(NB, TPB * P, D)
```

```python
from contextlib import ExitStack, contextmanager

import numpy as np

import concourse.bass as bass
from concourse import mybir

F32 = mybir.dt.float32
BF16 = mybir.dt.bfloat16
I32 = mybir.dt.int32
ALU = mybir.AluOpType
ACT = mybir.ActivationFunctionType
AX = mybir.AxisListType.X
ds = bass.ds

P = 128
NB = 32
TPB = 2
NT = NB * TPB
D = 128
EPS = 1e-5
H, HD, F = 16, 8, 128
KVW = HD + 1
CT = 32
U = 16
E, HID, GD = 8, 512, 16
HC = HID // P
HT = NT // 2
HBLK = HT + E - 1
NBLK = 2 * HBLK
ZBLK = 6
ZCHUNKS = NBLK // ZBLK
GT = 4
W1W = HID + HC
RH, KD, VD = 8, 16, 256
RHD = VD // RH
RW = 64
PART_A, PART_B = (0, 0, 1, 1, 0, 2), (0, 1, 0, 1, 2, 0)
NTERM = len(PART_A)
SC = 3 * P


@contextmanager
def phase(nc, name):
    with ExitStack() as c:
        taken = []

        def sem(n):
            taken.append(c.enter_context(nc.semaphore(n)))
            return taken[-1]

        yield sem
        with nc.Block(f"{name}_clear") as block:
            @block.vector
            def _(dve):
                for one in taken[0::3]:
                    dve.sem_clear(one)

            @block.scalar
            def _(act):
                for one in taken[1::3]:
                    act.sem_clear(one)

            @block.gpsimd
            def _(pool):
                for one in taken[2::3]:
                    pool.sem_clear(one)


def known(b):
    return isinstance(b, int)


def build(nc, ap, out):
    ctx = ExitStack()

    def sb(name, shape, dt=F32):
        return ctx.enter_context(nc.sbuf_tensor(name, shape, dt))

    def sem(name):
        return ctx.enter_context(nc.semaphore(name))

    with ctx:
        bank = [ctx.enter_context(nc.psum_tensor(f"bank{i}", [P, 512], F32)) for i in range(8)]
        xs = sb("xs", [P, NT, D])
        xn_all = sb("xn_all", [P, NT, D])
        ident = sb("ident", [P, P])
        next_stats = sb("next_stats", [P, NT, 6])
        buf = dict(
            bank=bank, xs=xs, xn_all=xn_all, ident=ident, next_stats=next_stats,
            xn=sb("xn", [P, TPB, D]), xnT=sb("xnT", [P, TPB * P]),
            stats=sb("stats", [P, TPB, 6]), both=sb("both", [P, TPB, 2]),
            diff=sb("diff", [P, TPB]), sq=sb("sq", [P, TPB]), mean=sb("mean", [P, TPB]), quarter=sb("quarter", [P, HT]),
            var=sb("var", [P, TPB]), rstd=sb("rstd", [P, TPB]), mhalf=sb("mhalf", [P, HT]),
        )
        xdisp = nc.dram_tensor("xdisp", (NBLK * P, D), F32).ap()
        ydisp = nc.dram_tensor("ydisp", (NBLK * P, D), F32).ap()
        bulk = dict(x0=sem("ld_x0"), x=sem("ld_x"), w=sem("ld_moe"), zero=sem("ld_zero"))

        moe = dict(
            w1b=sb("w1b", [P, E, W1W]), w2s=sb("w2s", [P, E * HC, D]), b2bc=sb("b2bc", [P, E * D]),
            zrow=sb("zrow", [P, ZBLK * D]), G=sb("G", [P, E]),
            posi=sb("posi", [P, NT], I32), sc=sb("sc", [P, NT]),
            earlier=sb("earlier", [P, P]), ones=sb("ones", [P, P]), xdisp=xdisp, ydisp=ydisp,
        )
        setup(nc, ap, buf, moe, bulk, sem)
        with phase(nc, "attention") as psem:
            linear_attention(nc, ap, buf, moe, bulk, psem)
        with ExitStack() as c:
            shapes = dict(w4=[P, 4, D], wv=[P, VD], wgate=[P, VD], wo=[P, 2, D], tab=[P, 4, 256], mask=[P, RH, SC])
            const = {n: c.enter_context(nc.sbuf_tensor(n, shape, F32)) for n, shape in shapes.items()}
            with phase(nc, "experts_0") as psem:
                expert_layer(nc, ap, buf, moe, psem, "f0", const=const)
            with phase(nc, "retention") as psem:
                retention(nc, ap, buf, moe, const, psem)
        with phase(nc, "experts_1") as psem:
            expert_layer(nc, ap, buf, moe, psem, "f1", out=out)


def setup(nc, ap, buf, moe, bulk, sem):
    ld_c, gate_step = sem("ld_const"), sem("gate_step")
    pe_g, dve_g = sem("gate_pe"), sem("gate_dve")
    bank = buf["bank"]
    with (
        nc.sbuf_tensor("wgr", [GD, D], F32) as wgr,
        nc.sbuf_tensor("wge", [E, GD], F32) as wge,
        nc.sbuf_tensor("wsq", [E, GD], F32) as wsq,
        nc.sbuf_tensor("wn", [E, 4], F32) as wn,
        nc.sbuf_tensor("wgT", [GD, E], F32) as wgT,
        nc.Block() as block,
    ):
        @block.sync
        def _(sp):
            sp.dma_start(wge[:], ap["wg"]).then_inc(ld_c, 16)
            sp.dma_start(wgr[:], ap["wg_red"]).then_inc(ld_c, 16)
            sp.dma_start(buf["xs"][:, 0:8, :], ap["x"][:, 0:8, :]).then_inc(bulk["x0"], 16)

        @block.scalar
        def _(act):
            act.dma_start(buf["ident"][:], ap["ident"]).then_inc(ld_c, 16)
        @block.gpsimd
        def _(pool):
            nc.gpsimd.memset(moe["zrow"][:], 0.0)
            nc.gpsimd.memset(buf["mhalf"][:], -0.5)
            nc.gpsimd.memset(buf["quarter"][:], 0.25)

        @block.vector
        def _(dve):
            nc.vector.memset(moe["ones"][:], 1.0)
            dve.wait_ge(ld_c, 48)
            nc.vector.tensor_tensor(wsq[:], wge[:], wge[:], ALU.mult).then_inc(dve_g, 1)
            dve.wait_ge(dve_g, 1)
            nc.vector.reduce_sum(wn[:, 0:1], wsq[:], AX).then_inc(dve_g, 1)
            dve.wait_ge(gate_step, 1)
            nc.vector.tensor_scalar_max(wn[:, 2:3], wn[:, 1:2], 1e-4).then_inc(dve_g, 1)
            dve.wait_ge(dve_g, 3)
            nc.vector.reciprocal(wn[:, 3:4], wn[:, 2:3]).then_inc(dve_g, 1)
            dve.wait_ge(dve_g, 4)
            nc.vector.tensor_scalar(wsq[:], wge[:], wn[:, 3:4], None, ALU.mult).then_inc(dve_g, 1)
            dve.wait_ge(pe_g, 1)
            nc.vector.tensor_copy(wgT[:], bank[0][0:GD, 0:E]).then_inc(dve_g, 1)
            dve.wait_ge(pe_g, 2)
            nc.vector.tensor_copy(moe["G"][:], bank[1][:, 0:E])

        @block.scalar
        def _(act):
            act.wait_ge(dve_g, 2)
            nc.scalar.activation(wn[:, 1:2], wn[:, 0:1], ACT.Sqrt).then_inc(gate_step, 1)

        @block.tensor
        def _(pe):
            pe.wait_ge(dve_g, 5)
            nc.tensor.transpose(bank[0][0:GD, 0:E], wsq[:], buf["ident"][0:E, 0:E]).then_inc(pe_g, 1)
            pe.wait_ge(dve_g, 6)
            nc.tensor.matmul(bank[1][:, 0:E], wgr[:], wgT[:], start=True, stop=True).then_inc(pe_g, 1)


def stats_for_experts(nc, buf, b):
    for t in range(TPB):
        nc.vector.bn_stats(buf["next_stats"][:, 2 * b + t, :], buf["xs"][:, 2 * b + t, :])


class Norm:

    def __init__(self, nc, buf, sem, tag):
        self.nc, self.buf = nc, buf
        self.stat, self.power, self.done = sem(f"{tag}_ln_stat"), sem(f"{tag}_ln_power"), sem(f"{tag}_ln_done")
        self.centred = sem(f"{tag}_ln_centred")

    def stats(self, dve, b):
        nc, buf = self.nc, self.buf
        for t in range(TPB):
            nc.vector.bn_stats(buf["stats"][:, t, :], buf["xs"][:, 2 * b + t, :]).then_inc(self.stat, 1)
        st = buf["stats"][:].rearrange("p t (o c) -> p t o c", o=2)
        dve.wait_ge(self.stat, 4 * b + 2)
        nc.vector.tensor_tensor(buf["both"][:], st[:, :, 0, 1:3], st[:, :, 1, 1:3], ALU.add).then_inc(self.stat, 1)
        nc.vector.tensor_tensor(buf["diff"][:], st[:, :, 0, 1], st[:, :, 1, 1], ALU.subtract).then_inc(self.stat, 1)

    def root(self, pool, b):
        nc, buf = self.nc, self.buf
        pool.wait_ge(self.stat, 4 * b + 4)
        nc.gpsimd.tensor_tensor(buf["sq"][:], buf["diff"][:], buf["diff"][:], ALU.mult).then_inc(self.power, 1)
        nc.gpsimd.tensor_scalar(buf["mean"][:], buf["both"][:, :, 0], 0.5, 0.0, ALU.mult, ALU.add).then_inc(self.power, 1)
        nc.gpsimd.tensor_scalar(buf["var"][:], buf["both"][:, :, 1], 1.0 / D, EPS, ALU.mult, ALU.add).then_inc(self.power, 1)
        pool.wait_ge(self.power, 6 * b + 1)
        nc.gpsimd.tensor_tensor(buf["sq"][:], buf["sq"][:], buf["quarter"][:, 0:TPB], ALU.mult).then_inc(self.power, 1)
        pool.wait_ge(self.power, 6 * b + 4)
        nc.gpsimd.tensor_tensor(buf["var"][:], buf["var"][:], buf["sq"][:], ALU.add).then_inc(self.power, 1)
        pool.wait_ge(self.power, 6 * b + 5)
        nc.gpsimd.tensor_tensor(buf["rstd"][:], buf["var"][:], buf["mhalf"][:, 0:TPB], ALU.pow).then_inc(self.power, 1)

    def scale_on_pool(self, pool, b, used):
        nc, buf = self.nc, self.buf
        if not known(b) or b > 0:
            pool.wait_ge(used, b)
        nc.gpsimd.tensor_tensor(buf["xn"][:], buf["xs"][:, ds(2 * b, 2), :],
                                buf["mean"][:, :, None].to_broadcast([P, TPB, D]), ALU.subtract).then_inc(self.centred, 1)
        pool.wait_ge(self.power, 6 * b + 6)
        pool.wait_ge(self.centred, b + 1)
        nc.gpsimd.tensor_tensor(buf["xn"][:], buf["xn"][:],
                                buf["rstd"][:, :, None].to_broadcast([P, TPB, D]), ALU.mult).then_inc(self.done, 1)

    def scale(self, dve, b, dst):
        nc, buf = self.nc, self.buf
        dve.wait_ge(self.power, 6 * b + 6)
        for t in range(TPB):
            last = nc.vector.tensor_scalar(dst(t), buf["xs"][:, 2 * b + t, :], buf["mean"][:, t:t + 1],
                                           buf["rstd"][:, t:t + 1], ALU.subtract, ALU.mult)
        last.then_inc(self.done, 1)


def load_bulk(sp, ap, buf, moe, bulk, part):
    if part == 0:
        for i in range(1, NT // 8):
            sp.dma_start(buf["xs"][:, 8 * i:8 * i + 8, :], ap["x"][:, 8 * i:8 * i + 8, :]).then_inc(bulk["x"], 16)
    if part == 1:
        sp.dma_start(moe["w1b"][:, :, 0:HID], ap["w1"]).then_inc(bulk["w"], 16)
        sp.dma_start(moe["w1b"][:, :, HID:W1W], ap["b1"]).then_inc(bulk["w"], 16)
    if part == 2:
        sp.dma_start(moe["earlier"][:], ap["earlier"]).then_inc(bulk["w"], 16)
        sp.dma_start(moe["w2s"][:], ap["w2"]).then_inc(bulk["w"], 16)
        sp.dma_start(moe["b2bc"][:], ap["b2"].to_broadcast([P, E * D])).then_inc(bulk["w"], 16)
    if part in (3, 4):
        for i in range(0, ZCHUNKS // 2) if part == 3 else range(ZCHUNKS // 2, ZCHUNKS):
            sp.dma_start(moe["xdisp"][i * ZBLK * P:(i + 1) * ZBLK * P, :].rearrange("(p r) d -> p (r d)", p=P),
                         moe["zrow"][:]).then_inc(bulk["zero"], 16)


def linear_attention(nc, ap, buf, moe, bulk, sem):
    bank, ident, xs = buf["bank"], buf["ident"], buf["xs"]
    RING, KV_BANK, AT_BANK, BT_BANK, MISC = bank[0:4], bank[4], bank[5], bank[6], bank[7]
    v_ps = AT_BANK[:, 0:TPB * D].rearrange("p (t h c) -> p t h c", t=TPB, h=H)
    back = BT_BANK[:].rearrange("p (t h c) -> p t h c", t=TPB, c=CT)
    y_ps = MISC[:, 0:TPB * D].rearrange("p (t c) -> p t c", t=TPB)
    S = lambda n: sem(f"a_{n}")
    ln = Norm(nc, buf, sem, "a")
    ld, init, v_zero, p_split, p_stored, p_zero, p_stacked = (S(n) for n in (
        "ld", "init", "v_zero", "p_split", "p_stored", "p_zero", "p_stacked"))
    xnT_ps, xnT_sb, qk_ps, qk_sb, rest_done, mid_done, lo_done = (S(n) for n in (
        "xnT_ps", "xnT_sb", "qk_ps", "qk_sb", "rest", "mid", "lo"))
    stored, stacked = [S("stored0"), S("stored1")], [S("stacked0"), S("stacked1")]
    v_done, v_sb, feat, neg_act, neg_dve, expd, phi = (S(n) for n in (
        "v_ps", "v_sb", "feature", "neg_act", "neg_dve", "exp", "phi"))
    kv_done, kvT_sb, kvb_done, kv_sb, at_done, at_sb, bt_done, an_step, an_done = (S(n) for n in (
        "kv_ps", "kvT_sb", "kvb_ps", "kv_sb", "at_ps", "at_sb", "bt_ps", "an_step", "an"))
    anT_ps, anT_sb, y_done, biased, x_added = (S(n) for n in ("anT_ps", "anT_sb", "y_ps", "biased", "x_added"))
    bounce = nc.dram_tensor("a_bounce", (2, P, 3, 2, 256), BF16).ap()
    p_bounce = nc.dram_tensor("a_proj_bounce", (P, 3, F), BF16).ap()
    with ExitStack() as c:
        def sb(name, shape, dt=F32):
            return c.enter_context(nc.sbuf_tensor("a_" + name, shape, dt))
        wqkv, wout, bout = sb("wqkv", [P, 3 * D]), sb("wout", [P, D]), sb("bout", [P, D])
        proj, p_rest, p_parts = sb("proj", [P, F]), sb("p_rest", [P, F]), sb("p_parts", [P, 3, F], BF16)
        pstk = sb("pstk", [NTERM * 16, H, F], BF16)
        qk, rest = sb("qk", [P, 2, 256]), sb("rest", [P, 2, 256])
        parts = sb("parts", [P, 3, 2, 256], BF16)
        stk = sb("stk", [NTERM * 16, 2, H // 2, 2, 256], BF16)
        v32 = sb("v32", [P, 2, TPB, H, CT])
        kvT = sb("kvT", [P, 512])
        neg, ex = sb("neg", [P, 4, 512]), sb("ex", [P, 4, 512])
        kphi, qphi = sb("kphi", [P, 8, 512]), sb("qphi", [P, 8, 512])
        kvS = sb("kvS", [P, H, CT])
        atS = sb("atS", [P, 2, 512])
        den, rec = sb("den", [P, TPB, H // 2]), sb("rec", [P, TPB, H // 2])
        an, anT = sb("an", [P, TPB, D]), sb("anT", [P, TPB * P])
        block = c.enter_context(nc.Block())

        def rounds(eng, body):
            for b in (0, 1):
                body(b, b)
            with eng.Fori(0, (NB - 6) // 2) as i:
                body(2 * i + 2, 0)
                body(2 * i + 3, 1)
            for b in range(NB - 4, NB):
                body(b, b % 2)

        def holds(b, more):
            return not known(b) or b + more < NB

        @block.sync
        def _(sp):
            sp.dma_start(proj[:], ap["proj"].rearrange("h d f -> (h d) f")).then_inc(ld, 16)
            sp.dma_start(wqkv[:], ap["wqkvT"]).then_inc(ld, 16)
            sp.dma_start(wout[:], ap["woutT"]).then_inc(ld, 16)
            sp.dma_start(bout[:], ap["b_out"].to_broadcast([P, D])).then_inc(ld, 16)
            sp.wait_ge(p_split, 4)
            sp.dma_start(p_bounce, p_parts[:]).then_inc(p_stored, 16)
            sp.wait_ge(p_stored, 16)
            sp.wait_ge(p_zero, 1)
            for t in range(NTERM):
                for q in range(2):
                    sp.dma_start(pstk[16 * t + 8 * q:16 * t + 8 * q + 8].rearrange("r (h q) f -> r h q f", q=2)[:, :, q, :],
                                 p_bounce[:, PART_B[t], :].rearrange("(h q d) f -> q d h f", q=2, d=HD)[q]).then_inc(p_stacked, 16)

            def stack(b, p, turn):
                sp.wait_ge(lo_done, b + 1)
                sp.dma_start(bounce[p], parts[:]).then_inc(stored[p], 16)
                if not known(b) or b >= 2:
                    sp.wait_ge(feat, U * (b - 1))
                sp.wait_ge(stored[p], 16 * turn)
                for t in range(NTERM):
                    sp.dma_start(stk[16 * t:16 * t + 16, p], bounce[p, :, PART_A[t]].rearrange(
                        "(h r) s n -> r h s n", r=16)).then_inc(stacked[p], 16)
            stack(0, 0, 1)
            stack(1, 1, 1)
            for part in range(5):
                load_bulk(sp, ap, buf, moe, bulk, part)
                if part < 4:
                    stack(part + 2, part % 2, part // 2 + 2)
            with sp.Fori(3, NB // 2) as i:
                stack(2 * i, 0, i + 1)
                stack(2 * i + 1, 1, i + 1)
            sp.wait_ge(bulk["w"], 80)
            sp.wait_ge(bulk["zero"], 16 * ZCHUNKS)

        @block.gpsimd
        def _(pool):
            nc.gpsimd.memset(pstk[:], 0.0).then_inc(p_zero, 1)
            nc.gpsimd.memset(v32[:, :, :, :, HD:CT], 0.0).then_inc(v_zero, 1)
            pool.wait_ge(v_zero, 1)
            nc.gpsimd.memset(v32[:, :, :, :, HD:HD + 1], 1.0).then_inc(init, 1)

            def split(b):
                pool.wait_ge(qk_sb, 2 * b + 2)
                nc.gpsimd.tensor_tensor(rest[:], qk[:], parts[:, 0], ALU.subtract).then_inc(rest_done, 1)
                pool.wait_ge(mid_done, b + 1)
                nc.gpsimd.tensor_tensor(parts[:, 2], rest[:], parts[:, 1], ALU.subtract).then_inc(lo_done, 1)

            def add_bias(b):
                pool.wait_ge(ln.done, b + 1)
                nc.gpsimd.tensor_tensor(xs[:, ds(2 * b, 2), :], xs[:, ds(2 * b, 2), :],
                                        bout[:, None, :].to_broadcast([P, TPB, D]), ALU.add).then_inc(biased, 1)

            def body(b, p):
                if holds(b, 2):
                    split(b + 2)
                add_bias(b)
                if holds(b, 3):
                    ln.root(pool, b + 3)
                    ln.scale_on_pool(pool, b + 3, xnT_ps)
            pool.wait_ge(ld, 64)
            ln.root(pool, 0)
            ln.scale_on_pool(pool, 0, xnT_ps)
            for b in range(2):
                ln.root(pool, b + 1)
                ln.scale_on_pool(pool, b + 1, xnT_ps)
                split(b)
            rounds(pool, body)

        @block.tensor
        def _(pe):
            def norm_transposes(b):
                pe.wait_ge(ln.done, b + 1)
                if not known(b) or b >= 1:
                    pe.wait_ge(qk_sb, 2 * b)
                if not known(b) or b >= 4:
                    pe.wait_ge(x_added, b - 3)
                for t in range(TPB):
                    last = nc.tensor.transpose(MISC[:, t * P:(t + 1) * P], buf["xn"][:, t, :], ident[:])
                last.then_inc(xnT_ps, 1)

            def queries_keys(b, j):
                if j == 0:
                    pe.wait_ge(xnT_sb, b + 1)
                nc.tensor.matmul(MISC[:, j * 256:(j + 1) * 256], wqkv[:, j * D:(j + 1) * D], buf["xnT"][:],
                                 start=True, stop=True).then_inc(qk_ps, 1)

            def values(b):
                if not known(b) or b >= 3:
                    pe.wait_ge(at_sb, 2 * (b - 2))
                for t in range(TPB):
                    last = nc.tensor.matmul(AT_BANK[:, t * D:(t + 1) * D], buf["xnT"][:, t * P:(t + 1) * P],
                                            wqkv[:, 2 * D:3 * D], start=True, stop=True)
                last.then_inc(v_done, 1)

            def feature(b, p, s):
                if s == 0:
                    pe.wait_ge(stacked[p], 8 * NTERM * (b - p + 2))
                if not known(b) or b > 0 or s >= 4:
                    pe.wait_ge(phi, U * b + s - 3)
                for j in range(2):
                    dst = RING[s % 4][:, j * 256:(j + 1) * 256]
                    if s < 8:
                        pair, t = 2 * (s // 2) + j, s % 2
                        last = nc.tensor.matmul(dst, stk[:, p, pair, 1, t * P:(t + 1) * P],
                                                pstk[:, 2 * pair:2 * pair + 2, :], start=True, stop=True)
                    else:
                        last = nc.tensor.matmul(dst, pstk[:, 2 * (s - 8) + j, :], stk[:, p, s - 8, 0, :],
                                                start=True, stop=True)
                last.then_inc(feat, 1)

            def key_value(b, p, g):
                pe.wait_ge(phi, U * b + 2 * g + 2)
                if g == 0:
                    pe.wait_ge(v_sb, b + 1)
                    if not known(b) or b > 0:
                        pe.wait_ge(kvT_sb, b)
                for t in range(TPB):
                    for j in range(4):
                        last = nc.tensor.matmul(KV_BANK[CT * j:CT * (j + 1), g * F:(g + 1) * F],
                                                v32[:, p, t, 4 * g + j, :], kphi[:, 2 * g + t, j * F:(j + 1) * F],
                                                start=(t == 0), stop=(t == 1))
                last.then_inc(kv_done, 1)

            def kv_transposes(b):
                pe.wait_ge(kvT_sb, b + 1)
                if not known(b) or b > 0:
                    pe.wait_ge(an_done, 2 * b)
                for g in range(4):
                    last = nc.tensor.transpose(BT_BANK[:, g * P:(g + 1) * P], kvT[:, g * F:(g + 1) * F], ident[:])
                last.then_inc(kvb_done, 1)

            def attend(b, w):
                pe.wait_ge(phi, U * b + 8 + w + 1)
                if w == 0:
                    pe.wait_ge(kv_sb, b + 1)
                    pe.wait_ge(v_sb, b + 3 if holds(b, 2) else NB)
                if w == 4:
                    pe.wait_ge(at_sb, 2 * b + 1)
                for j in range(2):
                    r, g = 2 * (w % 2) + j, (w // 2) % 2
                    last = nc.tensor.matmul(AT_BANK[CT * r:CT * (r + 1), g * 256:(g + 1) * 256], kvS[:, 2 * w + j, :],
                                            qphi[:, w, j * 256:(j + 1) * 256], start=True, stop=True)
                last.then_inc(at_done, 1)

            def back_transposes(b, half):
                pe.wait_ge(at_sb, 2 * b + half + 1)
                if half:
                    pe.wait_ge(an_done, 2 * b + 1)
                for t in range(TPB):
                    for g in range(2):
                        last = nc.tensor.transpose(BT_BANK[:, (2 * t + g) * P:(2 * t + g + 1) * P],
                                                   atS[:, half, g * 256 + t * P:g * 256 + (t + 1) * P], ident[:])
                last.then_inc(bt_done, 1)

            def an_transposes(b):
                pe.wait_ge(an_done, 2 * b + 2)
                pe.wait_ge(qk_sb, 2 * (b + 4) if holds(b, 3) else 2 * NB)
                for t in range(TPB):
                    last = nc.tensor.transpose(MISC[:, t * P:(t + 1) * P], an[:, t, :], ident[:])
                last.then_inc(anT_ps, 1)

            def project(b):
                pe.wait_ge(anT_sb, b + 1)
                for t in range(TPB):
                    last = nc.tensor.matmul(y_ps[:, t, :], anT[:, t * P:(t + 1) * P], wout[:], start=True, stop=True)
                last.then_inc(y_done, 1)

            def body(b, p):
                before = not known(b) or b > 0
                for s in range(U):
                    feature(b, p, s)
                    if s < 3 and before:
                        attend(b - 1, s + 1)
                    if s == 0 and holds(b, 2):
                        norm_transposes(b + 2)
                    if s in (2, 3) and holds(b, 2):
                        queries_keys(b + 2, s - 2)
                    if s == 5 and before:
                        back_transposes(b - 1, 0)
                    if 4 <= s <= 7 and before:
                        attend(b - 1, s)
                    if s in (5, 7, 9, 11):
                        key_value(b, p, (s - 5) // 2)
                    if s == 8 and before:
                        back_transposes(b - 1, 1)
                    if s == 11 and before:
                        an_transposes(b - 1)
                    if s == 12 and holds(b, 2):
                        values(b + 2)
                    if s == 13:
                        if before:
                            project(b - 1)
                        kv_transposes(b)
                    if s == 15:
                        attend(b, 0)

            pe.wait_ge(ld, 64)
            pe.wait_ge(init, 1)
            for b in range(2):
                norm_transposes(b)
                queries_keys(b, 0)
                queries_keys(b, 1)
                if b:
                    pe.wait_ge(v_sb, b)
                values(b)
            pe.wait_ge(p_stacked, 16 * 2 * NTERM)
            rounds(pe, body)
            b = NB - 1
            for w in range(1, 4):
                attend(b, w)
            back_transposes(b, 0)
            for w in range(4, 8):
                attend(b, w)
            back_transposes(b, 1)
            an_transposes(b)
            project(b)

        @block.scalar
        def _(act):
            def copy_xnT(b):
                act.wait_ge(xnT_ps, b + 1)
                if not known(b) or b >= 1:
                    act.wait_ge(v_done, b)
                nc.scalar.copy(buf["xnT"][:], MISC[:, 0:256]).then_inc(xnT_sb, 1)

            def copy_qk(b, p):
                act.wait_ge(qk_ps, 2 * b + 2)
                if not known(b) or b > 0:
                    act.wait_ge(lo_done, b)
                nc.scalar.copy(qk[:], MISC[:].rearrange("p (s n) -> p s n", s=2)).then_inc(qk_sb, 1)

            def high(b, p):
                if not known(b) or b > 0:
                    act.wait_ge(stored[1 - p], 8 * (b + p))
                nc.scalar.copy(parts[:, 0], MISC[:].rearrange("p (s n) -> p s n", s=2)).then_inc(qk_sb, 1)

            def middle(b):
                act.wait_ge(rest_done, b + 1)
                nc.scalar.copy(parts[:, 1], rest[:]).then_inc(mid_done, 1)

            def copy_v(b, p):
                act.wait_ge(v_done, b + 1)
                if not known(b) or b >= 2:
                    act.wait_ge(kv_done, 4 * (b - 1))
                nc.scalar.copy(v32[:, p, :, :, 0:HD], v_ps).then_inc(v_sb, 1)

            def copy_kvT(b):
                act.wait_ge(kv_done, 4 * b + 4)
                nc.scalar.copy(kvT[:], KV_BANK[:]).then_inc(kvT_sb, 1)

            def copy_at(b, half):
                act.wait_ge(at_done, 8 * b + 4 * half + 4)
                nc.scalar.copy(atS[:, half, :], AT_BANK[:]).then_inc(at_sb, 1)

            def copy_anT(b):
                act.wait_ge(anT_ps, b + 1)
                nc.scalar.copy(anT[:], MISC[:, 0:256]).then_inc(anT_sb, 1)

            def negative(b, s):
                act.wait_ge(feat, U * b + s + 1)
                nc.scalar.activation(neg[:, s % 4, :], RING[s % 4][:], ACT.Relu, scale=-1.0).then_inc(neg_act, 1)

            def exponential(b, s):
                if s % 2 == 0 or s == 9:
                    act.wait_ge(neg_act, (U // 2 + 1) * b + s // 2 + (2 if s >= 9 else 1))
                else:
                    act.wait_ge(neg_dve, (U // 2 - 1) * b + s // 2 + (0 if s > 9 else 1))
                nc.scalar.activation(ex[:, s % 4, :], neg[:, s % 4, :], ACT.Exp,
                                     scale=-1.0 if s % 2 == 0 or s == 9 else 1.0).then_inc(expd, 1)

            def body(b, p):
                before = not known(b) or b > 0
                for s in range(U):
                    if s % 2 == 0 or s == 9:
                        negative(b, s)
                    if s > 0:
                        exponential(b, s - 1)
                    elif before:
                        exponential(b - 1, U - 1)
                    if s == 1 and holds(b, 2):
                        copy_xnT(b + 2)
                    if s == 3 and before:
                        copy_at(b - 1, 0)
                    if s == 4 and holds(b, 2):
                        copy_qk(b + 2, p)
                    if s == 5 and holds(b, 2):
                        high(b + 2, p)
                    if s == 7 and before:
                        copy_at(b - 1, 1)
                    if s == 7 and holds(b, 2):
                        middle(b + 2)
                    if s == 11 and before:
                        copy_anT(b - 1)
                    if s == 12:
                        copy_kvT(b)
                    if s == 13 and holds(b, 2):
                        copy_v(b + 2, p)

            act.wait_ge(init, 1)
            act.wait_ge(ld, 64)
            nc.scalar.copy(p_parts[:, 0], proj[:]).then_inc(p_split, 1)
            act.wait_ge(p_split, 2)
            nc.scalar.copy(p_parts[:, 1], p_rest[:]).then_inc(p_split, 1)
            for b in range(2):
                copy_xnT(b)
                copy_qk(b, b)
                high(b, b)
                middle(b)
                copy_v(b, b)
            rounds(act, body)
            b = NB - 1
            exponential(b, U - 1)
            copy_at(b, 0)
            copy_at(b, 1)
            copy_anT(b)

        @block.vector
        def _(dve):
            def negative(b, s):
                dve.wait_ge(feat, U * b + s + 1)
                nc.vector.tensor_scalar_min(neg[:, s % 4, :], RING[s % 4][:], 0.0).then_inc(neg_dve, 1)

            def features(b, s):
                dve.wait_ge(expd, U * b + s + 1)
                if s < 8:
                    if not known(b) or b > 0:
                        dve.wait_ge(kv_done, 4 * b - 4 + s // 2 + 1)
                    dst = kphi[:, s, :]
                else:
                    w = s - 8
                    if not known(b) or b > 0:
                        dve.wait_ge(at_done, 8 * b + w - 7)
                    dst = qphi[:, w, :]
                nc.vector.scalar_tensor_tensor(dst, RING[s % 4][:], 0.0, ex[:, s % 4, :], ALU.max,
                                               ALU.add).then_inc(phi, 1)

            def copy_kv(b):
                dve.wait_ge(kvb_done, b + 1)
                nc.vector.tensor_copy(kvS[:], BT_BANK[:].rearrange("p (h c) -> p h c", c=CT)).then_inc(kv_sb, 1)

            def normalise(b, half):
                n = 2 * b + half
                dve.wait_ge(bt_done, n + 1)
                nc.vector.tensor_scalar(den[:], back[:, :, :, HD], 1e-8, None, ALU.add).then_inc(an_step, 1)
                dve.wait_ge(an_step, 2 * n + 1)
                nc.vector.reciprocal(rec[:], den[:]).then_inc(an_step, 1)
                dve.wait_ge(an_step, 2 * n + 2)
                for t in range(TPB):
                    dst = an[:, t, half * (D // 2):(half + 1) * (D // 2)].rearrange("p (h c) -> p h c", c=HD)
                    last = nc.vector.tensor_tensor(dst, back[:, t, :, 0:HD],
                                                   rec[:, t, :, None].to_broadcast([P, H // 2, HD]), ALU.mult)
                last.then_inc(an_done, 1)

            def add(b):
                dve.wait_ge(y_done, b + 1)
                dve.wait_ge(biased, b + 1)
                nc.vector.tensor_tensor(xs[:, ds(2 * b, 2), :], y_ps, xs[:, ds(2 * b, 2), :],
                                        ALU.add).then_inc(x_added, 1)

            def body(b, p):
                before = not known(b) or b > 0
                for s in range(U):
                    if s % 2 and s != 9:
                        negative(b, s)
                    if s >= 2:
                        features(b, s - 2)
                    elif before:
                        features(b - 1, U - 2 + s)
                    if s == 6 and before:
                        normalise(b - 1, 0)
                    if s == 7 and known(b) and b == 1:
                        dve.wait_ge(bulk["x"], 16 * (NT // 8 - 1))
                    if s == 7 and holds(b, 3):
                        dve.wait_ge(ln.power, 6 * b + 18)
                        ln.stats(dve, b + 3)
                    if s == 9 and before:
                        normalise(b - 1, 1)
                    if s == 13:
                        copy_kv(b)
                    if s == 15 and (not known(b) or b >= 2):
                        dve.wait_ge(x_added, b - 1)
                        stats_for_experts(nc, buf, b - 2)
                    if s == 13 and before:
                        add(b - 1)

            dve.wait_ge(bulk["x0"], 16)
            ln.stats(dve, 0)
            dve.wait_ge(ld, 64)
            dve.wait_ge(init, 1)
            dve.wait_ge(p_split, 1)
            nc.vector.tensor_tensor(p_rest[:], proj[:], p_parts[:, 0], ALU.subtract).then_inc(p_split, 1)
            dve.wait_ge(p_split, 3)
            nc.vector.tensor_tensor(p_parts[:, 2], p_rest[:], p_parts[:, 1], ALU.subtract).then_inc(p_split, 1)
            for b in (1, 2):
                dve.wait_ge(ln.power, 6 * b)
                ln.stats(dve, b)
            rounds(dve, body)
            b = NB - 1
            features(b, U - 2)
            features(b, U - 1)
            normalise(b, 0)
            normalise(b, 1)
            add(b)
            dve.wait_ge(x_added, NB)
            for b in (NB - 2, NB - 1):
                stats_for_experts(nc, buf, b)


def fetch_rows(pool, buf, moe, tile, done):
    rows = moe["ydisp"][0:(tile // HT + 1) * HBLK * P, :]
    pool.indirect_dma_start(buf["xn_all"][:, tile, :], None, rows,
                            bass.IndirectOffsetOnAxis(ap=moe["posi"][:, tile:tile + 1], axis=0)).then_inc(done, 16)


def add_rows(nc, buf, moe, tile):
    xs = buf["xs"][:, tile, :]
    return nc.vector.scalar_tensor_tensor(xs, buf["xn_all"][:, tile, :], moe["sc"][:, tile:tile + 1], xs, ALU.mult, ALU.add)


def expert_layer(nc, ap, buf, moe, sem, tag, const=None, out=None):
    back = NT if out is not None else HT
    bank, ident, xs, xn_all = buf["bank"], buf["ident"], buf["xs"], buf["xn_all"]
    S = lambda n: sem(f"{tag}_{n}")
    stat, power, normed = S("ln_stat"), S("ln_power"), S("normed")
    xnT_ps, xnT_sb, kept, lg_ps = S("xnT_ps"), S("xnT_sb"), S("kept"), S("logit_ps")
    step, expd, rank_ps, routed = S("step"), S("exp"), S("rank_ps"), S("routed")
    pld, onehot, shifted, mapped = S("ld_pos"), S("onehot"), S("shifted"), S("mapped")
    scat = [S(f"scatter{i}") for i in range(2)]
    wl, xl, st = [S(f"ld_w{p}") for p in range(4)], [S(f"ld_x{p}") for p in range(4)], [S(f"st_y{p}") for p in range(4)]
    gat = [S(f"gather{i}") for i in range(8)]
    xT_ps, xT_sb, h_ps, h_sb, y_ps_done, y_sb = (S(n) for n in ("xT_ps", "xT_sb", "h_ps", "h_sb", "y_ps", "y_sb"))
    x_added, out_st, const_ld = S("x_added"), S("store_out"), S("ld_next")
    with ExitStack() as c:
        def sb(name, shape, dt=F32):
            return c.enter_context(nc.sbuf_tensor(f"{tag}_{name}", shape, dt))
        stats, both = buf["next_stats"], sb("both", [P, NT, 2])
        diff, sq, mean, var, rstd = (sb(n, [P, NT]) for n in ("diff", "sq", "mean", "var", "rstd"))
        xg, xgT = sb("xg", [P, 2, GT, D]), sb("xgT", [P, 2, GT * P])
        oh, t1, t2, t3 = (sb(n, [P, HT, E]) for n in ("oh", "t1", "t2", "t3"))
        m, pos = sb("m", [P, HT]), sb("pos", [P, HT])
        sc, posi = moe["sc"], moe["posi"]
        off, nbi = sb("off", [P, 2, E + 1]), sb("nbi", [P, E], I32)
        cnt, eb, cmp8 = sb("cnt", [P, HBLK]), sb("eb", [P, NBLK], I32), sb("cmp8", [P, HBLK, E])
        prio, start = sb("prio", [P, E]), sb("start", [P, NBLK])
        wc = sb("wc", [P, 4, W1W])
        xb, xT, hT, yb = sb("xb", [P, 4, D]), sb("xT", [P, 4, P]), sb("hT", [P, 4, HC * P]), sb("yb", [P, 4, D])
        LG_BANK = (bank[6], bank[7])
        TR_BANK = (bank[4], bank[5])
        block = c.enter_context(nc.Block())

        PAIRS = HT // GT // 2
        POWERS = 5 + PAIRS

        def groups(eng, body, half):
            if half == 0:
                body(0, 0)
                body(1, 1)
            with eng.Fori(1 if half == 0 else PAIRS, PAIRS * (half + 1)) as i:
                body(2 * i, 0)
                body(2 * i + 1, 1)

        def tiles(half):
            return slice(half * HT, (half + 1) * HT)

        @block.vector
        def _(dve):
            def norm_stats(half):
                st4 = stats[:, tiles(half), :].rearrange("p t (o c) -> p t o c", o=2)
                nc.vector.tensor_tensor(both[:, tiles(half)], st4[:, :, 0, 1:3], st4[:, :, 1, 1:3], ALU.add).then_inc(stat, 1)
                nc.vector.tensor_tensor(diff[:, tiles(half)], st4[:, :, 0, 1], st4[:, :, 1, 1], ALU.subtract).then_inc(stat, 1)

            def normalise(half):
                def group(g, p):
                    if p == 0:
                        dve.wait_ge(power, 5 * (half + 1) + g // 2 + 1)
                    if not known(g) or g >= 2:
                        dve.wait_ge(xnT_ps, g - 1)
                        dve.wait_ge(kept, g - 1)
                    for t in range(GT):
                        last = nc.vector.tensor_scalar(
                            xg[:, p, t, :], xs[:, ds(g * GT + t, 1), :].rearrange("p o c -> p (o c)"),
                            mean[:, ds(g * GT + t, 1)], rstd[:, ds(g * GT + t, 1)], ALU.subtract, ALU.mult)
                    last.then_inc(normed, 1)
                groups(dve, group, half)

            n = [0]

            def then(ins):
                n[0] += 1
                ins.then_inc(step, 1)
                dve.wait_ge(step, n[0])

            def over_e(a):
                return a[:, :, None].to_broadcast([P, HT, E])

            def route(half):
                logits = LG_BANK[half][:, 0:HT * E].rearrange("p (t e) -> p t e", e=E)
                score, blocks = sc[:, tiles(half)], slice(half * HBLK, (half + 1) * HBLK)
                dve.wait_ge(lg_ps, HT // GT * (half + 1))
                then(nc.vector.reduce_max(m[:], logits, AX))
                nc.vector.tensor_tensor(t1[:], logits, over_e(m), ALU.subtract).then_inc(shifted, 1)
                dve.wait_ge(shifted, 2 * half + 1)
                nc.vector.tensor_scalar(t2[:], t1[:], 0.0, None, ALU.is_equal).then_inc(shifted, 1)
                dve.wait_ge(shifted, 2 * half + 2)
                then(nc.vector.tensor_tensor(t2[:], t2[:], prio[:, None, :].to_broadcast([P, HT, E]), ALU.mult))
                then(nc.vector.reduce_max(m[:], t2[:], AX))
                nc.vector.tensor_tensor(oh[:], t2[:], over_e(m), ALU.is_equal).then_inc(onehot, 1)
                dve.wait_ge(expd, half + 1)
                then(nc.vector.reduce_sum(score, t1[:], AX))
                then(nc.vector.reciprocal(score, score))
                dve.wait_ge(rank_ps, half + 1)
                then(nc.vector.tensor_copy(t3[:], bank[3][:, 0:HT * E].rearrange("p (t e) -> p t e", e=E)))
                a, z = t3, t2
                k = 1
                while k < HT:
                    nc.vector.tensor_copy(z[:, 0:k, :], a[:, 0:k, :])
                    then(nc.vector.tensor_tensor(z[:, k:HT, :], a[:, k:HT, :], a[:, 0:HT - k, :], ALU.add))
                    a, z = z, a
                    k *= 2
                then(nc.vector.tensor_scalar(nbi[:], a[:, HT - 1, :], float(P - 1), None, ALU.add))
                then(nc.vector.tensor_single_scalar(nbi[:], nbi[:], -P, ALU.bitwise_and))
                nc.vector.memset(off[:, 0, 0:1], float(half * HBLK * P))
                nc.vector.memset(off[:, 1, 0:1], float(half * HBLK * P))
                then(nc.vector.tensor_copy(off[:, 0, 1:E + 1], nbi[:]))
                o, k = 0, 1
                while k < E + 1:
                    if k > 1:
                        nc.vector.tensor_copy(off[:, 1 - o, 1:k], off[:, o, 1:k])
                    then(nc.vector.tensor_tensor(off[:, 1 - o, k:E + 1], off[:, o, k:E + 1], off[:, o, 0:E + 1 - k], ALU.add))
                    o, k = 1 - o, 2 * k
                then(nc.vector.tensor_tensor(a[:], a[:], bank[2][:, 0:HT * E].rearrange("p (t e) -> p t e", e=E), ALU.add))
                then(nc.vector.tensor_tensor(a[:], a[:], off[:, o, None, 0:E].to_broadcast([P, HT, E]), ALU.add))
                then(nc.vector.tensor_tensor(a[:], a[:], oh[:], ALU.mult))
                then(nc.vector.reduce_sum(pos[:], a[:], AX))
                nc.vector.tensor_copy(posi[:, tiles(half)], pos[:]).then_inc(routed, 1)
                then(nc.vector.tensor_tensor(cmp8[:], off[:, o, None, 1:E + 1].to_broadcast([P, HBLK, E]),
                                             start[:, blocks, None].to_broadcast([P, HBLK, E]), ALU.is_le))
                then(nc.vector.reduce_sum(cnt[:], cmp8[:], AX))
                nc.vector.tensor_scalar(eb[:, blocks], cnt[:], float(E - 1), None, ALU.min).then_inc(mapped, 1)

            norm_stats(0)
            norm_stats(1)
            normalise(0)
            dve.wait_ge(pld, 32)
            route(0)
            normalise(1)
            route(1)

        @block.gpsimd
        def _(pool):
            for half in range(2):
                r = tiles(half)
                pool.wait_ge(stat, 2 * (half + 1))
                nc.gpsimd.tensor_tensor(sq[:, r], diff[:, r], diff[:, r], ALU.mult).then_inc(power, 1)
                nc.gpsimd.tensor_scalar(mean[:, r], both[:, r, 0], 0.5, 0.0, ALU.mult, ALU.add).then_inc(power, 1)
                nc.gpsimd.tensor_scalar(var[:, r], both[:, r, 1], 1.0 / D, EPS, ALU.mult, ALU.add).then_inc(power, 1)
                pool.wait_ge(power, POWERS * half + 1)
                nc.gpsimd.tensor_tensor(sq[:, r], sq[:, r], buf["quarter"][:, 0:HT], ALU.mult).then_inc(power, 1)
                pool.wait_ge(power, POWERS * half + 4)
                nc.gpsimd.tensor_tensor(var[:, r], var[:, r], sq[:, r], ALU.add).then_inc(power, 1)
                pool.wait_ge(power, POWERS * half + 5)
                for i in range(PAIRS):
                    part = slice(half * HT + 2 * GT * i, half * HT + 2 * GT * (i + 1))
                    nc.gpsimd.tensor_tensor(rstd[:, part], var[:, part], buf["mhalf"][:, 0:2 * GT], ALU.pow).then_inc(power, 1)
            for half in range(2):
                pool.wait_ge(routed, half + 1)
                pool.wait_ge(kept, HT // GT * (half + 1))
                for i in range(half * HT, (half + 1) * HT):
                    pool.indirect_dma_start(moe["xdisp"], bass.IndirectOffsetOnAxis(ap=posi[:, i:i + 1], axis=0),
                                            xn_all[:, i, :], None).then_inc(scat[half], 16)

        @block.tensor
        def _(pe):
            def transposes(g, p):
                pe.wait_ge(normed, g + 1)
                if not known(g) or g >= 2:
                    pe.wait_ge(xnT_sb, g - 1)
                for t in range(GT):
                    last = nc.tensor.transpose(TR_BANK[p][:, t * P:(t + 1) * P], xg[:, p, t, :], ident[:])
                last.then_inc(xnT_ps, 1)

            def route(half):
                def logits(g, p):
                    pe.wait_ge(xnT_sb, g + 1)
                    for t in range(GT):
                        tile = (g - half * HT // GT) * GT + t
                        last = nc.tensor.matmul(LG_BANK[half][:, ds(tile * E, E)], xgT[:, p, t * P:(t + 1) * P],
                                                moe["G"][:], start=True, stop=True)
                    last.then_inc(lg_ps, 1)

                def group(g, p):
                    if not known(g):
                        transposes(g, p)
                        logits(g - 1, 1 - p)
                    elif g == 0:
                        transposes(0, 0)
                    else:
                        transposes(1, 1)
                        logits(0, 0)
                if half == 0:
                    groups(pe, group, 0)
                else:
                    transposes(HT // GT, 0)
                    transposes(HT // GT + 1, 1)
                    logits(HT // GT, 0)
                    with pe.Fori(HT // GT // 2 + 1, HT // GT) as i:
                        group(2 * i, 0)
                        group(2 * i + 1, 1)
                logits(HT // GT * (half + 1) - 1, 1)
                pe.wait_ge(onehot, half + 1)
                ohf = oh[:].rearrange("p t e -> p (t e)")
                nc.tensor.matmul(bank[2][:, 0:HT * E], moe["earlier"][:], ohf, start=True, stop=True)
                nc.tensor.matmul(bank[3][:, 0:HT * E], moe["ones"][:], ohf, start=True, stop=True).then_inc(rank_ps, 1)

            route(0)
            route(1)

        @block.scalar
        def _(act):
            def group(g, p):
                act.wait_ge(xnT_ps, g + 1)
                if not known(g) or g >= 2:
                    act.wait_ge(lg_ps, g - 1)
                nc.scalar.copy(xgT[:, p, :], TR_BANK[p][:]).then_inc(xnT_sb, 1)
                nc.scalar.copy(xn_all[:, ds(g * GT, GT), :], xg[:, p]).then_inc(kept, 1)

            for half in range(2):
                groups(act, group, half)
                act.wait_ge(shifted, 2 * half + 2)
                nc.scalar.activation(t1[:], t1[:], ACT.Exp).then_inc(expd, 1)

        NS, LAG = 4, 6

        def quads(eng, body, between=None):
            for j in range(2 * NS):
                body(j, j % NS)
            end = NBLK // NS - 1
            cuts = (2, HBLK // NS, end) if between else (2, end)
            for lo, hi in zip(cuts, cuts[1:]):
                with eng.Fori(lo, hi) as i:
                    for p in range(NS):
                        body(NS * i + p, p)
                if between and hi == HBLK // NS:
                    between()
            for j in range(end * NS, NBLK):
                body(j, j % NS)

        def early(j, n):
            return known(j) and j < n

        def slot_count(j, p):
            return 16 * (j // NS + 1) if known(j) else (j - p + NS) * (16 // NS)

        def stored_rows(p, blocks):
            return 16 * ((blocks - p + NS - 1) // NS)

        @block.sync
        def _(sp):
            def load(j, p):
                if not early(j, NS):
                    sp.wait_ge(xT_ps, j - NS + 1)
                sp.dma_start(xb[:, p, :], moe["xdisp"][ds(j * P, P), :]).then_inc(xl[p], 16)

            def store(j, p):
                sp.wait_ge(y_sb, j + 1)
                sp.dma_start(moe["ydisp"][ds(j * P, P), :], yb[:, p, :]).then_inc(st[p], 16)

            def body(j, p):
                load(j, p)
                if not early(j, LAG):
                    store(j - LAG, (p - LAG) % NS)

            sp.dma_start(prio[:], ap["prio"].to_broadcast([P, E])).then_inc(pld, 16)
            sp.dma_start(start[:], ap["start"].to_broadcast([P, NBLK])).then_inc(pld, 16)
            for name, dst in (const or {}).items():
                sp.dma_start(dst[:], ap[name]).then_inc(const_ld, 16)
            sp.wait_ge(scat[0], 16 * HT)
            quads(sp, body, lambda: sp.wait_ge(scat[1], 16 * HT))
            for j in range(NBLK - LAG, NBLK):
                store(j, j % NS)
            for p in range(NS):
                sp.wait_ge(st[p], stored_rows(p, NBLK))
            if const:
                sp.wait_ge(const_ld, 16 * len(const))
            if out is not None:
                for i in range(NT // 8):
                    sp.wait_ge(x_added, 8 * (i + 1))
                    sp.dma_start(out[:, 8 * i:8 * i + 8, :], xs[:, 8 * i:8 * i + 8, :]).then_inc(out_st, 16)
                sp.wait_ge(out_st, 16 * NT // 8)

        @block.tensor
        def _(pe):
            def rows_transpose(j, p):
                pe.wait_ge(xl[p], slot_count(j, p))
                if not early(j, 2):
                    pe.wait_ge(xT_sb, j - 1)
                nc.tensor.transpose(bank[p % 2][:, 0:P], xb[:, p, :], ident[:]).then_inc(xT_ps, 1)

            def hidden(j, p):
                pe.wait_ge(xT_sb, j + 1)
                pe.wait_ge(wl[p], slot_count(j, p))
                if not early(j, 2):
                    pe.wait_ge(h_sb, HC * (j - 1))
                for k in range(HC):
                    last = nc.tensor.matmul(bank[2 + p % 2][:, k * P:(k + 1) * P], wc[:, p, k * P:(k + 1) * P],
                                            xT[:, p, :], start=True, stop=True)
                last.then_inc(h_ps, 1)

            def result(j, p):
                e = pe.value_load(eb[0:1, ds(j, 1)], min_val=0, max_val=E - 1)
                pe.wait_ge(h_sb, HC * (j + 1))
                if not early(j, 2):
                    pe.wait_ge(y_sb, j - 1)
                for k in range(HC):
                    last = nc.tensor.matmul(bank[4 + p % 2][:, None, 0:D], hT[:, p, k * P:(k + 1) * P],
                                            moe["w2s"][:, ds(e * HC + k, 1), :], start=(k == 0), stop=(k == HC - 1))
                last.then_inc(y_ps_done, 1)

            def body(j, p):
                if not known(j) or j + 1 < NBLK:
                    rows_transpose(j + 1, (p + 1) % NS)
                hidden(j, p)
                if not early(j, 2):
                    result(j - 2, (p - 2) % NS)

            pe.wait_ge(mapped, 2)
            rows_transpose(0, 0)
            quads(pe, body)
            for j in (NBLK - 2, NBLK - 1):
                result(j, j % NS)

        @block.scalar
        def _(act):
            def gelu(j, p):
                act.wait_ge(h_ps, j + 1)
                if not early(j, NS):
                    act.wait_ge(y_ps_done, j - NS + 1)
                for k in range(HC):
                    nc.scalar.activation(hT[:, p, k * P:(k + 1) * P], bank[2 + p % 2][:, k * P:(k + 1) * P],
                                         ACT.Gelu, bias=wc[:, p, HID + k:HID + k + 1]).then_inc(h_sb, 1)

            def load_weights(j, p):
                e = act.value_load(eb[0:1, ds(j, 1)], min_val=0, max_val=E - 1)
                if not early(j, NS):
                    act.wait_ge(h_sb, HC * (j - NS + 1))
                act.dma_start(wc[:, p, None, :], moe["w1b"][:, ds(e, 1), :]).then_inc(wl[p], 16)

            def body(j, p):
                gelu(j, p)
                if not known(j) or j + NS - 1 < NBLK:
                    load_weights(j + NS - 1, (p + NS - 1) % NS)

            act.wait_ge(mapped, 2)
            for j in range(NS - 1):
                load_weights(j, j)
            quads(act, body)

        @block.vector
        def _(dve):
            def copy_xT(j, p):
                dve.wait_ge(xT_ps, j + 1)
                if not early(j, NS):
                    dve.wait_ge(h_ps, j - NS + 1)
                nc.vector.tensor_copy(xT[:, p, :], bank[p % 2][:, 0:P]).then_inc(xT_sb, 1)

            def copy_y(j, p):
                e = dve.value_load(eb[0:1, ds(j, 1)], min_val=0, max_val=E - 1)
                dve.wait_ge(y_ps_done, j + 1)
                if not early(j, NS):
                    dve.wait_ge(st[p], slot_count(j, p) - 16)
                nc.vector.tensor_tensor(yb[:, p, :], bank[4 + p % 2][:, 0:D], moe["b2bc"][:, ds(e * D, D)],
                                        ALU.add).then_inc(y_sb, 1)

            def body(j, p):
                if not known(j) or j + 1 < NBLK:
                    copy_xT(j + 1, (p + 1) % NS)
                if not early(j, 2):
                    copy_y(j - 2, (p - 2) % NS)

            dve.wait_ge(mapped, 2)
            copy_xT(0, 0)
            quads(dve, body)
            for j in (NBLK - 2, NBLK - 1):
                copy_y(j, j % NS)

        @block.gpsimd
        def _(pool):
            for half in range(back // HT):
                for p in range(NS):
                    pool.wait_ge(st[p], stored_rows(p, HBLK * (half + 1)))
                for i in range(half * HT, (half + 1) * HT):
                    fetch_rows(pool, buf, moe, i, gat[i // 8])

        @block.vector
        def _(dve):
            for i in range(back):
                if i % 8 == 0:
                    dve.wait_ge(gat[i // 8], 128)
                add_rows(nc, buf, moe, i).then_inc(x_added, 1)


def retention(nc, ap, buf, moe, const, sem):
    bank, ident, xs = buf["bank"], buf["ident"], buf["xs"]
    T_BANK, Q_BANK, K_BANK, VG_BANK = bank[0], bank[1], bank[2], bank[3]
    S_BANK, O_BANK = bank[4:6], bank[6:8]
    S = lambda n: sem(f"r_{n}")
    ln = Norm(nc, buf, sem, "r")
    init = S("init")
    fetched = [S(f"fetched{i}") for i in range(4)]
    xnT_ps, xnT_sb, q_ps, k_ps, v_ps, g_ps, v_sb, g_sb = (S(n) for n in (
        "xnT_ps", "xnT_sb", "q_ps", "k_ps", "v_ps", "g_ps", "v_sb", "g_sb"))
    turned, rotated, hi_done, rest_done, mid_done, lo_done = (S(n) for n in (
        "turned", "rotated", "hi", "rest", "mid", "lo"))
    stored, stacked = [S("stored0"), S("stored1")], [S("stacked0"), S("stacked1")]
    oT_sb, o_back, o_sb = S("oT_sb"), S("o_back"), S("o_sb")
    s_ps, s_sb, o_ps, squared, o_step, root, scaled, gated = (S(n) for n in (
        "s_ps", "s_sb", "o_ps", "squared", "o_step", "root", "scaled", "gated"))
    gT_ps, gT_sb, y_ps, x_added = (S(n) for n in ("gT_ps", "gT_sb", "y_ps", "x_added"))
    bounce = nc.dram_tensor("r_bounce", (2, P, 3, 2, 256), BF16).ap()
    with ExitStack() as c:
        def sb(name, shape, dt=F32):
            return c.enter_context(nc.sbuf_tensor("r_" + name, shape, dt))
        w4, wv, wg, wo, tab, mask = (const[n] for n in ("w4", "wv", "wgate", "wo", "tab", "mask"))
        xnT = sb("xnT", [P, 2, 256])
        r1, r2 = sb("r1", [P, 2, 256]), sb("r2", [P, 2, 256])
        qk, rest = sb("qk", [P, 2, 256]), sb("rest", [P, 2, 256])
        parts = sb("parts", [P, 3, 2, 256], BF16)
        stk = sb("stk", [NTERM * KD, 2, 2, RH, 256], BF16)
        v64, gate = sb("v64", [P, 2, TPB, RH, RW]), sb("gate", [P, 2, TPB, VD])
        sT = sb("sT", [P, RH, SC])
        oTs, osb = sb("oTs", [P, 2, 512]), sb("osb", [P, TPB, RH, RW])
        osq, dn, ms, fac = sb("osq", [P, TPB, RH, RHD]), sb("dn", [P, 16]), sb("ms", [P, 16]), sb("fac", [P, TPB, RH])
        oh, on, onT = sb("oh", [P, TPB, RH, RHD]), sb("on", [P, TPB, VD]), sb("onT", [P, 4 * P])
        block = c.enter_context(nc.Block())

        FETCH_ROUNDS = 6

        def rounds(eng, body):
            for b in range(FETCH_ROUNDS):
                body(b, b % 2)
            with eng.Fori(FETCH_ROUNDS // 2, NB // 2 - 2) as i:
                body(2 * i, 0)
                body(2 * i + 1, 1)
            for b in range(NB - 4, NB):
                body(b, b % 2)

        @block.sync
        def _(sp):
            def stack(b, p, turn):
                sp.wait_ge(lo_done, b + 1)
                sp.dma_start(bounce[p], parts[:]).then_inc(stored[p], 16)
                if not known(b) or b >= 2:
                    sp.wait_ge(s_ps, RH * (b - 1))
                sp.wait_ge(stored[p], 16 * turn)
                for t in range(NTERM):
                    for side, part in ((0, PART_A[t]), (1, PART_B[t])):
                        sp.dma_start(stk[KD * t:KD * (t + 1), p, side, :, :],
                                     bounce[p, :, part, side, :].rearrange("(h d) n -> d h n", d=KD)).then_inc(stacked[p], 16)
            stack(0, 0, 1)
            stack(1, 1, 1)
            with sp.Fori(0, NB // 2 - 1) as i:
                stack(2 * i + 2, 0, i + 2)
                stack(2 * i + 3, 1, i + 2)

        @block.gpsimd
        def _(pool):
            nc.gpsimd.memset(v64[:, :, :, :, RHD:RHD + 1], 1.0).then_inc(init, 1)
            nc.gpsimd.memset(v64[:, :, :, :, RHD + 1:RW], 0.0).then_inc(init, 1)

            def split(b):
                pool.wait_ge(hi_done, b + 1)
                nc.gpsimd.tensor_tensor(rest[:], qk[:], parts[:, 0], ALU.subtract).then_inc(rest_done, 1)
                pool.wait_ge(mid_done, b + 1)
                nc.gpsimd.tensor_tensor(parts[:, 2], rest[:], parts[:, 1], ALU.subtract).then_inc(lo_done, 1)

            def head_root(b):
                pool.wait_ge(o_step, 6 * b + 6)
                nc.gpsimd.tensor_tensor(fac[:].rearrange("p t h -> p (t h)"), ms[:], buf["mhalf"][:, 0:TPB * RH],
                                        ALU.pow).then_inc(root, 1)

            def body(b, p):
                if not known(b) or b > 0:
                    head_root(b - 1)
                if not known(b) or b + 2 < NB:
                    split(b + 2)
                if not known(b) or b + 3 < NB:
                    ln.root(pool, b + 3)
                if known(b) and b < FETCH_ROUNDS:
                    fetch(8 + 4 * b, 4)

            def fetch(first, count):
                for i in range(first, first + count):
                    fetch_rows(pool, buf, moe, HT + i, fetched[i // 8])

            ln.root(pool, 0)
            for b in range(2):
                ln.root(pool, b + 1)
                split(b)
            fetch(0, 8)
            rounds(pool, body)
            head_root(NB - 1)

        @block.tensor
        def _(pe):
            def norm_transposes(b, p):
                pe.wait_ge(ln.done, b + 1)
                if not known(b) or b >= 4:
                    pe.wait_ge(gT_sb, b - 3)
                if not known(b) or b >= 1:
                    pe.wait_ge(xnT_sb, b)
                for t in range(TPB):
                    last = nc.tensor.transpose(T_BANK[:, t * P:(t + 1) * P], buf["xn"][:, t, :], ident[:])
                last.then_inc(xnT_ps, 1)

            def project(b, p, side):
                if side == 0:
                    pe.wait_ge(xnT_sb, b + 1)
                if not known(b) or b >= 1:
                    pe.wait_ge(turned, 2 * b - (1 - side))
                for j in range(2):
                    last = nc.tensor.matmul((Q_BANK, K_BANK)[side][:, j * 256:j * 256 + 256], w4[:, 2 * side + j, :],
                                            xnT[:, p, :], start=True, stop=True)
                last.then_inc((q_ps, k_ps)[side], 1)

            def values(b, p):
                if not known(b) or b >= 3:
                    pe.wait_ge(x_added, b - 2)
                if not known(b) or b >= 1:
                    pe.wait_ge(g_sb, b)
                for t in range(TPB):
                    last = nc.tensor.matmul(VG_BANK[:, t * VD:(t + 1) * VD], xnT[:, p, t * P:(t + 1) * P], wv[:],
                                            start=True, stop=True)
                last.then_inc(v_ps, 1)

            def gates(b, p):
                pe.wait_ge(v_sb, b + 1)
                for t in range(TPB):
                    last = nc.tensor.matmul(VG_BANK[:, t * VD:(t + 1) * VD], xnT[:, p, t * P:(t + 1) * P], wg[:],
                                            start=True, stop=True)
                last.then_inc(g_ps, 1)

            def scores(b, p, h):
                if h == 0:
                    pe.wait_ge(stacked[p], 16 * 2 * NTERM * ((b - p) // 2 + 1) if known(b) else 16 * NTERM * (b - p + 2))
                if not known(b) or b > 0 or h >= 2:
                    pe.wait_ge(s_sb, RH * b + h - 1)
                dst = S_BANK[h % 2]
                nc.tensor.matmul(dst[:, 0:256], stk[:, p, 1, h, 0:P], stk[:, p, 0, h, :], start=True, stop=True)
                nc.tensor.matmul(dst[:, 256:SC], stk[:, p, 1, h, P:256], stk[:, p, 0, h, P:256],
                                 start=True, stop=True).then_inc(s_ps, 1)

            def outputs(b, p, h):
                pe.wait_ge(s_sb, RH * b + h + 1)
                if h == 0:
                    pe.wait_ge(v_sb, b + 1)
                    if not known(b) or b > 0:
                        pe.wait_ge(o_sb, b)
                r, g = h % 2, h // 2
                dst = O_BANK[g // 2][RW * r:RW * (r + 1), g % 2 * 256:(g % 2 + 1) * 256]
                nc.tensor.matmul(dst, v64[:, p, 0, h, :], sT[:, h, 0:256], start=True, stop=False)
                nc.tensor.matmul(dst[:, P:256], v64[:, p, 1, h, :], sT[:, h, 256:SC], start=False,
                                 stop=True).then_inc(o_ps, 1)

            def back_transposes(b):
                pe.wait_ge(oT_sb, 2 * b + 2)
                for t in range(TPB):
                    for g in range(4):
                        last = nc.tensor.transpose(O_BANK[t][:, g * P:(g + 1) * P],
                                                   oTs[:, g // 2, g % 2 * 256 + t * P:g % 2 * 256 + (t + 1) * P], ident[:])
                last.then_inc(o_back, 1)

            def gated_transposes(b):
                pe.wait_ge(gated, b + 1)
                pe.wait_ge(xnT_sb, b + 4 if not known(b) or b + 4 <= NB else NB)
                for t in range(TPB):
                    for k in range(2):
                        last = nc.tensor.transpose(T_BANK[:, (2 * t + k) * P:(2 * t + k + 1) * P],
                                                   on[:, t, k * P:(k + 1) * P], ident[:])
                last.then_inc(gT_ps, 1)

            def output_product(b):
                pe.wait_ge(gT_sb, b + 1)
                pe.wait_ge(g_sb, b + 3 if not known(b) or b + 3 <= NB else NB)
                for t in range(TPB):
                    for k in range(2):
                        last = nc.tensor.matmul(VG_BANK[:, t * D:(t + 1) * D], onT[:, (2 * t + k) * P:(2 * t + k + 1) * P],
                                                wo[:, k, :], start=(k == 0), stop=(k == 1))
                last.then_inc(y_ps, 1)

            def body(b, p):
                first, two_more, one_more = known(b) and b == 0, not known(b) or b + 2 < NB, not known(b) or b + 1 < NB
                scores(b, p, 0)
                scores(b, p, 1)
                if not first:
                    back_transposes(b - 1)
                if one_more:
                    values(b + 1, 1 - p)
                scores(b, p, 2)
                if two_more:
                    norm_transposes(b + 2, p)
                scores(b, p, 3)
                if two_more:
                    project(b + 2, p, 0)
                scores(b, p, 4)
                if two_more:
                    project(b + 2, p, 1)
                outputs(b, p, 0)
                scores(b, p, 5)
                outputs(b, p, 1)
                if one_more:
                    gates(b + 1, 1 - p)
                scores(b, p, 6)
                outputs(b, p, 2)
                scores(b, p, 7)
                outputs(b, p, 3)
                outputs(b, p, 4)
                if not first:
                    gated_transposes(b - 1)
                outputs(b, p, 5)
                outputs(b, p, 6)
                outputs(b, p, 7)
                if not first:
                    output_product(b - 1)

            for b in range(2):
                norm_transposes(b, b)
                project(b, b, 0)
                project(b, b, 1)
            values(0, 0)
            gates(0, 0)
            rounds(pe, body)
            back_transposes(NB - 1)
            gated_transposes(NB - 1)
            output_product(NB - 1)

        @block.scalar
        def _(act):
            def copy_xnT(b, p):
                act.wait_ge(xnT_ps, b + 1)
                if not known(b) or b >= 2:
                    act.wait_ge(g_ps, b - 1)
                nc.scalar.copy(xnT[:, p, :], T_BANK[:, 0:256]).then_inc(xnT_sb, 1)

            def copy_v(b, p):
                act.wait_ge(v_ps, b + 1)
                if not known(b) or b >= 2:
                    act.wait_ge(o_ps, RH * (b - 1))
                nc.scalar.copy(v64[:, p, :, :, 0:RHD], VG_BANK[:].rearrange("p (t h c) -> p t h c", t=TPB, h=RH)).then_inc(v_sb, 1)

            def silu_g(b, p):
                act.wait_ge(g_ps, b + 1)
                if not known(b) or b >= 2:
                    act.wait_ge(gated, b - 1)
                nc.scalar.activation(gate[:, p], VG_BANK[:].rearrange("p (t c) -> p t c", t=TPB), ACT.Silu).then_inc(g_sb, 1)

            def high(b, p):
                act.wait_ge(rotated, b + 1)
                if not known(b) or b > 0:
                    act.wait_ge(stored[1 - p], 8 * (b + p))
                nc.scalar.copy(parts[:, 0], qk[:]).then_inc(hi_done, 1)

            def middle(b):
                act.wait_ge(rest_done, b + 1)
                nc.scalar.copy(parts[:, 1], rest[:]).then_inc(mid_done, 1)

            def copy_oT(b, half):
                act.wait_ge(o_ps, RH * b + 4 * half + 4)
                nc.scalar.copy(oTs[:, half, :], O_BANK[half][:]).then_inc(oT_sb, 1)

            def squares(b):
                act.wait_ge(o_back, b + 1)
                if not known(b) or b > 0:
                    act.wait_ge(scaled, 2 * b)
                for t in range(TPB):
                    o4 = O_BANK[t][:].rearrange("p (h c) -> p h c", c=RW)
                    nc.scalar.activation(osq[:, t], o4[:, :, 0:RHD], ACT.Square).then_inc(squared, 1)
                for t in range(TPB):
                    o4 = O_BANK[t][:].rearrange("p (h c) -> p h c", c=RW)
                    last = nc.scalar.copy(osb[:, t, :, 0:RHD + 1], o4[:, :, 0:RHD + 1])
                last.then_inc(o_sb, 1)

            def copy_onT(b):
                act.wait_ge(gT_ps, b + 1)
                nc.scalar.copy(onT[:], T_BANK[:]).then_inc(gT_sb, 1)

            def body(b, p):
                first, two_more, one_more = known(b) and b == 0, not known(b) or b + 2 < NB, not known(b) or b + 1 < NB
                if not first:
                    copy_oT(b - 1, 1)
                if not first:
                    squares(b - 1)
                if one_more:
                    copy_v(b + 1, 1 - p)
                if two_more:
                    copy_xnT(b + 2, p)
                if two_more:
                    high(b + 2, p)
                if one_more:
                    silu_g(b + 1, 1 - p)
                if two_more:
                    middle(b + 2)
                copy_oT(b, 0)
                if not first:
                    copy_onT(b - 1)

            act.wait_ge(init, 2)
            for b in range(2):
                copy_xnT(b, b)
                high(b, b)
                middle(b)
            copy_v(0, 0)
            silu_g(0, 0)
            rounds(act, body)
            copy_oT(NB - 1, 1)
            squares(NB - 1)
            copy_onT(NB - 1)

        @block.vector
        def _(dve):
            def xn(t):
                return buf["xn"][:, t, :]

            def normalised(b):
                if not known(b) or b > 0:
                    dve.wait_ge(xnT_ps, b)
                ln.scale(dve, b, xn)

            def rotate(b):
                for i in range(2):
                    dve.wait_ge((q_ps, k_ps)[i], b + 1)
                    nc.vector.tensor_tensor(r1[:, i, :], (Q_BANK, K_BANK)[i][:, 0:256], tab[:, 2 * i, :], ALU.mult)
                    nc.vector.tensor_tensor(r2[:, i, :], (Q_BANK, K_BANK)[i][:, 256:512], tab[:, 2 * i + 1, :],
                                            ALU.mult).then_inc(turned, 1)
                dve.wait_ge(turned, 2 * b + 2)
                if not known(b) or b > 0:
                    dve.wait_ge(lo_done, b)
                nc.vector.tensor_tensor(qk[:], r1[:], r2[:], ALU.add).then_inc(rotated, 1)

            def masked(b, h):
                dve.wait_ge(s_ps, RH * b + h + 1)
                if not known(b) or b > 0:
                    dve.wait_ge(o_ps, RH * b - RH + h + 1)
                nc.vector.tensor_tensor(sT[:, h, :], S_BANK[h % 2][:, 0:SC], mask[:, h, :], ALU.mult).then_inc(s_sb, 1)

            def head_stats(b):
                dve.wait_ge(o_sb, b + 1)
                sums = [osb[:, t, :, RHD] for t in range(TPB)]
                for t in range(TPB):
                    nc.vector.tensor_scalar(dn[:, t * RH:(t + 1) * RH], sums[t], 1.0, None, ALU.max).then_inc(o_step, 1)
                nc.vector.reduce_sum(ms[:], osq[:].rearrange("p t h c -> p (t h) c"), AX).then_inc(o_step, 1)
                dve.wait_ge(o_step, 6 * b + 2)
                for t in range(TPB):
                    last = nc.vector.scalar_tensor_tensor(dn[:, t * RH:(t + 1) * RH], sums[t], -1.0,
                                                          dn[:, t * RH:(t + 1) * RH], ALU.mult, ALU.max)
                last.then_inc(o_step, 1)
                dve.wait_ge(o_step, 6 * b + 4)
                nc.vector.scalar_tensor_tensor(dn[:], dn[:], EPS, dn[:], ALU.mult, ALU.mult).then_inc(o_step, 1)
                dve.wait_ge(o_step, 6 * b + 5)
                nc.vector.scalar_tensor_tensor(ms[:], ms[:], 1.0 / RHD, dn[:], ALU.mult, ALU.add).then_inc(o_step, 1)

            def scale_heads(b, p):
                dve.wait_ge(root, b + 1)
                for t in range(TPB):
                    nc.vector.tensor_tensor(oh[:, t], osb[:, t, :, 0:RHD], fac[:, t, :, None].to_broadcast([P, RH, RHD]),
                                            ALU.mult).then_inc(scaled, 1)
                dve.wait_ge(scaled, 2 * b + 2)
                dve.wait_ge(g_sb, b + 1)
                if not known(b) or b > 0:
                    dve.wait_ge(gT_ps, b)
                nc.vector.tensor_tensor(on[:], oh[:].rearrange("p t h c -> p t (h c)"), gate[:, p],
                                        ALU.mult).then_inc(gated, 1)

            def add_fetched(k):
                dve.wait_ge(fetched[k], 128)
                for i in range(8):
                    add_rows(nc, buf, moe, HT + 8 * k + i)

            def add(b):
                dve.wait_ge(y_ps, b + 1)
                nc.vector.tensor_tensor(xs[:, ds(2 * b, 2), :], VG_BANK[:, 0:256].rearrange("p (t c) -> p t c", t=TPB),
                                        xs[:, ds(2 * b, 2), :], ALU.add).then_inc(x_added, 1)

            def body(b, p):
                first, two_more = known(b) and b == 0, not known(b) or b + 2 < NB
                masked(b, 0)
                masked(b, 1)
                masked(b, 2)
                if not first:
                    head_stats(b - 1)
                masked(b, 3)
                masked(b, 4)
                if two_more:
                    rotate(b + 2)
                masked(b, 5)
                if not first:
                    scale_heads(b - 1, 1 - p)
                masked(b, 6)
                if not known(b) or b + 3 < NB:
                    ln.stats(dve, b + 3)
                masked(b, 7)
                if not known(b) or b >= 2:
                    dve.wait_ge(x_added, b - 1)
                    stats_for_experts(nc, buf, b - 2)
                if not first:
                    add(b - 1)
                if not known(b) or b + 3 < NB:
                    normalised(b + 3)
                if known(b) and b < FETCH_ROUNDS and b % 2:
                    add_fetched(b // 2)
                if known(b) and b == FETCH_ROUNDS - 1:
                    add_fetched(3)

            ln.stats(dve, 0)
            normalised(0)
            for b in range(2):
                ln.stats(dve, b + 1)
                normalised(b + 1)
                rotate(b)
            rounds(dve, body)
            head_stats(NB - 1)
            scale_heads(NB - 1, 1)
            add(NB - 1)
            dve.wait_ge(x_added, NB)
            for b in (NB - 2, NB - 1):
                stats_for_experts(nc, buf, b)


def tables():
    f = np.float32
    S = TPB * P
    angle = np.repeat(f(1.0) / f(10000.0) ** np.linspace(0.0, 1.0, KD // 2, dtype=f), 2).astype(f)
    idx = np.arange(S, dtype=f)
    arg = (idx[None, :] * angle[:, None]).astype(f)
    cos, sin = np.cos(arg).astype(f), np.sin(arg).astype(f)
    sign = np.where(np.arange(KD) % 2 == 0, -1.0, 1.0).astype(f)[:, None]
    c, s = np.tile(cos, (RH, 1)), np.tile(sin * sign, (RH, 1))
    scale = f(KD ** -0.5)
    tab = np.stack([c, s, c * scale, s * scale], 1).astype(f)
    decay = np.log1p(-2.0 ** (-5.0 - np.arange(RH))).astype(f)
    diff = idx[:, None] - idx[None, :]
    m = np.where(diff[None] >= 0, np.exp(diff[None] * decay[:, None, None]), 0.0).astype(f)
    m = (m / np.sqrt(m.sum(-1, keepdims=True, dtype=f))).astype(f)
    mt = m.transpose(2, 0, 1)
    mask = np.concatenate([mt[0:P], mt[P:S, :, P:S]], 2)
    return dict(
        tab=tab, mask=mask, ident=np.eye(P, dtype=f), earlier=np.triu(np.ones((P, P), f), 1) - 1,
        prio=(E - np.arange(E, dtype=f))[None], start=(P * np.arange(NBLK, dtype=f))[None],
    )


def kernel(L0_attn_a_x, L0_attn_a_W_qkv, L0_attn_a_proj, L0_attn_a_W_out, L0_attn_a_b_out, L0_attn_b_wq, L0_attn_b_wk,
           L0_attn_b_wv, L0_attn_b_wg, L0_attn_b_wo, L0_ffn_wg_red, L0_ffn_wg, L0_ffn_w1, L0_ffn_b1, L0_ffn_w2, L0_ffn_b2):
    import concourse.bacc as bacc
    from concourse.bass_utils import run_bass_kernel_spmd

    A = lambda a: np.asarray(a)
    swap = np.arange(D) ^ 1
    wq, wk = A(L0_attn_b_wq), A(L0_attn_b_wk)
    arrays = dict(
        x=A(L0_attn_a_x).reshape(NT, P, D).transpose(1, 0, 2),
        wqkvT=A(L0_attn_a_W_qkv).T, proj=A(L0_attn_a_proj), woutT=A(L0_attn_a_W_out).T, b_out=A(L0_attn_a_b_out)[None],
        w4=np.stack([wq, wq[:, swap], wk, wk[:, swap]], 1), wv=A(L0_attn_b_wv), wgate=A(L0_attn_b_wg),
        wo=A(L0_attn_b_wo).reshape(2, P, D).transpose(1, 0, 2),
        wg_red=A(L0_ffn_wg_red), wg=A(L0_ffn_wg), w1=A(L0_ffn_w1).transpose(1, 0, 2),
        b1=A(L0_ffn_b1).reshape(E, HC, P).transpose(2, 0, 1),
        w2=A(L0_ffn_w2).reshape(E * HC, P, D).transpose(1, 0, 2), b2=A(L0_ffn_b2).reshape(1, E * D),
        **tables(),
    )
    arrays = {k: np.ascontiguousarray(v) for k, v in arrays.items()}
    nc = bacc.Bacc("TRN2", target_bir_lowering=False, num_devices=1)
    ap = {k: nc.dram_tensor("in_" + k, v.shape, F32, kind="ExternalInput").ap() for k, v in arrays.items()}
    out = nc.dram_tensor("out", (P, NT, D), F32, kind="ExternalOutput").ap()
    build(nc, ap, out)
    r = run_bass_kernel_spmd(nc, [{"in_" + k: v for k, v in arrays.items()}], core_ids=[0])
    return r.results[0]["out"].transpose(1, 0, 2).reshape(NB, TPB * P, D)
```
